# Optimizing a Trainium2 kernel written in Bass

```python
import numpy as np
import jax
import jax.numpy as jnp

def _softmax(x, axis=-1):
    return jax.nn.softmax(x, axis=axis)

def _gelu(x):
    return jax.nn.gelu(x, approximate=True)

def _silu(x):
    return jax.nn.silu(x)

def _sigmoid(x):
    return jax.nn.sigmoid(x)

def _layernorm(x, axis=-1, eps=1e-05):
    m = jnp.mean(x, axis=axis, keepdims=True)
    v = jnp.var(x, axis=axis, keepdims=True)
    return (x - m) / jnp.sqrt(v + eps)

def _scatter_add(tgt, idx, src, axis=0):
    return tgt.at[idx].add(src)

def _segment_sum(src, seg, n):
    return jax.ops.segment_sum(src, seg, n)
kernel_name = 'mk_decoder_postln_d2_seqx_r4_d0435d'

def setup_inputs(seed: int=0):
    np.random.seed(seed)
    _w = jnp.asarray

    def _rec_inputs():
        import jax
        import jax.numpy as jnp
        _rk = jax.random.key(seed)
        x = -0.000125 + 0.9999 * jax.random.normal(jax.random.fold_in(_rk, 1), (8, 256, 256), jnp.float32)
        _lenS = 256 - jax.random.randint(jax.random.fold_in(_rk, 7), (8,), 0, max(1, 256 // 4) + 1, jnp.int32)
        _lenS2 = 120 - jax.random.randint(jax.random.fold_in(_rk, 8), (8,), 0, max(1, 120 // 4) + 1, jnp.int32)
        _ctx_768P = jax.random.normal(jax.random.fold_in(_rk, 11), (8, 16, 192), jnp.float32)
        _ctx_768c = jax.random.dirichlet(jax.random.fold_in(_rk, 511), 0.3 * jnp.ones((16,), jnp.float32), (8, 120))
        _ctx_768t = jnp.einsum('bsk,bkd->bsd', _ctx_768c, _ctx_768P)
        _ctx_768t = _ctx_768t * jax.lax.rsqrt(jnp.mean(jnp.square(_ctx_768t)) + 1e-12) * 0.953939
        ctx_768 = 0.00243539 + 0.99952 * (_ctx_768t + 0.3 * jax.random.normal(jax.random.fold_in(_rk, 611), (8, 120, 192), jnp.float32))
        return (x, ctx_768)
    x, ctx_768 = _rec_inputs()

    def _L0_attn_setup():
        import jax, jax.numpy as jnp
        import numpy as np
        key = jax.random.key(seed)
        kx, kf = jax.random.split(key)
        x = jax.random.normal(kx, (4, 2048, 256), dtype=jnp.float32)
        filt = jax.random.normal(kf, (512,), dtype=jnp.float32)
        return {'x': x, 'filt': filt}
    _L0_attn_all = _L0_attn_setup()
    _L0_attn_in = {k: v for k, v in _L0_attn_all.items() if k in ('filt',)}
    del _L0_attn_all

    def _L0_xattn_setup():
        import jax, jax.numpy as jnp
        import numpy as np
        HEADS = 16
        DIM_HEAD = 64
        RANK = 32
        LORA_W = 1.0
        IPA_SCALE = 1.0
        IPA_TOKENS = 4
        SCALE = DIM_HEAD ** (-0.5)

        def _split_heads(t):
            b, n, _ = t.shape
            return t.reshape(b, n, HEADS, DIM_HEAD).transpose(0, 2, 1, 3)

        def _merge_heads(t):
            b, h, n, d = t.shape
            return t.transpose(0, 2, 1, 3).reshape(b, n, h * d)

        def _attention(q_in, k_in, v_in):
            q = _split_heads(q_in)
            k = _split_heads(k_in)
            v = _split_heads(v_in)
            s = jnp.einsum('bhid,bhjd->bhij', q, k) * SCALE
            p = jax.nn.softmax(s, axis=-1)
            o = jnp.einsum('bhij,bhjd->bhid', p, v)
            return _merge_heads(o)

        def _lora(t, down, up, alpha):
            return t @ down @ up * (LORA_W * alpha[0] / RANK)
        key = jax.random.key(seed)
        ks = jax.random.split(key, 20)
        B, N, QD, CD, ID = (8, 1024, 256, 192, HEADS * DIM_HEAD)
        CTX = 77 + IPA_TOKENS
        s = 0.02
        return {'x': jax.random.normal(ks[0], (B, N, QD), jnp.float32), 'context': jax.random.normal(ks[1], (B, CTX, CD), jnp.float32), 'Wq': jax.random.normal(ks[2], (QD, ID), jnp.float32) * s, 'Wk': jax.random.normal(ks[3], (CD, ID), jnp.float32) * s, 'Wv': jax.random.normal(ks[4], (CD, ID), jnp.float32) * s, 'Wo': jax.random.normal(ks[5], (ID, QD), jnp.float32) * s, 'bo': jnp.zeros((QD,), jnp.float32), 'q_down': jax.random.normal(ks[6], (QD, RANK), jnp.float32) * s, 'q_up': jax.random.normal(ks[7], (RANK, ID), jnp.float32) * s, 'q_alpha': jnp.ones((1,), jnp.float32) * RANK, 'k_down': jax.random.normal(ks[8], (CD, RANK), jnp.float32) * s, 'k_up': jax.random.normal(ks[9], (RANK, ID), jnp.float32) * s, 'k_alpha': jnp.ones((1,), jnp.float32) * RANK, 'v_down': jax.random.normal(ks[10], (CD, RANK), jnp.float32) * s, 'v_up': jax.random.normal(ks[11], (RANK, ID), jnp.float32) * s, 'v_alpha': jnp.ones((1,), jnp.float32) * RANK, 'o_down': jax.random.normal(ks[12], (ID, RANK), jnp.float32) * s, 'o_up': jax.random.normal(ks[13], (RANK, QD), jnp.float32) * s, 'o_alpha': jnp.ones((1,), jnp.float32) * RANK, 'Wk_ipa': jax.random.normal(ks[14], (CD, ID), jnp.float32) * s, 'Wv_ipa': jax.random.normal(ks[15], (CD, ID), jnp.float32) * s}
    _L0_xattn_all = _L0_xattn_setup()
    _L0_xattn_in = {k: v for k, v in _L0_xattn_all.items() if k in ('Wq', 'Wk', 'Wv', 'Wo', 'bo', 'q_down', 'q_up', 'q_alpha', 'k_down', 'k_up', 'k_alpha', 'v_down', 'v_up', 'v_alpha', 'o_down', 'o_up', 'o_alpha', 'Wk_ipa', 'Wv_ipa')}
    del _L0_xattn_all

    def _L0_ffn_setup():
        import jax, jax.numpy as jnp
        import numpy as np
        D_MODEL = 256
        D_FF = 1024
        N_EXPERTS = 8
        TOP_K = 2
        D_FF_PER = D_FF // N_EXPERTS
        B, T = (4, 512)
        key = jax.random.key(seed)
        ks = jax.random.split(key, 7)
        b1_bound = 1.0 / np.sqrt(D_MODEL)
        b2_bound = 1.0 / np.sqrt(D_FF_PER)
        return {'x': jax.random.normal(ks[0], (B, T, D_MODEL), dtype=jnp.float32), 'router_w': jax.random.uniform(ks[1], (D_MODEL, N_EXPERTS), minval=-b1_bound, maxval=b1_bound, dtype=jnp.float32), 'router_b': jax.random.uniform(ks[2], (N_EXPERTS,), minval=-b1_bound, maxval=b1_bound, dtype=jnp.float32), 'W1': jax.random.uniform(ks[3], (N_EXPERTS, D_MODEL, D_FF_PER), minval=-b1_bound, maxval=b1_bound, dtype=jnp.float32), 'b1': jax.random.uniform(ks[4], (N_EXPERTS, D_FF_PER), minval=-b1_bound, maxval=b1_bound, dtype=jnp.float32), 'W2': jax.random.uniform(ks[5], (N_EXPERTS, D_FF_PER, D_MODEL), minval=-b2_bound, maxval=b2_bound, dtype=jnp.float32), 'b2': jax.random.uniform(ks[6], (N_EXPERTS, D_MODEL), minval=-b2_bound, maxval=b2_bound, dtype=jnp.float32)}
    _L0_ffn_all = _L0_ffn_setup()
    _L0_ffn_in = {k: v for k, v in _L0_ffn_all.items() if k in ('router_w', 'router_b', 'W1', 'b1', 'W2', 'b2')}
    del _L0_ffn_all

    def _L1_attn_setup():
        import jax, jax.numpy as jnp
        import numpy as np
        D_MODEL, D_INNER, D_STATE, DT_RANK, D_CONV = (256, 512, 16, 64, 4)
        B, L = (2, 512)

        def _rmsnorm(x, w, eps=1e-05):
            return x * jax.lax.rsqrt(jnp.mean(x * x, axis=-1, keepdims=True) + eps) * w

        def _causal_depthwise_conv(x, conv_w, conv_b):
            K = conv_w.shape[1]
            xp = jnp.pad(x, ((0, 0), (K - 1, 0), (0, 0)))
            Lx = x.shape[1]
            out = conv_b
            for k in range(K):
                out = out + xp[:, k:k + Lx, :] * conv_w[:, k]
            return out

        def _selective_scan(x, delta, Bm, Cm, A):
            h0 = jnp.zeros((x.shape[0], A.shape[0], A.shape[1]), x.dtype)

            def step(h, inp):
                xt, dt, bt, ct = inp
                A_bar = jnp.exp(dt[..., None] * A)
                h = A_bar * h + (dt * xt)[..., None] * bt[:, None, :]
                y = jnp.einsum('ben,bn->be', h, ct)
                return (h, y)
            xs = tuple((jnp.swapaxes(a, 0, 1) for a in (x, delta, Bm, Cm)))
            _, ys = jax.lax.scan(step, h0, xs)
            return jnp.swapaxes(ys, 0, 1)
        key = jax.random.key(seed)
        ks = jax.random.split(key, 14)
        s = lambda k, shp, fan: jax.random.normal(k, shp, jnp.float32) / np.sqrt(fan)
        return {'resid': jax.random.normal(ks[0], (B, L, D_MODEL), jnp.float32), 'norm_w': jnp.ones((D_MODEL,), jnp.float32), 'skip_w': s(ks[1], (D_INNER, D_MODEL), D_MODEL), 'in_w': s(ks[2], (D_INNER, D_MODEL), D_MODEL), 'conv_w': s(ks[3], (D_INNER, D_CONV), D_CONV), 'conv_b': jnp.zeros((D_INNER,), jnp.float32), 'wd1': s(ks[4], (DT_RANK, D_INNER), D_INNER), 'wd2': s(ks[5], (D_INNER, DT_RANK), DT_RANK), 'wd2_b': jnp.zeros((D_INNER,), jnp.float32), 'wb': s(ks[6], (D_STATE, D_INNER), D_INNER), 'wc': s(ks[7], (D_STATE, D_INNER), D_INNER), 'A_log': jax.random.normal(ks[8], (D_INNER, D_STATE), jnp.float32), 'W_D': jnp.ones((D_INNER,), jnp.float32), 'out_w': s(ks[9], (D_MODEL, D_INNER), D_INNER)}
    _L1_attn_all = _L1_attn_setup()
    _L1_attn_in = {k: v for k, v in _L1_attn_all.items() if k in ('norm_w', 'skip_w', 'in_w', 'conv_w', 'conv_b', 'wd1', 'wd2', 'wd2_b', 'wb', 'wc', 'A_log', 'W_D', 'out_w')}
    del _L1_attn_all

    def _L1_xattn_setup():
        import jax, jax.numpy as jnp
        import numpy as np
        QUERY_DIM = 256
        KEY_DIM = 192
        NUM_HEADS = 16
        HEAD_DIM = QUERY_DIM // NUM_HEADS
        SCALE = HEAD_DIM ** (-0.5)
        key = jax.random.key(seed)
        ks = jax.random.split(key, 11)
        B, Nq, Nk = (4, 1024, 256)
        s_q = QUERY_DIM ** (-0.5)
        s_k = KEY_DIM ** (-0.5)
        return {'query': jax.random.normal(ks[0], (B, Nq, QUERY_DIM), jnp.float32), 'key': jax.random.normal(ks[1], (B, Nk, KEY_DIM), jnp.float32), 'value': jax.random.normal(ks[2], (B, Nk, KEY_DIM), jnp.float32), 'Wq': jax.random.normal(ks[3], (QUERY_DIM, QUERY_DIM), jnp.float32) * s_q, 'bq': jnp.zeros((QUERY_DIM,), jnp.float32), 'Wk': jax.random.normal(ks[4], (KEY_DIM, QUERY_DIM), jnp.float32) * s_k, 'bk': jnp.zeros((QUERY_DIM,), jnp.float32), 'Wv': jax.random.normal(ks[5], (KEY_DIM, QUERY_DIM), jnp.float32) * s_k, 'bv': jnp.zeros((QUERY_DIM,), jnp.float32), 'Wo': jax.random.normal(ks[6], (QUERY_DIM, QUERY_DIM), jnp.float32) * s_q, 'bo': jnp.zeros((QUERY_DIM,), jnp.float32)}
    _L1_xattn_all = _L1_xattn_setup()
    _L1_xattn_in = {k: v for k, v in _L1_xattn_all.items() if k in ('Wq', 'bq', 'Wk', 'bk', 'Wv', 'bv', 'Wo', 'bo')}
    del _L1_xattn_all

    def _L1_ffn_setup():
        import jax, jax.numpy as jnp
        import numpy as np
        LATENT = 256
        LEAF_W = 64
        DEPTH = 4
        N_LEAVES = 2 ** DEPTH
        N_NODES = 2 ** DEPTH - 1
        B, S = (4, 512)

        def _fff_params(key, prefix):
            ks = jax.random.split(key, 4)
            d, h, l, n = (LATENT, LEAF_W, N_LEAVES, N_NODES)
            s_in = 1.0 / np.sqrt(d).astype(np.float32)
            s_h = 1.0 / np.sqrt(h).astype(np.float32)
            return {f'{prefix}_node_w': jax.random.normal(ks[0], (n, d), jnp.float32) * s_in, f'{prefix}_node_b': jax.random.normal(ks[1], (n,), jnp.float32) * s_in, f'{prefix}_w1': jax.random.normal(ks[2], (l, d, h), jnp.float32) * s_in, f'{prefix}_b1': jnp.zeros((l, h), jnp.float32), f'{prefix}_w2': jax.random.normal(ks[3], (l, h, d), jnp.float32) * s_h, f'{prefix}_b2': jnp.zeros((l, d), jnp.float32)}

        def _fff(x, node_w, node_b, w1, b1, w2, b2):
            Bx, Sx, D = x.shape
            xf = x.reshape(-1, D)
            N = xf.shape[0]
            cur = jnp.zeros((N,), jnp.int32)
            for _ in range(DEPTH):
                pw = node_w[cur]
                score = jnp.einsum('nd,nd->n', xf, pw) + node_b[cur]
                cur = 2 * cur + 1 + (score >= 0).astype(jnp.int32)
            leaf = cur - N_NODES
            sel = jax.nn.one_hot(leaf, N_LEAVES, dtype=xf.dtype)
            hidden_all = jax.nn.relu(jnp.einsum('nd,ldh->lnh', xf, w1) + b1[:, None, :])
            hidden = hidden_all * sel.T[:, :, None]
            out = jnp.einsum('lnh,lho->no', hidden, w2) + sel @ b2
            return out.reshape(Bx, Sx, D)
        key = jax.random.key(seed)
        kx, kq, kk, kv = jax.random.split(key, 4)
        inp = {'x': jax.random.normal(kx, (B, S, LATENT), jnp.float32)}
        inp.update(_fff_params(kq, 'q'))
        inp.update(_fff_params(kk, 'k'))
        inp.update(_fff_params(kv, 'v'))
        return inp
    _L1_ffn_all = _L1_ffn_setup()
    _L1_ffn_in = {k: v for k, v in _L1_ffn_all.items() if k in ('q_node_w', 'q_node_b', 'q_w1', 'q_b1', 'q_w2', 'q_b2', 'k_node_w', 'k_node_b', 'k_w1', 'k_b1', 'k_w2', 'k_b2', 'v_node_w', 'v_node_b', 'v_w1', 'v_b1', 'v_w2', 'v_b2')}
    del _L1_ffn_all
    return {'x': x, 'ctx_768': ctx_768, 'L0_attn_filt': _L0_attn_in['filt'], 'L0_xattn_Wq': _L0_xattn_in['Wq'], 'L0_xattn_Wk': _L0_xattn_in['Wk'], 'L0_xattn_Wv': _L0_xattn_in['Wv'], 'L0_xattn_Wo': _L0_xattn_in['Wo'], 'L0_xattn_bo': _L0_xattn_in['bo'], 'L0_xattn_q_down': _L0_xattn_in['q_down'], 'L0_xattn_q_up': _L0_xattn_in['q_up'], 'L0_xattn_q_alpha': _L0_xattn_in['q_alpha'], 'L0_xattn_k_down': _L0_xattn_in['k_down'], 'L0_xattn_k_up': _L0_xattn_in['k_up'], 'L0_xattn_k_alpha': _L0_xattn_in['k_alpha'], 'L0_xattn_v_down': _L0_xattn_in['v_down'], 'L0_xattn_v_up': _L0_xattn_in['v_up'], 'L0_xattn_v_alpha': _L0_xattn_in['v_alpha'], 'L0_xattn_o_down': _L0_xattn_in['o_down'], 'L0_xattn_o_up': _L0_xattn_in['o_up'], 'L0_xattn_o_alpha': _L0_xattn_in['o_alpha'], 'L0_xattn_Wk_ipa': _L0_xattn_in['Wk_ipa'], 'L0_xattn_Wv_ipa': _L0_xattn_in['Wv_ipa'], 'L0_ffn_router_w': _L0_ffn_in['router_w'], 'L0_ffn_router_b': _L0_ffn_in['router_b'], 'L0_ffn_W1': _L0_ffn_in['W1'], 'L0_ffn_b1': _L0_ffn_in['b1'], 'L0_ffn_W2': _L0_ffn_in['W2'], 'L0_ffn_b2': _L0_ffn_in['b2'], 'L1_attn_norm_w': _L1_attn_in['norm_w'], 'L1_attn_skip_w': _L1_attn_in['skip_w'], 'L1_attn_in_w': _L1_attn_in['in_w'], 'L1_attn_conv_w': _L1_attn_in['conv_w'], 'L1_attn_conv_b': _L1_attn_in['conv_b'], 'L1_attn_wd1': _L1_attn_in['wd1'], 'L1_attn_wd2': _L1_attn_in['wd2'], 'L1_attn_wd2_b': _L1_attn_in['wd2_b'], 'L1_attn_wb': _L1_attn_in['wb'], 'L1_attn_wc': _L1_attn_in['wc'], 'L1_attn_A_log': _L1_attn_in['A_log'], 'L1_attn_W_D': _L1_attn_in['W_D'], 'L1_attn_out_w': _L1_attn_in['out_w'], 'L1_xattn_Wq': _L1_xattn_in['Wq'], 'L1_xattn_bq': _L1_xattn_in['bq'], 'L1_xattn_Wk': _L1_xattn_in['Wk'], 'L1_xattn_bk': _L1_xattn_in['bk'], 'L1_xattn_Wv': _L1_xattn_in['Wv'], 'L1_xattn_bv': _L1_xattn_in['bv'], 'L1_xattn_Wo': _L1_xattn_in['Wo'], 'L1_xattn_bo': _L1_xattn_in['bo'], 'L1_ffn_q_node_w': _L1_ffn_in['q_node_w'], 'L1_ffn_q_node_b': _L1_ffn_in['q_node_b'], 'L1_ffn_q_w1': _L1_ffn_in['q_w1'], 'L1_ffn_q_b1': _L1_ffn_in['q_b1'], 'L1_ffn_q_w2': _L1_ffn_in['q_w2'], 'L1_ffn_q_b2': _L1_ffn_in['q_b2'], 'L1_ffn_k_node_w': _L1_ffn_in['k_node_w'], 'L1_ffn_k_node_b': _L1_ffn_in['k_node_b'], 'L1_ffn_k_w1': _L1_ffn_in['k_w1'], 'L1_ffn_k_b1': _L1_ffn_in['k_b1'], 'L1_ffn_k_w2': _L1_ffn_in['k_w2'], 'L1_ffn_k_b2': _L1_ffn_in['k_b2'], 'L1_ffn_v_node_w': _L1_ffn_in['v_node_w'], 'L1_ffn_v_node_b': _L1_ffn_in['v_node_b'], 'L1_ffn_v_w1': _L1_ffn_in['v_w1'], 'L1_ffn_v_b1': _L1_ffn_in['v_b1'], 'L1_ffn_v_w2': _L1_ffn_in['v_w2'], 'L1_ffn_v_b2': _L1_ffn_in['v_b2']}

def reference(x, ctx_768, L0_attn_filt, L0_xattn_Wq, L0_xattn_Wk, L0_xattn_Wv, L0_xattn_Wo, L0_xattn_bo, L0_xattn_q_down, L0_xattn_q_up, L0_xattn_q_alpha, L0_xattn_k_down, L0_xattn_k_up, L0_xattn_k_alpha, L0_xattn_v_down, L0_xattn_v_up, L0_xattn_v_alpha, L0_xattn_o_down, L0_xattn_o_up, L0_xattn_o_alpha, L0_xattn_Wk_ipa, L0_xattn_Wv_ipa, L0_ffn_router_w, L0_ffn_router_b, L0_ffn_W1, L0_ffn_b1, L0_ffn_W2, L0_ffn_b2, L1_attn_norm_w, L1_attn_skip_w, L1_attn_in_w, L1_attn_conv_w, L1_attn_conv_b, L1_attn_wd1, L1_attn_wd2, L1_attn_wd2_b, L1_attn_wb, L1_attn_wc, L1_attn_A_log, L1_attn_W_D, L1_attn_out_w, L1_xattn_Wq, L1_xattn_bq, L1_xattn_Wk, L1_xattn_bk, L1_xattn_Wv, L1_xattn_bv, L1_xattn_Wo, L1_xattn_bo, L1_ffn_q_node_w, L1_ffn_q_node_b, L1_ffn_q_w1, L1_ffn_q_b1, L1_ffn_q_w2, L1_ffn_q_b2, L1_ffn_k_node_w, L1_ffn_k_node_b, L1_ffn_k_w1, L1_ffn_k_b1, L1_ffn_k_w2, L1_ffn_k_b2, L1_ffn_v_node_w, L1_ffn_v_node_b, L1_ffn_v_w1, L1_ffn_v_b1, L1_ffn_v_w2, L1_ffn_v_b2):
    import jax
    import jax.numpy as jnp

    def _L0_attn_ref(x, filt):
        import jax, jax.numpy as jnp
        import numpy as np
        batch, seq, dim = x.shape
        L = filt.shape[0]
        pad = seq + L - 1
        xt = jnp.swapaxes(x, 1, 2)
        fx = jnp.fft.rfft(xt, n=pad, axis=-1)
        ff = jnp.fft.rfft(filt[::-1], n=pad)
        conv = jnp.fft.irfft(fx * ff, n=pad, axis=-1)
        conv = conv[:, :, L - 1:L - 1 + seq]
        return jnp.swapaxes(conv, 1, 2)

    def _L0_xattn_ref(x, context, Wq, Wk, Wv, Wo, bo, q_down, q_up, q_alpha, k_down, k_up, k_alpha, v_down, v_up, v_alpha, o_down, o_up, o_alpha, Wk_ipa, Wv_ipa):
        import jax, jax.numpy as jnp
        import numpy as np
        HEADS = 16
        DIM_HEAD = 64
        RANK = 32
        LORA_W = 1.0
        IPA_SCALE = 1.0
        IPA_TOKENS = 4
        SCALE = DIM_HEAD ** (-0.5)

        def _split_heads(t):
            b, n, _ = t.shape
            return t.reshape(b, n, HEADS, DIM_HEAD).transpose(0, 2, 1, 3)

        def _merge_heads(t):
            b, h, n, d = t.shape
            return t.transpose(0, 2, 1, 3).reshape(b, n, h * d)

        def _attention(q_in, k_in, v_in):
            q = _split_heads(q_in)
            k = _split_heads(k_in)
            v = _split_heads(v_in)
            s = jnp.einsum('bhid,bhjd->bhij', q, k) * SCALE
            p = jax.nn.softmax(s, axis=-1)
            o = jnp.einsum('bhij,bhjd->bhid', p, v)
            return _merge_heads(o)

        def _lora(t, down, up, alpha):
            return t @ down @ up * (LORA_W * alpha[0] / RANK)
        q_in = x @ Wq + _lora(x, q_down, q_up, q_alpha)
        end = context.shape[1] - IPA_TOKENS
        org_ctx = context[:, :end, :]
        ipa_ctx = context[:, end:, :]
        k_in = org_ctx @ Wk + _lora(org_ctx, k_down, k_up, k_alpha)
        v_in = org_ctx @ Wv + _lora(org_ctx, v_down, v_up, v_alpha)
        out = _attention(q_in, k_in, v_in)
        ipa_k = ipa_ctx @ Wk_ipa
        ipa_v = ipa_ctx @ Wv_ipa
        out_ipa = _attention(q_in, ipa_k, ipa_v)
        out = out + IPA_SCALE * out_ipa
        return out @ Wo + bo + _lora(out, o_down, o_up, o_alpha)

    def _L0_ffn_ref(x, router_w, router_b, W1, b1, W2, b2):
        import jax, jax.numpy as jnp
        import numpy as np
        D_MODEL = 256
        D_FF = 1024
        N_EXPERTS = 8
        TOP_K = 2
        D_FF_PER = D_FF // N_EXPERTS
        B, T = (4, 512)
        router_logits = x @ router_w + router_b
        routing_weights = jax.nn.softmax(router_logits, axis=-1)
        top_k_weights, top_k_indices = jax.lax.top_k(routing_weights, TOP_K)
        top_k_weights = top_k_weights / jnp.sum(top_k_weights, axis=-1, keepdims=True)
        routing_mask = jnp.zeros_like(routing_weights)
        routing_mask = jnp.take_along_axis(routing_mask, top_k_indices, axis=-1)
        b_idx = jnp.arange(x.shape[0])[:, None, None]
        t_idx = jnp.arange(x.shape[1])[None, :, None]
        routing_mask = jnp.zeros_like(routing_weights).at[b_idx, t_idx, top_k_indices].set(top_k_weights)
        h1 = jnp.einsum('btd,nde->btne', x, W1) + b1
        h1 = jax.nn.gelu(h1, approximate=False)
        out_per_expert = jnp.einsum('btne,nef->btnf', h1, W2) + b2
        output = jnp.sum(out_per_expert * routing_mask[..., None], axis=-2)
        return output

    def _L1_attn_ref(resid, norm_w, skip_w, in_w, conv_w, conv_b, wd1, wd2, wd2_b, wb, wc, A_log, W_D, out_w):
        import jax, jax.numpy as jnp
        import numpy as np
        D_MODEL, D_INNER, D_STATE, DT_RANK, D_CONV = (256, 512, 16, 64, 4)
        B, L = (2, 512)

        def _rmsnorm(x, w, eps=1e-05):
            return x * jax.lax.rsqrt(jnp.mean(x * x, axis=-1, keepdims=True) + eps) * w

        def _causal_depthwise_conv(x, conv_w, conv_b):
            K = conv_w.shape[1]
            xp = jnp.pad(x, ((0, 0), (K - 1, 0), (0, 0)))
            Lx = x.shape[1]
            out = conv_b
            for k in range(K):
                out = out + xp[:, k:k + Lx, :] * conv_w[:, k]
            return out

        def _selective_scan(x, delta, Bm, Cm, A):
            h0 = jnp.zeros((x.shape[0], A.shape[0], A.shape[1]), x.dtype)

            def step(h, inp):
                xt, dt, bt, ct = inp
                A_bar = jnp.exp(dt[..., None] * A)
                h = A_bar * h + (dt * xt)[..., None] * bt[:, None, :]
                y = jnp.einsum('ben,bn->be', h, ct)
                return (h, y)
            xs = tuple((jnp.swapaxes(a, 0, 1) for a in (x, delta, Bm, Cm)))
            _, ys = jax.lax.scan(step, h0, xs)
            return jnp.swapaxes(ys, 0, 1)
        x = _rmsnorm(resid, norm_w)
        skip = x @ skip_w.T
        x = x @ in_w.T
        x = _causal_depthwise_conv(x, conv_w, conv_b)
        x = jax.nn.silu(x)
        A = -jnp.exp(A_log)
        delta = jax.nn.softplus(x @ wd1.T @ wd2.T + wd2_b)
        Bm = x @ wb.T
        Cm = x @ wc.T
        y = _selective_scan(x, delta, Bm, Cm, A)
        y = y + x * W_D
        y = y * jax.nn.silu(skip)
        y = y @ out_w.T
        return resid + y

    def _L1_xattn_ref(query, key, value, Wq, bq, Wk, bk, Wv, bv, Wo, bo):
        import jax, jax.numpy as jnp
        import numpy as np
        QUERY_DIM = 256
        KEY_DIM = 192
        NUM_HEADS = 16
        HEAD_DIM = QUERY_DIM // NUM_HEADS
        SCALE = HEAD_DIM ** (-0.5)
        B, Nq, _ = query.shape
        Nk = key.shape[1]
        q = (query @ Wq + bq).reshape(B, Nq, NUM_HEADS, HEAD_DIM).transpose(0, 2, 1, 3)
        k = (key @ Wk + bk).reshape(B, Nk, NUM_HEADS, HEAD_DIM).transpose(0, 2, 1, 3)
        v = (value @ Wv + bv).reshape(B, Nk, NUM_HEADS, HEAD_DIM).transpose(0, 2, 1, 3)
        attn = jnp.einsum('bhqd,bhkd->bhqk', q, k) * SCALE
        attn = jax.nn.softmax(attn, axis=-1)
        out = jnp.einsum('bhqk,bhkd->bhqd', attn, v)
        out = out.transpose(0, 2, 1, 3).reshape(B, Nq, QUERY_DIM)
        return out @ Wo + bo

    def _L1_ffn_ref(x, q_node_w, q_node_b, q_w1, q_b1, q_w2, q_b2, k_node_w, k_node_b, k_w1, k_b1, k_w2, k_b2, v_node_w, v_node_b, v_w1, v_b1, v_w2, v_b2):
        import jax, jax.numpy as jnp
        import numpy as np
        LATENT = 256
        LEAF_W = 64
        DEPTH = 4
        N_LEAVES = 2 ** DEPTH
        N_NODES = 2 ** DEPTH - 1
        B, S = (4, 512)

        def _fff_params(key, prefix):
            ks = jax.random.split(key, 4)
            d, h, l, n = (LATENT, LEAF_W, N_LEAVES, N_NODES)
            s_in = 1.0 / np.sqrt(d).astype(np.float32)
            s_h = 1.0 / np.sqrt(h).astype(np.float32)
            return {f'{prefix}_node_w': jax.random.normal(ks[0], (n, d), jnp.float32) * s_in, f'{prefix}_node_b': jax.random.normal(ks[1], (n,), jnp.float32) * s_in, f'{prefix}_w1': jax.random.normal(ks[2], (l, d, h), jnp.float32) * s_in, f'{prefix}_b1': jnp.zeros((l, h), jnp.float32), f'{prefix}_w2': jax.random.normal(ks[3], (l, h, d), jnp.float32) * s_h, f'{prefix}_b2': jnp.zeros((l, d), jnp.float32)}

        def _fff(x, node_w, node_b, w1, b1, w2, b2):
            Bx, Sx, D = x.shape
            xf = x.reshape(-1, D)
            N = xf.shape[0]
            cur = jnp.zeros((N,), jnp.int32)
            for _ in range(DEPTH):
                pw = node_w[cur]
                score = jnp.einsum('nd,nd->n', xf, pw) + node_b[cur]
                cur = 2 * cur + 1 + (score >= 0).astype(jnp.int32)
            leaf = cur - N_NODES
            sel = jax.nn.one_hot(leaf, N_LEAVES, dtype=xf.dtype)
            hidden_all = jax.nn.relu(jnp.einsum('nd,ldh->lnh', xf, w1) + b1[:, None, :])
            hidden = hidden_all * sel.T[:, :, None]
            out = jnp.einsum('lnh,lho->no', hidden, w2) + sel @ b2
            return out.reshape(Bx, Sx, D)
        q = _fff(x, q_node_w, q_node_b, q_w1, q_b1, q_w2, q_b2)
        k = _fff(x, k_node_w, k_node_b, k_w1, k_b1, k_w2, k_b2)
        v = _fff(x, v_node_w, v_node_b, v_w1, v_b1, v_w2, v_b2)
        scale = 1.0 / np.sqrt(LATENT).astype(np.float32)
        attn = jax.nn.softmax(jnp.einsum('bqd,bkd->bqk', q, k) * scale, axis=-1)
        return jnp.einsum('bqk,bkd->bqd', attn, v)
    x = _layernorm(x + _L0_attn_ref(x, L0_attn_filt), axis=-1)
    x = _layernorm(x + _L0_xattn_ref(x, ctx_768, L0_xattn_Wq, L0_xattn_Wk, L0_xattn_Wv, L0_xattn_Wo, L0_xattn_bo, L0_xattn_q_down, L0_xattn_q_up, L0_xattn_q_alpha, L0_xattn_k_down, L0_xattn_k_up, L0_xattn_k_alpha, L0_xattn_v_down, L0_xattn_v_up, L0_xattn_v_alpha, L0_xattn_o_down, L0_xattn_o_up, L0_xattn_o_alpha, L0_xattn_Wk_ipa, L0_xattn_Wv_ipa), axis=-1)
    x = _layernorm(x + _L0_ffn_ref(x, L0_ffn_router_w, L0_ffn_router_b, L0_ffn_W1, L0_ffn_b1, L0_ffn_W2, L0_ffn_b2), axis=-1)
    x = _layernorm(x + _L1_attn_ref(x, L1_attn_norm_w, L1_attn_skip_w, L1_attn_in_w, L1_attn_conv_w, L1_attn_conv_b, L1_attn_wd1, L1_attn_wd2, L1_attn_wd2_b, L1_attn_wb, L1_attn_wc, L1_attn_A_log, L1_attn_W_D, L1_attn_out_w), axis=-1)
    x = _layernorm(x + _L1_xattn_ref(x, ctx_768, ctx_768, L1_xattn_Wq, L1_xattn_bq, L1_xattn_Wk, L1_xattn_bk, L1_xattn_Wv, L1_xattn_bv, L1_xattn_Wo, L1_xattn_bo), axis=-1)
    x = _layernorm(x + _L1_ffn_ref(x, L1_ffn_q_node_w, L1_ffn_q_node_b, L1_ffn_q_w1, L1_ffn_q_b1, L1_ffn_q_w2, L1_ffn_q_b2, L1_ffn_k_node_w, L1_ffn_k_node_b, L1_ffn_k_w1, L1_ffn_k_b1, L1_ffn_k_w2, L1_ffn_k_b2, L1_ffn_v_node_w, L1_ffn_v_node_b, L1_ffn_v_w1, L1_ffn_v_b1, L1_ffn_v_w2, L1_ffn_v_b2), axis=-1)
    return x

_drawn_inputs = setup_inputs


def setup_inputs(seed=0):
    import zlib

    import numpy as np

    out = dict(_drawn_inputs(seed))
    spreads = {'L0_xattn_bo': (0.0, 0.1),
     'L1_attn_norm_w': (1.0, 0.2),
     'L1_attn_conv_b': (0.0, 0.1),
     'L1_attn_wd2_b': (0.0, 0.433),
     'L1_attn_W_D': (1.0, 0.2),
     'L1_xattn_bq': (0.0, 0.322),
     'L1_xattn_bk': (0.0, 0.8),
     'L1_xattn_bv': (0.0, 0.1),
     'L1_xattn_bo': (0.0, 0.1),
     'L1_ffn_q_b1': (0.0, 0.8),
     'L1_ffn_q_b2': (0.0, 0.8),
     'L1_ffn_k_b1': (0.0, 0.8),
     'L1_ffn_k_b2': (0.0, 0.8),
     'L1_ffn_v_b1': (0.0, 0.418),
     'L1_ffn_v_b2': (0.0, 0.1)}
    factors = {'L0_xattn_Wq': 4.277,
     'L0_xattn_Wk': 7.42,
     'L0_xattn_q_down': 8.0,
     'L0_xattn_q_up': 8.0,
     'L0_xattn_k_down': 8.0,
     'L0_xattn_k_up': 8.0,
     'L0_xattn_v_down': 3.595,
     'L0_xattn_v_up': 3.439,
     'L0_xattn_Wk_ipa': 4.786,
     'L0_ffn_b1': 4.831,
     'L1_ffn_q_node_b': 8.0,
     'L1_ffn_q_w1': 2.979,
     'L1_ffn_k_node_b': 8.0,
     'L1_ffn_k_w1': 2.856}
    for name, (base, spread) in spreads.items():
        noise = np.random.default_rng([zlib.crc32(name.encode()), seed]).standard_normal(out[name].shape)
        drawn = base * np.exp(spread * noise) if base else spread * noise
        out[name] = jnp.asarray(drawn.astype(out[name].dtype))
    for name, factor in factors.items():
        out[name] = (out[name] * factor).astype(out[name].dtype)
    return out
```

```python
import concourse.bass as bass
from concourse import mybir
from contextlib import ExitStack

NB, T, D = 8, 256, 256
P = 128
NT, ND = T // P, D // P
KEYS, IPA = 120, 4
TEXT = KEYS - IPA
CTX = 192
CH = CTX // 2
RANK = 32
H0, DH0 = 16, 64
M0 = H0 * DH0 // P
H1, DH1 = 16, 16
EXPERTS, EF = 8, 128
DI, NS, DTR, KC = 512, 16, 64, 4
NM = DI // P
LEAVES, LW, NODES = 16, 64, 15
MF = LEAVES * LW // P
EPS = 1e-5
BIG = float(2.0 ** 100)

COLS = {}
_at = 0
for _name, _n in (("moe_b1", EXPERTS), ("conv_w", NM * KC), ("conv_b", NM), ("wd2_b", NM), ("W_D", NM),
                  ("x_bq", ND), ("x_bk", ND), ("f_b1", 3 * MF), ("norm_w", ND), ("A_log", NM * NS),
                  ("alpha", 4)):
    COLS[_name] = (_at, _at + _n)
    _at += _n
NCOLS = _at
ROWS = {}
_at = 0
for _name, _n in (("x0_bo", D), ("router_b", EXPERTS), ("x1_bv", D), ("x1_bo", D), ("node_b", 3 * NODES),
                  ("iota", EXPERTS)):
    ROWS[_name] = (_at, _at + _n)
    _at += _n
NROWS = _at


class Ring:

    def __init__(self, fills):
        self.order = {name: n for n, (name, _) in enumerate(fills)}
        self.bank, self.use, self.uses = {}, {}, {}
        for name, bank in fills:
            self.bank[name] = bank
            self.use[name] = self.uses.get(bank, 0)
            self.uses[bank] = self.use[name] + 1

    def filled(self, name, i):
        return i * len(self.order) + (self.order[name] + 1)

    def turn(self, name, i):
        b = self.bank[name]
        return i * self.uses[b] + (self.use[name] + 1)


def numbered(names, banks=4):
    return [(name, n % banks) for n, name in enumerate(names)]


SROUND = [("S", t, g) for t in range(NT) for g in range(4)]
TROUND = [("PT", t, g) for t in range(NT) for g in range(4)]
RING_A = Ring(numbered(
    ["conv", "x1T"] + [("q", g) for g in range(4)] + SROUND + TROUND + [("O", g) for g in range(4)]
    + ["y1", "x2T", "router", "maskT"] + [("h", g) for g in range(4)] + [("mb", g) for g in range(4)] + ["y2"]))
RING_B = Ring(
    numbered(["xrT", ("u", 0), ("u", 1), ("skip", 0), ("skip", 1), "dbc", ("z", 0), ("z", 1)])
    + [(("bc", n), n % 2) for n in range(NS)] + [(("ysum", 0), 2), (("ysum", 1), 3)]
    + numbered(["my", "x4T", "q2"] + SROUND + TROUND + [("o", 0), ("o", 1), "oT", "y3", "x5T", "node", "selT"]
               + [(s, j, g) for j in range(3) for s, n in (("hid", 4), ("out", 1)) for g in range(n)]
               + ["S3", "P3T", "y4"]))

MERGES = [("mk", c, f) for c in range(2) for f in range(2)] + [("mv", c, f) for c in range(2) for f in range(2)]
KV = ([("k", m, f) for m in range(M0) for f in range(2)] + [("v", b, f) for b in range(NB) for f in range(2)]
      + [("vi", f) for f in range(2)] + [("k2", m, f) for m in range(ND) for f in range(2)])
SETUP = (MERGES + KV + [("v2", b) for b in range(NB)] + [("mq", k, f) for k in range(ND) for f in range(2)]
         + [("mo", g) for g in range(4)])
BY_ACT = {name: n for n, name in enumerate(KV)}
BY_DVE = {name: n for n, name in enumerate([x for x in SETUP if x not in BY_ACT])}
STAGED = KV + [("v2", b) for b in range(NB)]
SLOT = {name: n for n, name in enumerate(STAGED)}
SLOTS = 4

LINKS_VEC_A, LINKS_VEC_B, LINKS_ACT_B = 26, 49, 2
LOADS = (3, 9)


def decoder(nc, x, toep, ctxT, ctxiT, cols, rows, ident_in, sel24_in, sel96_in, sel48_in,
            wq, wk, wv, wo, qdT, kdT, vdT, odT, qu, ku, vu, ou, wki, wvi,
            rw, w1, w2, b2, win, wsk, wdbc, wd2, wout, wq2, wk2, wv2, wo2, nw, fw1, fw2, fb2, out):
    fp32, bf16, u32 = mybir.dt.float32, mybir.dt.bfloat16, mybir.dt.uint32
    ALU, ACT, AX = mybir.AluOpType, mybir.ActivationFunctionType, mybir.AxisListType

    k0_all = nc.dram_tensor("k0_all", (NB, M0 * P, KEYS), fp32).ap()
    v0_all = nc.dram_tensor("v0_all", (NB, KEYS, H0 * DH0), fp32).ap()
    k2_all = nc.dram_tensor("k2_all", (NB, D, KEYS), fp32).ap()
    v2_all = nc.dram_tensor("v2_all", (NB, KEYS, H1 * (DH1 + 1)), fp32).ap()

    ctx = ExitStack()
    with ctx:
        def sb(name, shape, dt=fp32, stack=ctx):
            return stack.enter_context(nc.sbuf_tensor(name, shape, dt))

        def sem(name):
            return ctx.enter_context(nc.semaphore(name))

        Wq = sb("Wq", [P, ND, 1024]); Wo = sb("Wo", [P, M0, D])
        W1 = sb("W1", [P, ND, 1024]); W2 = sb("W2", [P, EXPERTS, D]); B2 = sb("B2", [24, D])
        Rw = sb("Rw", [P, ND, EXPERTS])
        Win = sb("Win", [P, ND, DI]); Wsk = sb("Wsk", [P, ND, DI]); Wdbc = sb("Wdbc", [P, NM, 96])
        Wd2 = sb("Wd2", [DTR, DI]); Wout = sb("Wout", [P, NM, D])
        Wq2 = sb("Wq2", [P, ND, D]); Wo2 = sb("Wo2", [P, ND, D])
        Nw = sb("Nw", [P, ND, 3 * NODES])
        FW1 = sb("FW1", [P, ND, 1024]); FW2 = sb("FW2", [P, MF, D])
        FB2 = sb("FB2", [48, 3, D])
        Toep = sb("Toep", [P, 2, P]); ident = sb("ident", [P, P])
        Sel24 = sb("Sel24", [24, EXPERTS, P], bf16); Sel96 = sb("Sel96", [96, 32, P], bf16)
        Sel48 = sb("Sel48", [48, 3, MF, P], bf16)
        Cols = sb("Cols", [P, NCOLS]); Rows = sb("Rows", [P, NROWS])
        Aneg = sb("Aneg", [P, NM, NS]); half = sb("half", [P, 4]); lora = sb("lora", [P, 4])
        xin = sb("xin", [P, NT, D])

        def col(name, n):
            a = COLS[name][0] + n
            return Cols[:, a:a + 1]

        def row(name):
            return Rows[:, ROWS[name][0]:ROWS[name][1]]

        psA = ctx.enter_context(nc.psum_tensor("psA", [P, 4, 512], fp32))
        psB = ctx.enter_context(nc.psum_tensor("psB", [P, 4, 512], fp32))

        with ExitStack() as st:
            Wk = sb("Wk", [CH, 2, 1024], stack=st); Wv = sb("Wv", [CH, 2, 1024], stack=st)
            Wki = sb("Wki", [CH, 2, 1024], stack=st); Wvi = sb("Wvi", [CH, 2, 1024], stack=st)
            Wk2 = sb("Wk2", [CH, 2, D], stack=st); Wv2 = sb("Wv2", [CH, 2, D], stack=st)
            Ct = sb("Ct", [CH, 2, NB * KEYS], stack=st); Ci = sb("Ci", [CH, 2, NB * IPA], stack=st)
            Up = sb("Up", [RANK, 3, 1024], stack=st); Ou = sb("Ou", [RANK, D], stack=st)
            Dn = sb("Dn", [RANK, 1024 + D + 2 * CTX], stack=st)
            Stage = sb("Stage", [P, SLOTS, 512], stack=st)
            V2s = sb("V2s", [KEYS, 2, H1, DH1 + 1], stack=st)
        DnO, DnQ, DnK, DnV = 0, 1024, 1024 + D, 1024 + D + CTX

        x3 = sb("x3", [P, NT, D])
        Kbd = sb("Kbd", [P, M0, 2 * KEYS]); V = sb("V", [KEYS, 1024])
        Kbd2 = sb("Kbd2", [P, ND, 8, KEYS]); V2 = sb("V2", [KEYS, H1, DH1 + 1])
        Uin = sb("Uin", [P, NM, KC - 1 + T])
        dA = sb("dA", [P, 2, NM, T])
        x6 = sb("x6", [P, NT, D])
        with ExitStack() as st:
            r = sb("r", [P, NT, D], stack=st)
            x1 = sb("x1", [P, NT, D], stack=st); x1b = sb("x1b", [P, NT, D], stack=st)
            x1T = sb("x1T", [P, ND, T], stack=st)
            qT = sb("qT", [P, M0, T], stack=st)
            Pr = sb("Pr", [P, NT, H0, KEYS], stack=st)
            PT = sb("PT", [KEYS, H0, T], stack=st)
            mx = sb("mx", [P, NT, 2, H0], stack=st); den = sb("den", [P, NT, 2, H0], stack=st)
            rden = sb("rden", [P, NT, 2, H0], stack=st)
            bn = sb("bn", [P, NT, 6], stack=st); mv = sb("mv", [P, NT, 2], stack=st)
            var = sb("var", [P, NT], stack=st); rstd = sb("rstd", [P, NT], stack=st)
            lg = sb("lg", [P, NT, EXPERTS], stack=st); lx = sb("lx", [P, NT], stack=st)
            pe_ = sb("pe_", [P, NT, EXPERTS], stack=st); top = sb("top", [P, NT, 8], stack=st)
            tix = sb("tix", [P, NT, 8], u32, stack=st); tif = sb("tif", [P, NT, 2], stack=st)
            tw = sb("tw", [P, NT, 2], stack=st); ts = sb("ts", [P, NT], stack=st); tr = sb("tr", [P, NT], stack=st)
            mk = sb("mk", [P, NT, 2, EXPERTS], stack=st); mask = sb("mask", [P, NT, EXPERTS], stack=st)
            mhi = sb("mhi", [P, NT, 2, EXPERTS], bf16, stack=st); mr = sb("mr", [P, NT, EXPERTS], stack=st)
            m3 = sb("m3", [P, NT, 3, EXPERTS], stack=st)
            mT = sb("mT", [24, T], stack=st); mTb = sb("mTb", [24, T], bf16, stack=st)
            x2 = x1b
            x2T = x1T
            OT = qT
            hT = sb("hT", [P, EXPERTS, T], stack=st)
        with ExitStack() as st:
            rB = sb("rB", [P, NT, D], stack=st); sq = sb("sq", [P, NT, D], stack=st)
            x3d = sb("x3d", [P, NT, D], stack=st); xr = sb("xr", [P, NT, D], stack=st)
            xrT = sb("xrT", [P, ND, T], stack=st)
            bnB = sb("bnB", [P, NT, 6], stack=st); mvB = sb("mvB", [P, NT, 2], stack=st)
            varB = sb("varB", [P, NT], stack=st); rstdB = sb("rstdB", [P, NT], stack=st)
            ssq = sb("ssq", [P, NT], stack=st)
            x4 = sb("x4", [P, NT, D], stack=st); x4b = sb("x4b", [P, NT, D], stack=st)
            x4T = sb("x4T", [P, ND, T], stack=st)
            with ExitStack() as mm:
                xs = sb("xs", [P, NM, T], stack=mm); gate = sb("gate", [P, NM, T], stack=mm)
                dbc = sb("dbc", [96, T], stack=mm); bcr = sb("bcr", [64, T], stack=mm)
                bc3 = sb("bc3", [96, T], bf16, stack=mm)
                dt_ = sb("dt_", [P, NM, T], stack=mm); sp = sb("sp", [P, NM, T], stack=mm)
                dtx = sb("dtx", [P, NM, T], stack=mm)
                dBx = sb("dBx", [P, 2, NM, T], stack=mm); hs = sb("hs", [P, NM, T], stack=mm)
                hC = sb("hC", [P, 2, NM, T], stack=mm); yT = sb("yT", [P, NM, T], stack=mm)
            with ExitStack() as mm:
                q2T = sb("q2T", [P, ND, T], stack=mm)
                Pr2 = sb("Pr2", [P, NT, H1, KEYS], stack=mm); PT2 = sb("PT2", [KEYS, H1, T], stack=mm)
                mx2 = sb("mx2", [P, NT, H1], stack=mm); rd2 = sb("rd2", [P, NT, H1], stack=mm)
                o2 = sb("o2", [P, NT, H1, DH1], stack=mm); o2T = sb("o2T", [P, ND, T], stack=mm)
            x5 = sb("x5", [P, NT, D], stack=st); x5T = sb("x5T", [P, ND, T], stack=st)
            with ExitStack() as mm:
                sc = sb("sc", [P, NT * 3, NODES], stack=mm); dec = sb("dec", [P, NT * 3, NODES], stack=mm)
                lv = [sb(f"lv{n}", [P, NT * 3, 2 ** (n + 1)], stack=mm) for n in range(4)]
                selT = sb("selT", [48, T], stack=mm); nsel = sb("nsel", [48, T], bf16, stack=mm)
                hid = sb("hid", [P, MF, T], stack=mm)
                qk3 = sb("qk3", [P, 2, ND, T], stack=mm); v3 = sb("v3", [P, NT, D], stack=mm)
                P3 = sb("P3", [P, NT, T], stack=mm); P3T = sb("P3T", [P, NT, T], stack=mm)
                mx3 = sb("mx3", [P, NT], stack=mm); nm3 = sb("nm3", [P, NT], stack=mm)
                den3 = sb("den3", [P, NT], stack=mm); rd3 = sb("rd3", [P, NT], stack=mm)

        weights_loaded = sem("weights_loaded"); kvw_loaded = sem("kvw_loaded")
        setup_full = sem("setup_full"); setup_act = sem("setup_act"); setup_dve = sem("setup_dve")
        setup_pool = sem("setup_pool"); setup_init = sem("setup_init")
        slot_stored = [sem(f"slot_stored{s}") for s in range(SLOTS)]
        v2_stored = [sem(f"v2_stored{s}") for s in range(2)]
        x_loaded = sem("x_loaded"); kv_loaded = sem("kv_loaded"); kv2_loaded = sem("kv2_loaded")
        out_stored = sem("out_stored")
        full_A = sem("full_A"); full_B = sem("full_B")
        free_A = [sem(f"free_A{b}") for b in range(4)]
        free_B = [sem(f"free_B{b}") for b in range(4)]
        links_vec_A = sem("links_vec_A"); links_vec_B = sem("links_vec_B"); links_act_B = sem("links_act_B")
        setup_vec = sem("setup_vec"); a_exp = sem("a_exp")
        fw1_loaded = sem("fw1_loaded"); fw2_loaded = sem("fw2_loaded")
        var_A = sem("var_A"); rstd_A = sem("rstd_A"); var_B = sem("var_B"); rstd_B = sem("rstd_B")
        x1_ready = sem("x1_ready"); x1b_ready = sem("x1b_ready")
        exp_done = sem("exp_done"); den_ready = sem("den_ready"); probs_ready = sem("probs_ready")
        x2_ready = sem("x2_ready"); logits_ready = sem("logits_ready"); gates_exp = sem("gates_exp")
        mask_ready = sem("mask_ready"); x3_ready = sem("x3_ready")
        sq_done = sem("sq_done"); xr_ready = sem("xr_ready"); conv_ready = sem("conv_ready")
        xs_ready = sem("xs_ready"); dbc_ready = sem("dbc_ready"); bc_hi = sem("bc_hi"); bc3_ready = sem("bc3_ready")
        dt_act = sem("dt_act"); dt_ready = sem("dt_ready"); dA_ready = sem("dA_ready")
        scan_done = sem("scan_done"); summed = sem("summed"); yT_ready = sem("yT_ready")
        x4_ready = sem("x4_ready"); x4b_ready = sem("x4b_ready"); exp2_done = sem("exp2_done")
        alone_vec = sem("alone_vec"); alone_pe = sem("alone_pe")
        x5_ready = sem("x5_ready"); sel_ready = sem("sel_ready"); selT_ready = sem("selT_ready")
        mx3_ready = sem("mx3_ready"); x6_ready = sem("x6_ready")

        def bA(name):
            return psA[:, RING_A.bank[name], :]

        def bB(name):
            return psB[:, RING_B.bank[name], :]

        weights = [
            (Rows[:], rows), (Cols[:], cols), (ident[:], ident_in),
            (Toep[:], toep.rearrange("k p t -> p k t")),
            (Wq[:], wq.rearrange("(k p) n -> p k n", p=P)), (Wo[:], wo.rearrange("(m p) n -> p m n", p=P)),
            (W1[:], w1.rearrange("(k p) n -> p k n", p=P)), (W2[:], w2.rearrange("e f n -> f e n")),
            (B2[:], b2), (Rw[:], rw.rearrange("(k p) n -> p k n", p=P)),
            (Win[:], win.rearrange("(k p) n -> p k n", p=P)), (Wsk[:], wsk.rearrange("(k p) n -> p k n", p=P)),
            (Wdbc[:], wdbc.rearrange("(k p) n -> p k n", p=P)), (Wd2[:], wd2),
            (Wout[:], wout.rearrange("(k p) n -> p k n", p=P)),
            (Wq2[:], wq2.rearrange("(k p) n -> p k n", p=P)), (Wo2[:], wo2.rearrange("(k p) n -> p k n", p=P)),
            (Nw[:], nw.rearrange("(k p) n -> p k n", p=P)),
            (FB2[:], fb2.rearrange("j r n -> r j n")),
            (Sel24[:], sel24_in), (Sel96[:], sel96_in), (Sel48[:], sel48_in),
            (Dn[:, DnO:DnQ], odT), (Dn[:, DnQ:DnK], qdT), (Up[:, 0], qu), (Ou[:], ou),
        ]
        N_WEIGHTS = len(weights)
        kv_weights = [
            (Dn[:, DnK:DnV], kdT), (Dn[:, DnV:DnV + CTX], vdT), (Up[:, 1], ku), (Up[:, 2], vu),
            (Wk[:], wk.rearrange("(c p) n -> p c n", p=CH)), (Wv[:], wv.rearrange("(c p) n -> p c n", p=CH)),
            (Ct[:], ctxT.rearrange("(c p) n -> p c n", p=CH)), (Ci[:], ctxiT.rearrange("(c p) n -> p c n", p=CH)),
            (Wki[:], wki.rearrange("(c p) n -> p c n", p=CH)), (Wvi[:], wvi.rearrange("(c p) n -> p c n", p=CH)),
            (Wk2[:], wk2.rearrange("(c p) n -> p c n", p=CH)), (Wv2[:], wv2.rearrange("(c p) n -> p c n", p=CH)),
        ]

        block = ctx.enter_context(nc.Block())

        def stored_by(n, s):
            return sum(16 * (NB if name[0] == "vi" else 1) for name in STAGED[:n]
                       if name[0] != "v2" and SLOT[name] % SLOTS == s)

        @block.sync
        def _(sp):
            def load_x(b):
                src = x[bass.ts(b, 1)] if not isinstance(b, int) else x[b:b + 1]
                sp.dma_start(xin[:], src.rearrange("o (t p) d -> p (o t) d", p=P)).then_inc(x_loaded, 16)

            def load_kv(b):
                k = k0_all[bass.ts(b, 1)] if not isinstance(b, int) else k0_all[b:b + 1]
                v = v0_all[bass.ts(b, 1)] if not isinstance(b, int) else v0_all[b:b + 1]
                for e in range(2):
                    sp.dma_start(Kbd[64 * e:64 * e + 64, :, e * KEYS:(e + 1) * KEYS],
                                 k.rearrange("o (m e p) j -> e p (o m) j", e=2, p=64)[e]).then_inc(kv_loaded, 16)
                sp.dma_start(V[:], v.rearrange("o j n -> j (o n)")).then_inc(kv_loaded, 16)

            def load_kv2(b):
                k = k2_all[bass.ts(b, 1)] if not isinstance(b, int) else k2_all[b:b + 1]
                v = v2_all[bass.ts(b, 1)] if not isinstance(b, int) else v2_all[b:b + 1]
                kk = k.rearrange("o (m h p) j -> h p (o m) j", h=8, p=DH1)
                for h in range(8):
                    sp.dma_start(Kbd2[DH1 * h:DH1 * (h + 1), :, h, :], kk[h]).then_inc(kv2_loaded, 16)
                sp.dma_start(V2[:].rearrange("j h d -> j (h d)"), v.rearrange("o j n -> j (o n)")).then_inc(kv2_loaded, 16)

            def load_fw1(j):
                sp.dma_start(FW1[:], fw1[j].rearrange("(k p) n -> p k n", p=P)).then_inc(fw1_loaded, 16)

            def load_fw2(j):
                sp.dma_start(FW2[:], fw2[j].rearrange("(m p) n -> p m n", p=P)).then_inc(fw2_loaded, 16)

            def store(b):
                dst = out[bass.ts(b, 1)] if not isinstance(b, int) else out[b:b + 1]
                sp.dma_start(dst.rearrange("o (t p) d -> p (o t) d", p=P), x6[:]).then_inc(out_stored, 16)

            for dst, src in kv_weights:
                sp.dma_start(dst, src).then_inc(kvw_loaded, 16)
            for dst, src in weights:
                sp.dma_start(dst, src).then_inc(weights_loaded, 16)
            load_x(0)
            load_fw1(0)
            load_fw2(0)
            for name in STAGED:
                s = SLOT[name] % SLOTS
                if name[0] == "v2":
                    b = name[1]
                    sp.wait_ge(setup_dve, BY_DVE[name] + 1)
                    sp.dma_start(v2_all[b], V2s[:, b % 2].rearrange("j h d -> j (h d)")).then_inc(v2_stored[b % 2], 16)
                    continue
                sp.wait_ge(setup_act, BY_ACT[name] + 1)
                if name[0] == "k":
                    _, m, f = name
                    sp.dma_start(k0_all[4 * f:4 * f + 4, m * P:(m + 1) * P, :].rearrange("b p j -> p b j"),
                                 Stage[:, s, 0:4 * KEYS].rearrange("p (b j) -> p b j", j=KEYS)).then_inc(slot_stored[s], 16)
                elif name[0] == "v":
                    _, b, f = name
                    sp.dma_start(v0_all[b, 0:TEXT, f * 512:(f + 1) * 512], Stage[0:TEXT, s, :]).then_inc(slot_stored[s], 16)
                elif name[0] == "vi":
                    f = name[1]
                    for b in range(NB):
                        sp.dma_start(v0_all[b, TEXT:KEYS, f * 512:(f + 1) * 512],
                                     Stage[IPA * b:IPA * (b + 1), s, :]).then_inc(slot_stored[s], 16)
                else:
                    _, m, f = name
                    sp.dma_start(k2_all[4 * f:4 * f + 4, m * P:(m + 1) * P, :].rearrange("b p j -> p b j"),
                                 Stage[:, s, 0:4 * KEYS].rearrange("p (b j) -> p b j", j=KEYS)).then_inc(slot_stored[s], 16)
            for s in range(SLOTS):
                sp.wait_ge(slot_stored[s], stored_by(len(SLOT), s))
            for s in range(2):
                sp.wait_ge(v2_stored[s], 16 * NB // 2)
            sp.wait_ge(setup_init, 1)
            load_kv(0)
            load_kv2(0)
            def nets(hid_taken, out_taken, again):
                for j in range(3):
                    if j < 2 or again:
                        sp.wait_ge(free_B[RING_B.bank["hid", j, 3]], hid_taken[j])
                        load_fw1((j + 1) % 3)
                        sp.wait_ge(free_B[RING_B.bank["out", j, 0]], out_taken[j])
                        load_fw2((j + 1) % 3)

            with sp.Fori(0, NB - 1) as i:
                nxt = sp.snap(i + 1)
                done = sp.snap(i + 2)
                o_taken = sp.snap(RING_A.turn(("O", 3), i) + 1)
                o2_taken = sp.snap(RING_B.turn(("o", 1), i) + 1)
                hid_taken = [sp.snap(RING_B.turn(("hid", j, 3), i) + 1) for j in range(3)]
                out_taken = [sp.snap(RING_B.turn(("out", j, 0), i) + 1) for j in range(3)]
                sp.wait_ge(x1_ready, nxt)
                load_x(nxt)
                sp.wait_ge(free_A[RING_A.bank["O", 3]], o_taken)
                load_kv(nxt)
                sp.wait_ge(free_B[RING_B.bank["o", 1]], o2_taken)
                load_kv2(nxt)
                nets(hid_taken, out_taken, True)
                sp.wait_ge(x6_ready, done)
                store(i)
            nets([RING_B.turn(("hid", j, 3), NB - 1) + 1 for j in range(3)],
                 [RING_B.turn(("out", j, 0), NB - 1) + 1 for j in range(3)], False)
            sp.wait_ge(x6_ready, NB + 1)
            store(NB - 1)
            sp.wait_ge(out_stored, 16 * NB + 16)

        @block.gpsimd
        def _(po):
            for s in free_A + free_B:
                po.sem_inc(s, 1)
            po.sem_inc(out_stored, 16)
            po.sem_inc(x6_ready, 1)
            nc.gpsimd.memset(half[:], -0.5).then_inc(setup_pool, 1)
            po.wait_ge(setup_pool, 1)
            nc.gpsimd.memset(V2s[:], 1.0).then_inc(setup_pool, 1)
            for s in range(2):
                po.wait_ge(v2_stored[s], 16 * NB // 2)
            for s in range(SLOTS):
                po.wait_ge(slot_stored[s], stored_by(len(SLOT), s))
            po.wait_ge(setup_dve, len(BY_DVE))
            nc.gpsimd.memset(Kbd[:], 0.0)
            nc.gpsimd.memset(Kbd2[:], 0.0)
            nc.gpsimd.memset(dA[:], 0.0)
            nc.gpsimd.memset(Uin[:], 0.0).then_inc(setup_init, 1)
            po.wait_ge(setup_init, 1)

            def rsqrt_A(n, i):
                po.wait_ge(var_A, i * 3 + (n + 1))
                nc.gpsimd.tensor_tensor(rstd[:], var[:], half[:, 0:NT], ALU.pow).then_inc(rstd_A, 1)

            def rsqrt_B(n, i):
                po.wait_ge(var_B, i * 4 + (n + 1))
                nc.gpsimd.tensor_tensor(rstdB[:], varB[:], half[:, 0:NT], ALU.pow).then_inc(rstd_B, 1)

            def pool_A(i):
                rsqrt_A(0, i)
                po.wait_ge(x1_ready, i + 1)
                nc.gpsimd.tensor_tensor(x1b[:], x1[:], row("x0_bo").unsqueeze(1).broadcast_to([P, NT, D]), ALU.add)\
                    .then_inc(x1b_ready, 1)
                for t in range(NT):
                    po.wait_ge(den_ready, i * NT + (t + 1))
                    nc.gpsimd.tensor_tensor(Pr[:, t, :, 0:TEXT], Pr[:, t, :, 0:TEXT],
                                            rden[:, t, 0, :].unsqueeze(2).broadcast_to([P, H0, TEXT]), ALU.mult)
                    nc.gpsimd.tensor_tensor(Pr[:, t, :, TEXT:KEYS], Pr[:, t, :, TEXT:KEYS],
                                            rden[:, t, 1, :].unsqueeze(2).broadcast_to([P, H0, IPA]), ALU.mult)\
                        .then_inc(probs_ready, 1)
                rsqrt_A(1, i)
                rsqrt_A(2, i)

            def pool_B(i):
                rsqrt_B(0, i)
                rsqrt_B(1, i)
                po.wait_ge(x4_ready, i + 1)
                nc.gpsimd.tensor_tensor(x4b[:], x4[:], row("x1_bo").unsqueeze(1).broadcast_to([P, NT, D]), ALU.add)\
                    .then_inc(x4b_ready, 1)
                rsqrt_B(2, i)
                rsqrt_B(3, i)

            po.wait_ge(weights_loaded, 16 * N_WEIGHTS)
            with po.Fori(0, NB) as i:
                pool_A(i)
                pool_B(i)

        @block.scalar
        def _(act):
            act.wait_ge(weights_loaded, 16 * N_WEIGHTS)
            a0, a1 = COLS["A_log"]
            nc.scalar.activation(Aneg[:], Cols[:, a0:a1].rearrange("p (m n) -> p m n", n=NS), ACT.Exp)\
                .then_inc(a_exp, 1)
            for name in KV:
                n = BY_ACT[name]
                s = SLOT[name] % SLOTS
                bank = SETUP.index(name) % 8
                ps = (psA if bank < 4 else psB)[:, bank % 4, :]
                act.wait_ge(setup_full, SETUP.index(name) + 1)
                if SLOT[name] >= SLOTS:
                    act.wait_ge(slot_stored[s], stored_by(SLOT[name], s))
                if name[0] == "k":
                    nc.scalar.activation(Stage[:, s, 0:480], ps[:, 0:480], ACT.Copy).then_inc(setup_act, 1)
                elif name[0] == "v":
                    nc.scalar.activation(Stage[0:KEYS, s, :], ps[0:KEYS, :], ACT.Copy).then_inc(setup_act, 1)
                elif name[0] == "vi":
                    nc.scalar.activation(Stage[0:NB * IPA, s, :], ps[0:NB * IPA, :], ACT.Copy).then_inc(setup_act, 1)
                else:
                    nc.scalar.activation(Stage[:, s, 0:480], ps[:, 0:480], ACT.Identity,
                                         bias=col("x_bk", name[1])).then_inc(setup_act, 1)
            act.wait_ge(setup_init, 1)
            act.wait_ge(setup_vec, 1)

            def take_A(name, i):
                act.wait_ge(full_A, RING_A.filled(name, i))

            def take_B(name, i):
                act.wait_ge(full_B, RING_B.filled(name, i))

            def act_A(i):
                take_A("x1T", i)
                nc.scalar.activation(x1T[:].rearrange("p k t -> p (k t)"), bA("x1T"), ACT.Copy)\
                    .then_inc(free_A[RING_A.bank["x1T"]], 1)
                for g in range(4):
                    take_A(("q", g), i)
                    nc.scalar.activation(qT[:, 2 * g:2 * g + 2, :].rearrange("p m t -> p (m t)"), bA(("q", g)), ACT.Copy)\
                        .then_inc(free_A[RING_A.bank["q", g]], 1)
                for t in range(NT):
                    act.wait_ge(free_A[RING_A.bank["S", t, 3]], RING_A.turn(("S", t, 3), i) + 1)
                    nc.scalar.activation(Pr[:, t].rearrange("p h j -> p (h j)"), Pr[:, t].rearrange("p h j -> p (h j)"),
                                         ACT.Exp, scale=DH0 ** -0.5).then_inc(exp_done, 1)
                for _, t, g in TROUND:
                    take_A(("PT", t, g), i)
                    nc.scalar.activation(PT[:, 4 * g:4 * g + 4, t * P:(t + 1) * P],
                                         bA(("PT", t, g))[0:KEYS].rearrange("j (h t) -> j h t", t=P), ACT.Copy)\
                        .then_inc(free_A[RING_A.bank["PT", t, g]], 1)
                for g in range(4):
                    take_A(("O", g), i)
                    nc.scalar.activation(OT[:, 2 * g:2 * g + 2, :].rearrange("p m t -> p (m t)"), bA(("O", g)), ACT.Copy)\
                        .then_inc(free_A[RING_A.bank["O", g]], 1)
                take_A("x2T", i)
                nc.scalar.activation(x2T[:].rearrange("p k t -> p (k t)"), bA("x2T"), ACT.Copy)\
                    .then_inc(free_A[RING_A.bank["x2T"]], 1)
                act.wait_ge(logits_ready, i + 1)
                nc.scalar.activation(pe_[:], lg[:], ACT.Exp).then_inc(gates_exp, 1)
                for g in range(4):
                    take_A(("h", g), i)
                    for e in (2 * g, 2 * g + 1):
                        last = nc.scalar.activation(hT[:, e, :], bA(("h", g))[:, (e % 2) * T:(e % 2 + 1) * T],
                                                    ACT.Gelu, bias=col("moe_b1", e))
                    last.then_inc(free_A[RING_A.bank["h", g]], 1)

            def act_B(i):
                c = 0

                def link(ins):
                    nonlocal c
                    c += 1
                    ins.then_inc(links_act_B, 1)
                    act.wait_ge(links_act_B, i * LINKS_ACT_B + c)

                act.wait_ge(x3_ready, i + 1)
                nc.scalar.activation(sq[:, 0], x3[:, 0], ACT.Square, accum_out=ssq[:, 0:1])
                nc.scalar.activation(sq[:, 1], x3[:, 1], ACT.Square, accum_out=ssq[:, 1:2]).then_inc(sq_done, 1)
                take_B("xrT", i)
                nc.scalar.activation(xrT[:].rearrange("p k t -> p (k t)"), bB("xrT"), ACT.Copy)\
                    .then_inc(free_B[RING_B.bank["xrT"]], 1)
                for g in range(2):
                    take_B(("u", g), i)
                    nc.scalar.activation(Uin[:, 2 * g:2 * g + 2, KC - 1:],
                                         bB(("u", g)).rearrange("p (m t) -> p m t", t=T), ACT.Copy)\
                        .then_inc(free_B[RING_B.bank["u", g]], 1)
                for g in range(2):
                    take_B(("skip", g), i)
                    nc.scalar.activation(gate[:, 2 * g:2 * g + 2, :].rearrange("p m t -> p (m t)"), bB(("skip", g)),
                                         ACT.Silu).then_inc(free_B[RING_B.bank["skip", g]], 1)
                for g in range(2):
                    act.wait_ge(conv_ready, i * 2 + (g + 1))
                    nc.scalar.activation(xs[:, 2 * g:2 * g + 2], xs[:, 2 * g:2 * g + 2], ACT.Silu).then_inc(xs_ready, 1)
                take_B("dbc", i)
                nc.scalar.activation(bc3[0:32], bB("dbc")[64:96, 0:T], ACT.Copy).then_inc(bc_hi, 1)
                act.wait_ge(bc_hi, i + 1)
                nc.scalar.activation(dbc[0:DTR], bB("dbc")[0:DTR, 0:T], ACT.Copy).then_inc(dbc_ready, 1)
                for m in range(NM):
                    if m % 2 == 0:
                        take_B(("z", m // 2), i)
                    ins = nc.scalar.activation(dt_[:, m], bB(("z", m // 2))[:, (m % 2) * T:(m % 2 + 1) * T],
                                               ACT.Identity, bias=col("wd2_b", m))
                    if m % 2:
                        ins.then_inc(free_B[RING_B.bank["z", m // 2]], 1)
                act.wait_ge(free_B[RING_B.bank["z", 1]], RING_B.turn(("z", 1), i) + 1)
                link(nc.scalar.activation(sp[:], dt_[:], ACT.Abs))
                link(nc.scalar.activation(sp[:], sp[:], ACT.Exp, scale=-1.0))
                nc.scalar.activation(sp[:], sp[:], ACT.Ln, bias=1.0).then_inc(dt_act, 1)
                act.wait_ge(dt_ready, i + 1)
                for n in range(NS):
                    if n >= 2:
                        act.wait_ge(scan_done, i * NS + (n - 1))
                    for m in range(NM):
                        last = nc.scalar.activation(dA[:, n % 2, m, 1:T], dt_[:, m, 1:T], ACT.Exp,
                                                    scale=Aneg[:, m, n:n + 1])
                    last.then_inc(dA_ready, 1)
                take_B("x4T", i)
                nc.scalar.activation(x4T[:].rearrange("p k t -> p (k t)"), bB("x4T"), ACT.Copy)\
                    .then_inc(free_B[RING_B.bank["x4T"]], 1)
                take_B("q2", i)
                for m in range(ND):
                    last = nc.scalar.activation(q2T[:, m], bB("q2")[:, m * T:(m + 1) * T], ACT.Identity,
                                                bias=col("x_bq", m))
                last.then_inc(free_B[RING_B.bank["q2"]], 1)
                for t in range(NT):
                    act.wait_ge(free_B[RING_B.bank["S", t, 3]], RING_B.turn(("S", t, 3), i) + 1)
                    nc.scalar.activation(Pr2[:, t].rearrange("p h j -> p (h j)"), Pr2[:, t].rearrange("p h j -> p (h j)"),
                                         ACT.Exp, scale=DH1 ** -0.5).then_inc(exp2_done, 1)
                for _, t, g in TROUND:
                    take_B(("PT", t, g), i)
                    nc.scalar.activation(PT2[:, 4 * g:4 * g + 4, t * P:(t + 1) * P],
                                         bB(("PT", t, g))[0:KEYS].rearrange("j (h t) -> j h t", t=P), ACT.Copy)\
                        .then_inc(free_B[RING_B.bank["PT", t, g]], 1)
                take_B("oT", i)
                nc.scalar.activation(o2T[:].rearrange("p k t -> p (k t)"), bB("oT"), ACT.Copy)\
                    .then_inc(free_B[RING_B.bank["oT"]], 1)
                take_B("x5T", i)
                nc.scalar.activation(x5T[:].rearrange("p k t -> p (k t)"), bB("x5T"), ACT.Copy)\
                    .then_inc(free_B[RING_B.bank["x5T"]], 1)
                take_B("selT", i)
                nc.scalar.activation(selT[:], bB("selT")[0:48, 0:T], ACT.Copy).then_inc(selT_ready, 1)
                for j in range(3):
                    for g in (0, 2):
                        take_B(("hid", j, g), i)
                        for m in (2 * g, 2 * g + 1):
                            last = nc.scalar.activation(hid[:, m], bB(("hid", j, g))[:, (m % 2) * T:(m % 2 + 1) * T],
                                                        ACT.Relu, bias=col("f_b1", MF * j + m))
                        last.then_inc(free_B[RING_B.bank["hid", j, g]], 1)
                    take_B(("out", j, 0), i)
                    dst = qk3[:, j].rearrange("p k t -> p (k t)") if j < 2 else v3[:].rearrange("p t d -> p (t d)")
                    nc.scalar.activation(dst, bB(("out", j, 0)), ACT.Copy).then_inc(free_B[RING_B.bank["out", j, 0]], 1)
                act.wait_ge(mx3_ready, i + 1)
                for t in range(NT):
                    last = nc.scalar.activation(P3[:, t], bB("S3")[:, t * T:(t + 1) * T], ACT.Exp, bias=nm3[:, t:t + 1],
                                                scale=D ** -0.5, accum_out=den3[:, t:t + 1])
                last.then_inc(free_B[RING_B.bank["S3"]], 1)
                take_B("P3T", i)
                nc.scalar.activation(P3T[:].rearrange("p k t -> p (k t)"), bB("P3T"), ACT.Copy)\
                    .then_inc(free_B[RING_B.bank["P3T"]], 1)
                assert c == LINKS_ACT_B, c

            with act.Fori(0, NB) as i:
                act_A(i)
                act_B(i)

        @block.vector
        def _(dve):
            vec = nc.vector

            dve.wait_ge(weights_loaded, 16 * N_WEIGHTS)
            dve.wait_ge(kvw_loaded, 16 * len(kv_weights))
            vec.tensor_scalar(lora[:], Cols[:, COLS["alpha"][0]:COLS["alpha"][1]], 1.0 / RANK, None, ALU.mult)\
                .then_inc(setup_vec, 1)
            dve.wait_ge(setup_vec, 1)
            merged = {"mq": (0, Wq), "mk": (1, Wk), "mv": (2, Wv), "mo": (3, Wo)}
            for name in BY_DVE:
                at = SETUP.index(name)
                ps = (psA if at % 8 < 4 else psB)[:, at % 4, :]
                dve.wait_ge(setup_full, at + 1)
                kind, f = name[0], name[-1]
                if kind == "v2":
                    if f == 0:
                        dve.wait_ge(setup_pool, 2)
                    if f >= 2:
                        dve.wait_ge(v2_stored[f % 2], 16 * (f // 2))
                    vec.tensor_tensor(V2s[:, f % 2, :, 0:DH1], ps[0:KEYS, 0:D].rearrange("j (h d) -> j h d", d=DH1),
                                      row("x1_bv")[0:KEYS].rearrange("j (h d) -> j h d", d=DH1), ALU.add)\
                        .then_inc(setup_dve, 1)
                    continue
                n, W = merged[kind]
                if kind == "mo":
                    w = W[:, 2 * f:2 * f + 2, :].rearrange("p m n -> p (m n)")
                else:
                    w = W[:, name[1], f * 512:(f + 1) * 512]
                h = CH if kind in ("mk", "mv") else P
                vec.scalar_tensor_tensor(w, ps[0:h], lora[0:h, n:n + 1], w, ALU.mult, ALU.add).then_inc(setup_dve, 1)
            for W in (Win, Wsk):
                for k in range(ND):
                    vec.tensor_scalar(W[:, k], W[:, k], col("norm_w", k), None, ALU.mult)
            dve.wait_ge(a_exp, 1)
            vec.tensor_scalar(Aneg[:], Aneg[:], -1.0, None, ALU.mult).then_inc(setup_vec, 1)
            dve.wait_ge(setup_init, 1)

            def dve_A(i):
                c = 0

                def link(ins):
                    nonlocal c
                    c += 1
                    ins.then_inc(links_vec_A, 1)
                    dve.wait_ge(links_vec_A, i * LINKS_VEC_A + c)

                def take(name):
                    dve.wait_ge(full_A, RING_A.filled(name, i))

                def give(ins, name):
                    ins.then_inc(free_A[RING_A.bank[name]], 1)

                def given(name):
                    dve.wait_ge(free_A[RING_A.bank[name]], RING_A.turn(name, i) + 1)

                def layernorm(n, dst, ready):
                    for t in range(NT):
                        last = vec.bn_stats(bn[:, t], r[:, t])
                    link(last)
                    dve.sem_inc(alone_vec, 1)
                    for t in range(NT):
                        last = vec.bn_aggr(mv[:, t], bn[:, t])
                    link(last)
                    vec.tensor_scalar(var[:], mv[:, :, 1], EPS, None, ALU.add).then_inc(var_A, 1)
                    dve.wait_ge(rstd_A, i * 3 + (n + 1))
                    for t in range(NT):
                        last = vec.tensor_scalar(dst[:, t], r[:, t], mv[:, t, 0:1], rstd[:, t:t + 1], ALU.subtract, ALU.mult)
                    last.then_inc(ready, 1)

                dve.wait_ge(x6_ready, i + 1)
                take("conv")
                give(vec.tensor_tensor(r[:].rearrange("p t d -> p (t d)"), bA("conv"),
                                       xin[:].rearrange("p t d -> p (t d)"), ALU.add), "conv")
                given("conv")
                layernorm(0, x1, x1_ready)
                for _, t, g in SROUND:
                    take(("S", t, g))
                    hs4 = slice(4 * g, 4 * g + 4)
                    s4 = bA(("S", t, g))[:, 0:4 * KEYS].rearrange("p (h j) -> p h j", j=KEYS)
                    vec.tensor_reduce(mx[:, t, 0, hs4], s4[:, :, 0:TEXT], AX.X, ALU.max)
                    link(vec.tensor_reduce(mx[:, t, 1, hs4], s4[:, :, TEXT:KEYS], AX.X, ALU.max))
                    vec.tensor_tensor(Pr[:, t, hs4, 0:TEXT], s4[:, :, 0:TEXT],
                                      mx[:, t, 0, hs4].unsqueeze(2).broadcast_to([P, 4, TEXT]), ALU.subtract)
                    give(vec.tensor_tensor(Pr[:, t, hs4, TEXT:KEYS], s4[:, :, TEXT:KEYS],
                                           mx[:, t, 1, hs4].unsqueeze(2).broadcast_to([P, 4, IPA]), ALU.subtract),
                         ("S", t, g))
                for t in range(NT):
                    dve.wait_ge(exp_done, i * NT + (t + 1))
                    vec.tensor_reduce(den[:, t, 0], Pr[:, t, :, 0:TEXT], AX.X, ALU.add)
                    link(vec.tensor_reduce(den[:, t, 1], Pr[:, t, :, TEXT:KEYS], AX.X, ALU.add))
                    vec.reciprocal(rden[:, t], den[:, t]).then_inc(den_ready, 1)
                take("y1")
                dve.wait_ge(x1b_ready, i + 1)
                give(vec.tensor_tensor(r[:].rearrange("p t d -> p (t d)"), bA("y1"),
                                       x1b[:].rearrange("p t d -> p (t d)"), ALU.add), "y1")
                given("y1")
                layernorm(1, x2, x2_ready)
                take("router")
                give(vec.tensor_tensor(lg[:], bA("router")[:, 0:NT * EXPERTS].rearrange("p (t e) -> p t e", e=EXPERTS),
                                       row("router_b").unsqueeze(1).broadcast_to([P, NT, EXPERTS]), ALU.add), "router")
                given("router")
                link(vec.tensor_reduce(lx[:], lg[:], AX.X, ALU.max))
                vec.tensor_tensor(lg[:], lg[:], lx[:].unsqueeze(2).broadcast_to([P, NT, EXPERTS]), ALU.subtract)\
                    .then_inc(logits_ready, 1)
                dve.wait_ge(gates_exp, i + 1)
                dve.sem_inc(alone_vec, 1)
                for t in range(NT):
                    last = vec.max(top[:, t], pe_[:, t])
                link(last)
                dve.sem_inc(alone_vec, 1)
                for t in range(NT):
                    vec.max_index(tix[:, t], top[:, t], pe_[:, t])
                link(vec.tensor_tensor(ts[:], top[:, :, 0], top[:, :, 1], ALU.add))
                vec.tensor_copy(tif[:], tix[:, :, 0:2])
                link(vec.reciprocal(tr[:], ts[:]))
                link(vec.tensor_tensor(tw[:], top[:, :, 0:2], tr[:].unsqueeze(2).broadcast_to([P, NT, 2]), ALU.mult))
                for t in range(NT):
                    for s in range(2):
                        last = vec.tensor_scalar(mk[:, t, s], row("iota"), tif[:, t, s:s + 1], tw[:, t, s:s + 1],
                                                 ALU.is_equal, ALU.mult)
                link(last)
                link(vec.tensor_tensor(mask[:], mk[:, :, 0], mk[:, :, 1], ALU.add))
                link(vec.tensor_copy(mhi[:, :, 0], mask[:]))
                vec.tensor_copy(m3[:, :, 0], mhi[:, :, 0])
                link(vec.tensor_tensor(mr[:], mask[:], mhi[:, :, 0], ALU.subtract))
                link(vec.tensor_copy(mhi[:, :, 1], mr[:]))
                vec.tensor_copy(m3[:, :, 1], mhi[:, :, 1])
                vec.tensor_tensor(m3[:, :, 2], mr[:], mhi[:, :, 1], ALU.subtract).then_inc(mask_ready, 1)
                take("maskT")
                vec.tensor_copy(mT[:], bA("maskT")[0:24, 0:T])
                give(vec.tensor_copy(mTb[:], bA("maskT")[0:24, 0:T]), "maskT")
                for g in range(4):
                    given(("h", g))
                    take(("mb", g))
                    h2 = hT[:, 2 * g:2 * g + 2, :].rearrange("p e t -> p (e t)")
                    give(vec.tensor_tensor(h2, h2, bA(("mb", g)), ALU.mult), ("mb", g))
                take("y2")
                give(vec.tensor_tensor(r[:].rearrange("p t d -> p (t d)"), bA("y2"),
                                       x2[:].rearrange("p t d -> p (t d)"), ALU.add), "y2")
                given("y2")
                layernorm(2, x3, x3_ready)
                assert c == LINKS_VEC_A, ("LINKS_VEC_A", c)

            def dve_B(i):
                c = 0

                def link(ins):
                    nonlocal c
                    c += 1
                    ins.then_inc(links_vec_B, 1)
                    dve.wait_ge(links_vec_B, i * LINKS_VEC_B + c)

                def take(name):
                    dve.wait_ge(full_B, RING_B.filled(name, i))

                def give(ins, name):
                    ins.then_inc(free_B[RING_B.bank[name]], 1)

                def given(name):
                    dve.wait_ge(free_B[RING_B.bank[name]], RING_B.turn(name, i) + 1)

                def layernorm(n, dst, ready):
                    for t in range(NT):
                        last = vec.bn_stats(bnB[:, t], rB[:, t])
                    link(last)
                    dve.sem_inc(alone_vec, 1)
                    for t in range(NT):
                        last = vec.bn_aggr(mvB[:, t], bnB[:, t])
                    link(last)
                    vec.tensor_scalar(varB[:], mvB[:, :, 1], EPS, None, ALU.add).then_inc(var_B, 1)
                    dve.wait_ge(rstd_B, i * 4 + (n + 1))
                    for t in range(NT):
                        last = vec.tensor_scalar(dst[:, t], rB[:, t], mvB[:, t, 0:1], rstdB[:, t:t + 1],
                                                 ALU.subtract, ALU.mult)
                    last.then_inc(ready, 1)

                dve.wait_ge(x3_ready, i + 1)
                vec.tensor_scalar(x3d[:], x3[:], 2.0, None, ALU.mult)
                dve.wait_ge(sq_done, i + 1)
                vec.tensor_scalar(varB[:], ssq[:], 1.0 / D, EPS, ALU.mult, ALU.add).then_inc(var_B, 1)
                dve.wait_ge(rstd_B, i * 4 + 1)
                for t in range(NT):
                    last = vec.tensor_scalar(xr[:, t], x3[:, t], rstdB[:, t:t + 1], None, ALU.mult)
                last.then_inc(xr_ready, 1)
                for g in range(2):
                    given(("u", g))
                    ms = (2 * g, 2 * g + 1)
                    for m in ms:
                        last = vec.tensor_scalar(xs[:, m], Uin[:, m, 0:T], col("conv_w", KC * m), col("conv_b", m),
                                                 ALU.mult, ALU.add)
                    link(last)
                    for k in range(1, KC):
                        for m in ms:
                            last = vec.scalar_tensor_tensor(xs[:, m], Uin[:, m, k:k + T], col("conv_w", KC * m + k),
                                                            xs[:, m], ALU.mult, ALU.add)
                        if k < KC - 1:
                            link(last)
                    last.then_inc(conv_ready, 1)
                dve.wait_ge(dbc_ready, i + 1)
                give(vec.tensor_tensor(bcr[32:64], bB("dbc")[64:96, 0:T], bc3[0:32], ALU.subtract), "dbc")
                given("dbc")
                link(vec.tensor_copy(bc3[32:64], bcr[32:64]))
                vec.tensor_tensor(bc3[64:96], bcr[32:64], bc3[32:64], ALU.subtract).then_inc(bc3_ready, 1)
                dve.wait_ge(dt_act, i + 1)
                vec.scalar_tensor_tensor(dt_[:].rearrange("p m t -> p (m t)"), dt_[:].rearrange("p m t -> p (m t)"), 0.0,
                                         sp[:].rearrange("p m t -> p (m t)"), ALU.max, ALU.add).then_inc(dt_ready, 1)
                dve.wait_ge(dt_ready, i + 1)
                link(vec.tensor_tensor(dtx[:], dt_[:], xs[:], ALU.mult))
                for n in range(NS):
                    take(("bc", n))
                    bc = bB(("bc", n)).rearrange("p (s t) -> p s t", s=2)
                    link(vec.tensor_tensor(dBx[:, n % 2], dtx[:], bc[:, 0:1, :].broadcast_to([P, NM, T]), ALU.mult))
                    dve.wait_ge(dA_ready, i * NS + (n + 1))
                    vec.tensor_tensor_scan(hs[:].rearrange("p m t -> p (m t)"),
                                           dA[:, n % 2].rearrange("p m t -> p (m t)"),
                                           dBx[:, n % 2].rearrange("p m t -> p (m t)"), 0.0, ALU.mult, ALU.add)\
                        .then_inc(scan_done, 1)
                    dve.wait_ge(scan_done, i * NS + (n + 1))
                    if n >= 2:
                        dve.wait_ge(summed, i * (NS - 1) + (n - 1))
                    give(vec.tensor_tensor(hC[:, n % 2], hs[:], bc[:, 1:2, :].broadcast_to([P, NM, T]), ALU.mult),
                         ("bc", n))
                given(("skip", 1))
                for g in range(2):
                    take(("ysum", g))
                    for m in (2 * g, 2 * g + 1):
                        last = vec.scalar_tensor_tensor(yT[:, m], xs[:, m], col("W_D", m),
                                                        bB(("ysum", g))[:, (m % 2) * T:(m % 2 + 1) * T],
                                                        ALU.mult, ALU.add)
                    give(last, ("ysum", g))
                    given(("ysum", g))
                vec.tensor_tensor(yT[:], yT[:], gate[:], ALU.mult).then_inc(yT_ready, 1)
                take("my")
                give(vec.tensor_tensor(rB[:].rearrange("p t d -> p (t d)"), bB("my"),
                                       x3d[:].rearrange("p t d -> p (t d)"), ALU.add), "my")
                given("my")
                layernorm(1, x4, x4_ready)
                for _, t, g in SROUND:
                    take(("S", t, g))
                    hs4 = slice(4 * g, 4 * g + 4)
                    s4 = bB(("S", t, g))[:, 0:4 * KEYS].rearrange("p (h j) -> p h j", j=KEYS)
                    link(vec.tensor_reduce(mx2[:, t, hs4], s4, AX.X, ALU.max))
                    give(vec.tensor_tensor(Pr2[:, t, hs4], s4, mx2[:, t, hs4].unsqueeze(2).broadcast_to([P, 4, KEYS]),
                                           ALU.subtract), ("S", t, g))
                for t in range(NT):
                    take(("o", t))
                    o = bB(("o", t))[:, 0:H1 * (DH1 + 1)].rearrange("p (h d) -> p h d", d=DH1 + 1)
                    link(vec.reciprocal(rd2[:, t], o[:, :, DH1]))
                    give(vec.tensor_tensor(o2[:, t], o[:, :, 0:DH1], rd2[:, t].unsqueeze(2).broadcast_to([P, H1, DH1]),
                                           ALU.mult), ("o", t))
                take("y3")
                dve.wait_ge(x4b_ready, i + 1)
                give(vec.tensor_tensor(rB[:].rearrange("p t d -> p (t d)"), bB("y3"),
                                       x4b[:].rearrange("p t d -> p (t d)"), ALU.add), "y3")
                given("y3")
                layernorm(2, x5, x5_ready)
                take("node")
                give(vec.tensor_tensor(sc[:].rearrange("p (t j) n -> p t (j n)", t=NT),
                                       bB("node")[:, 0:NT * 3 * NODES].rearrange("p (t n) -> p t n", t=NT),
                                       row("node_b").unsqueeze(1).broadcast_to([P, NT, 3 * NODES]), ALU.add), "node")
                given("node")
                link(vec.tensor_scalar(dec[:], sc[:], 0.0, None, ALU.is_ge))
                vec.tensor_copy(lv[0][:, :, 1], dec[:, :, 0])
                link(vec.tensor_scalar(lv[0][:, :, 0], dec[:, :, 0], -1.0, 1.0, ALU.mult, ALU.add))
                for n in range(1, 4):
                    w = 2 ** n
                    pair = lv[n][:].rearrange("p j (w c) -> p j w c", c=2)
                    link(vec.tensor_tensor(pair[:, :, :, 1], lv[n - 1][:], dec[:, :, w - 1:2 * w - 1], ALU.mult))
                    last = vec.tensor_tensor(pair[:, :, :, 0], lv[n - 1][:], pair[:, :, :, 1], ALU.subtract)
                    if n < 3:
                        link(last)
                last.then_inc(sel_ready, 1)
                dve.wait_ge(selT_ready, i + 1)
                give(vec.tensor_scalar(nsel[:], bB("selT")[0:48, 0:T], BIG, -BIG, ALU.mult, ALU.add), "selT")
                for j in range(3):
                    for g in (1, 3):
                        take(("hid", j, g))
                        for m in (2 * g, 2 * g + 1):
                            last = vec.tensor_scalar(hid[:, m], bB(("hid", j, g))[:, (m % 2) * T:(m % 2 + 1) * T],
                                                     col("f_b1", MF * j + m), 0.0, ALU.add, ALU.max)
                        give(last, ("hid", j, g))
                take("S3")
                link(vec.tensor_reduce(mx3[:], bB("S3").rearrange("p (t k) -> p t k", t=NT), AX.X, ALU.max))
                vec.tensor_scalar(nm3[:], mx3[:], -(D ** -0.5), None, ALU.mult).then_inc(mx3_ready, 1)
                given("S3")
                link(vec.reciprocal(rd3[:], den3[:]))
                take("y4")
                for t in range(NT):
                    last = vec.scalar_tensor_tensor(rB[:, t], bB("y4")[:, t * D:(t + 1) * D], rd3[:, t:t + 1], x5[:, t],
                                                    ALU.mult, ALU.add)
                give(last, "y4")
                given("y4")
                dve.wait_ge(out_stored, i * 16 + 16)
                layernorm(3, x6, x6_ready)
                assert c == LINKS_VEC_B, ("LINKS_VEC_B", c)

            with dve.Fori(0, NB) as i:
                dve_A(i)
                dve_B(i)

        @block.tensor
        def _(pe):
            mm, tp = nc.tensor.matmul, nc.tensor.transpose

            pe.wait_ge(kvw_loaded, 16 * len(kv_weights))
            pe.wait_ge(weights_loaded, 16 * N_WEIGHTS)
            for at, name in enumerate(SETUP):
                ps = (psA if at % 8 < 4 else psB)[:, at % 4, :]
                if at >= 8:
                    before = SETUP[at - 8]
                    if before in BY_ACT:
                        pe.wait_ge(setup_act, BY_ACT[before] + 1)
                    else:
                        pe.wait_ge(setup_dve, BY_DVE[before] + 1)
                kind = name[0]
                if kind in ("mk", "mv", "mq"):
                    _, c, f = name
                    d0, w, u = {"mk": (DnK, CH, 1), "mv": (DnV, CH, 2), "mq": (DnQ, P, 0)}[kind]
                    last = mm(ps[0:w], Dn[:, d0 + w * c:d0 + w * (c + 1)], Up[:, u, f * 512:(f + 1) * 512],
                              start=True, stop=True)
                elif kind == "mo":
                    for m in (2 * name[1], 2 * name[1] + 1):
                        last = mm(ps[:, (m % 2) * D:(m % 2 + 1) * D], Dn[:, DnO + m * P:DnO + (m + 1) * P], Ou[:],
                                  start=True, stop=True)
                elif kind == "k":
                    _, m, f = name
                    if m == f == 0:
                        pe.wait_ge(setup_dve, 4)
                    for c in range(2):
                        mm(ps[:, 0:480], Wk[:, c, m * P:(m + 1) * P], Ct[:, c, f * 480:(f + 1) * 480],
                           start=c == 0, stop=c == 1)
                    ipa = ps[:, 0:480].rearrange("p (b j) -> p b j", j=KEYS)[:, :, TEXT:KEYS]
                    for c in range(2):
                        last = mm(ipa, Wki[:, c, m * P:(m + 1) * P],
                                  Ci[:, c, f * 4 * IPA:(f + 1) * 4 * IPA].rearrange("p (b j) -> p b j", j=IPA),
                                  start=c == 0, stop=c == 1)
                elif kind == "v":
                    _, b, f = name
                    if b == f == 0:
                        pe.wait_ge(setup_dve, 8)
                    for c in range(2):
                        last = mm(ps[0:KEYS], Ct[:, c, b * KEYS:(b + 1) * KEYS], Wv[:, c, f * 512:(f + 1) * 512],
                                  start=c == 0, stop=c == 1)
                elif kind == "vi":
                    for c in range(2):
                        last = mm(ps[0:NB * IPA], Ci[:, c, :], Wvi[:, c, name[1] * 512:(name[1] + 1) * 512],
                                  start=c == 0, stop=c == 1)
                elif kind == "k2":
                    _, m, f = name
                    for c in range(2):
                        last = mm(ps[:, 0:480], Wk2[:, c, m * P:(m + 1) * P], Ct[:, c, f * 480:(f + 1) * 480],
                                  start=c == 0, stop=c == 1)
                else:
                    b = name[1]
                    for c in range(2):
                        last = mm(ps[0:KEYS, 0:D], Ct[:, c, b * KEYS:(b + 1) * KEYS], Wv2[:, c, :],
                                  start=c == 0, stop=c == 1)
                last.then_inc(setup_full, 1)
            pe.wait_ge(setup_act, len(BY_ACT))
            pe.wait_ge(setup_dve, len(BY_DVE))
            pe.wait_ge(setup_vec, 2)

            def pe_A(i):
                def room(name):
                    pe.wait_ge(free_A[RING_A.bank[name]], RING_A.turn(name, i))

                def taken(name):
                    pe.wait_ge(free_A[RING_A.bank[name]], RING_A.turn(name, i) + 1)

                def full(ins):
                    ins.then_inc(full_A, 1)

                def to_cols(name, rows_):
                    room(name)
                    for k in range(ND):
                        for t in range(NT):
                            last = tp(bA(name)[:, k * T + t * P:k * T + (t + 1) * P], rows_[:, t, k * P:(k + 1) * P],
                                      ident[:])
                    full(last)

                room("conv")
                pe.wait_ge(x_loaded, i * 16 + 16)
                mm(bA("conv")[:, 0:D], Toep[:, 0], xin[:, 0], start=True, stop=False)
                mm(bA("conv")[:, 0:D], Toep[:, 1], xin[:, 1], start=False, stop=True)
                full(mm(bA("conv")[:, D:2 * D], Toep[:, 0], xin[:, 1], start=True, stop=True))
                pe.wait_ge(x1_ready, i + 1)
                to_cols("x1T", x1)
                taken("x1T")
                for g in range(4):
                    room(("q", g))
                    for m in (2 * g, 2 * g + 1):
                        for k in range(ND):
                            last = mm(bA(("q", g))[:, (m % 2) * T:(m % 2 + 1) * T], Wq[:, k, m * P:(m + 1) * P],
                                      x1T[:, k], start=k == 0, stop=k == 1)
                    full(last)
                pe.wait_ge(kv_loaded, i * 16 * LOADS[0] + 16 * LOADS[0])
                for _, t, g in SROUND:
                    if t == 0:
                        taken(("q", g))
                    room(("S", t, g))
                    for m in (2 * g, 2 * g + 1):
                        last = mm(bA(("S", t, g))[:, (m % 2) * 2 * KEYS:(m % 2 + 1) * 2 * KEYS],
                                  qT[:, m, t * P:(t + 1) * P], Kbd[:, m], start=True, stop=True)
                    full(last)
                for _, t, g in TROUND:
                    if g == 0:
                        pe.wait_ge(probs_ready, i * NT + (t + 1))
                    room(("PT", t, g))
                    for h in range(4):
                        last = tp(bA(("PT", t, g))[0:KEYS, h * P:(h + 1) * P], Pr[:, t, 4 * g + h], ident[:])
                    full(last)
                for g in range(4):
                    taken(("PT", 1, g))
                    room(("O", g))
                    for h in range(4 * g, 4 * g + 4):
                        m = h // 2
                        last = mm(bA(("O", g))[64 * (h % 2):64 * (h % 2) + 64, (m % 2) * T:(m % 2 + 1) * T],
                                  V[:, h * DH0:(h + 1) * DH0], PT[:, h], start=True, stop=True)
                    full(last)
                taken(("O", 3))
                room("y1")
                for t in range(NT):
                    for m in range(M0):
                        last = mm(bA("y1")[:, t * D:(t + 1) * D], OT[:, m, t * P:(t + 1) * P], Wo[:, m],
                                  start=m == 0, stop=m == M0 - 1)
                full(last)
                pe.wait_ge(x2_ready, i + 1)
                to_cols("x2T", x2)
                taken("x2T")
                room("router")
                for t in range(NT):
                    for k in range(ND):
                        last = mm(bA("router")[:, t * EXPERTS:(t + 1) * EXPERTS], x2T[:, k, t * P:(t + 1) * P], Rw[:, k],
                                  start=k == 0, stop=k == 1)
                full(last)
                room("maskT")
                pe.wait_ge(mask_ready, i + 1)
                for t in range(NT):
                    last = tp(bA("maskT")[0:24, t * P:(t + 1) * P], m3[:, t].rearrange("p s e -> p (s e)"), ident[:])
                full(last)
                for g in range(4):
                    room(("h", g))
                    for e in (2 * g, 2 * g + 1):
                        for k in range(ND):
                            last = mm(bA(("h", g))[:, (e % 2) * T:(e % 2 + 1) * T], W1[:, k, e * EF:(e + 1) * EF],
                                      x2T[:, k], start=k == 0, stop=k == 1)
                    full(last)
                taken("maskT")
                for g in range(4):
                    room(("mb", g))
                    for e in (2 * g, 2 * g + 1):
                        last = mm(bA(("mb", g))[:, (e % 2) * T:(e % 2 + 1) * T], Sel24[:, e], mTb[:], start=True, stop=True)
                    full(last)
                taken(("mb", 3))
                room("y2")
                for t in range(NT):
                    for e in range(EXPERTS):
                        mm(bA("y2")[:, t * D:(t + 1) * D], hT[:, e, t * P:(t + 1) * P], W2[:, e],
                           start=e == 0, stop=False)
                    last = mm(bA("y2")[:, t * D:(t + 1) * D], mT[:, t * P:(t + 1) * P], B2[:], start=False, stop=True)
                full(last)

            def pe_B(i):
                def room(name):
                    pe.wait_ge(free_B[RING_B.bank[name]], RING_B.turn(name, i))

                def taken(name):
                    pe.wait_ge(free_B[RING_B.bank[name]], RING_B.turn(name, i) + 1)

                def full(ins):
                    ins.then_inc(full_B, 1)

                def to_cols(name, rows_):
                    room(name)
                    for k in range(ND):
                        for t in range(NT):
                            last = tp(bB(name)[:, k * T + t * P:k * T + (t + 1) * P], rows_[:, t, k * P:(k + 1) * P],
                                      ident[:])
                    full(last)

                pe.wait_ge(xr_ready, i + 1)
                to_cols("xrT", xr)
                taken("xrT")
                for s, W in (("u", Win), ("skip", Wsk)):
                    for g in range(2):
                        room((s, g))
                        for m in (2 * g, 2 * g + 1):
                            for k in range(ND):
                                last = mm(bB((s, g))[:, (m % 2) * T:(m % 2 + 1) * T], W[:, k, m * P:(m + 1) * P],
                                          xrT[:, k], start=k == 0, stop=k == 1)
                        full(last)
                room("dbc")
                for m in range(NM):
                    if m % 2 == 0:
                        pe.wait_ge(xs_ready, i * 2 + (m // 2 + 1))
                    last = mm(bB("dbc")[0:96, 0:T], Wdbc[:, m], xs[:, m], start=m == 0, stop=m == NM - 1)
                full(last)
                pe.wait_ge(dbc_ready, i + 1)
                for g in range(2):
                    room(("z", g))
                    for m in (2 * g, 2 * g + 1):
                        last = mm(bB(("z", g))[:, (m % 2) * T:(m % 2 + 1) * T], Wd2[:, m * P:(m + 1) * P], dbc[0:DTR],
                                  start=True, stop=True)
                    full(last)
                pe.wait_ge(bc3_ready, i + 1)

                def broadcast(n):
                    room(("bc", n))
                    mm(bB(("bc", n))[:, 0:T], Sel96[:, n], bc3[:], start=True, stop=True)
                    full(mm(bB(("bc", n))[:, T:2 * T], Sel96[:, NS + n], bc3[:], start=True, stop=True))

                broadcast(0)
                broadcast(1)
                room(("ysum", 0))
                room(("ysum", 1))
                for n in range(NS):
                    taken(("bc", n))
                    for g in range(2):
                        last = mm(bB(("ysum", g)), ident[:], hC[:, n % 2, 2 * g:2 * g + 2].rearrange("p m t -> p (m t)"),
                                  start=n == 0, stop=n == NS - 1, skip_group_check=True)
                        if n == NS - 1:
                            full(last)
                    if n < NS - 1:
                        last.then_inc(summed, 1)
                    if n + 2 < NS:
                        broadcast(n + 2)
                pe.wait_ge(yT_ready, i + 1)
                room("my")
                for t in range(NT):
                    for m in range(NM):
                        last = mm(bB("my")[:, t * D:(t + 1) * D], yT[:, m, t * P:(t + 1) * P], Wout[:, m],
                                  start=m == 0, stop=m == NM - 1)
                full(last)
                pe.wait_ge(x4_ready, i + 1)
                to_cols("x4T", x4)
                taken("x4T")
                room("q2")
                for m in range(ND):
                    for k in range(ND):
                        last = mm(bB("q2")[:, m * T:(m + 1) * T], Wq2[:, k, m * P:(m + 1) * P], x4T[:, k],
                                  start=k == 0, stop=k == 1)
                full(last)
                taken("q2")
                pe.wait_ge(kv2_loaded, i * 16 * LOADS[1] + 16 * LOADS[1])
                for _, t, g in SROUND:
                    room(("S", t, g))
                    full(mm(bB(("S", t, g))[:, 0:4 * KEYS], q2T[:, g // 2, t * P:(t + 1) * P],
                            Kbd2[:, g // 2, 4 * (g % 2):4 * (g % 2) + 4].rearrange("p h j -> p (h j)"),
                            start=True, stop=True))
                for _, t, g in TROUND:
                    if g == 0:
                        pe.wait_ge(exp2_done, i * NT + (t + 1))
                    room(("PT", t, g))
                    for h in range(4):
                        last = tp(bB(("PT", t, g))[0:KEYS, h * P:(h + 1) * P], Pr2[:, t, 4 * g + h], ident[:])
                    full(last)
                for t in range(NT):
                    taken(("PT", t, 3))
                    room(("o", t))
                    for h in range(H1):
                        last = mm(bB(("o", t))[:, h * (DH1 + 1):(h + 1) * (DH1 + 1)], PT2[:, h, t * P:(t + 1) * P],
                                  V2[:, h], start=True, stop=True)
                    full(last)
                taken(("o", 1))
                room("oT")
                for k in range(ND):
                    for t in range(NT):
                        last = tp(bB("oT")[:, k * T + t * P:k * T + (t + 1) * P],
                                  o2[:, t, 8 * k:8 * k + 8].rearrange("p h d -> p (h d)"), ident[:])
                full(last)
                taken("oT")
                room("y3")
                for t in range(NT):
                    for k in range(ND):
                        last = mm(bB("y3")[:, t * D:(t + 1) * D], o2T[:, k, t * P:(t + 1) * P], Wo2[:, k],
                                  start=k == 0, stop=k == 1)
                full(last)
                pe.wait_ge(x5_ready, i + 1)
                to_cols("x5T", x5)
                taken("x5T")
                room("node")
                for t in range(NT):
                    for k in range(ND):
                        last = mm(bB("node")[:, t * 3 * NODES:(t + 1) * 3 * NODES], x5T[:, k, t * P:(t + 1) * P],
                                  Nw[:, k], start=k == 0, stop=k == 1)
                full(last)
                room("selT")
                pe.wait_ge(sel_ready, i + 1)
                pe.sem_inc(alone_pe, 1)
                for t in range(NT):
                    last = tp(bB("selT")[0:48, t * P:(t + 1) * P],
                              lv[3][:, 3 * t:3 * t + 3].rearrange("p j l -> p (j l)"), ident[:])
                full(last)
                taken("selT")
                for j in range(3):
                    pe.wait_ge(fw1_loaded, i * 48 + 16 * (j + 1))
                    for g in range(4):
                        room(("hid", j, g))
                        for m in (2 * g, 2 * g + 1):
                            h = bB(("hid", j, g))[:, (m % 2) * T:(m % 2 + 1) * T]
                            for k in range(ND):
                                mm(h, FW1[:, k, m * P:(m + 1) * P], x5T[:, k], start=k == 0, stop=False)
                            last = mm(h, Sel48[:, j, m], nsel[:], start=False, stop=True)
                        full(last)
                    pe.wait_ge(fw2_loaded, i * 48 + 16 * (j + 1))
                    taken(("hid", j, 2))
                    taken(("hid", j, 3))
                    room(("out", j, 0))
                    for o in range(2):
                        dst = bB(("out", j, 0))[:, o * T:(o + 1) * T]
                        for m in range(MF):
                            if j < 2:
                                mm(dst, FW2[:, m, o * P:(o + 1) * P], hid[:, m], start=m == 0, stop=False)
                            else:
                                mm(dst, hid[:, m, o * P:(o + 1) * P], FW2[:, m], start=m == 0, stop=False)
                        if j < 2:
                            last = mm(dst, FB2[:, j, o * P:(o + 1) * P], selT[:], start=False, stop=True)
                        else:
                            last = mm(dst, selT[:, o * P:(o + 1) * P], FB2[:, j], start=False, stop=True)
                    full(last)
                taken(("out", 1, 0))
                room("S3")
                for t in range(NT):
                    for k in range(ND):
                        last = mm(bB("S3")[:, t * T:(t + 1) * T], qk3[:, 0, k, t * P:(t + 1) * P], qk3[:, 1, k],
                                  start=k == 0, stop=k == 1)
                full(last)
                taken("S3")
                room("P3T")
                for k in range(NT):
                    for t in range(NT):
                        last = tp(bB("P3T")[:, k * T + t * P:k * T + (t + 1) * P], P3[:, t, k * P:(k + 1) * P], ident[:])
                full(last)
                taken("P3T")
                taken(("out", 2, 0))
                room("y4")
                for t in range(NT):
                    for k in range(NT):
                        last = mm(bB("y4")[:, t * D:(t + 1) * D], P3T[:, k, t * P:(t + 1) * P], v3[:, k],
                                  start=k == 0, stop=k == 1)
                full(last)

            with pe.Fori(0, NB) as i:
                pe_A(i)
                pe_B(i)


def kernel(**inputs):
    import numpy as np
    import ml_dtypes
    import concourse.bacc as bacc
    from concourse.bass_utils import run_bass_kernel_spmd as run

    g = {k: np.asarray(v) for k, v in inputs.items()}
    f32 = np.float32

    padded = np.concatenate([np.zeros(P - 1, f32), g["L0_attn_filt"][:T]])
    k, t = np.arange(P)[:, None], np.arange(P)[None, :]
    toep = np.stack([padded[k - t + P - 1], padded[k - t + 2 * P - 1]])

    def vec(a):
        return np.asarray(a).reshape(-1, P).T

    cols = np.concatenate([
        vec(g["L0_ffn_b1"]),
        g["L1_attn_conv_w"].reshape(NM, P, KC).transpose(1, 0, 2).reshape(P, NM * KC),
        vec(g["L1_attn_conv_b"]), vec(g["L1_attn_wd2_b"]), vec(g["L1_attn_W_D"]),
        vec(g["L1_xattn_bq"]), vec(g["L1_xattn_bk"]),
        vec(g["L1_ffn_q_b1"]), vec(g["L1_ffn_k_b1"]), vec(g["L1_ffn_v_b1"]),
        vec(g["L1_attn_norm_w"]),
        g["L1_attn_A_log"].reshape(NM, P, NS).transpose(1, 0, 2).reshape(P, NM * NS),
        np.broadcast_to(np.concatenate([g[f"L0_xattn_{s}_alpha"] for s in "qkvo"])[None], (P, 4)),
    ], axis=1)
    rows = np.broadcast_to(np.concatenate([
        g["L0_xattn_bo"], g["L0_ffn_router_b"], g["L1_xattn_bv"], g["L1_xattn_bo"],
        g["L1_ffn_q_node_b"], g["L1_ffn_k_node_b"], g["L1_ffn_v_node_b"],
        np.arange(EXPERTS).astype(f32)])[None], (P, NROWS))

    ctxT = g["ctx_768"].transpose(2, 0, 1)
    sel24 = np.zeros((24, EXPERTS, P), f32)
    for e in range(EXPERTS):
        sel24[e::EXPERTS, e] = 1
    sel96 = np.zeros((96, 32, P), f32)
    for n in range(32):
        sel96[n::32, n] = 1
    sel48 = np.zeros((48, 3, MF, P), f32)
    for j in range(3):
        for m in range(MF):
            for a in range(2):
                sel48[LEAVES * j + 2 * m + a, j, m, LW * a:LW * (a + 1)] = 1
    fb2 = np.zeros((3, 48, D), f32)
    for j, s in enumerate("qkv"):
        fb2[j, LEAVES * j:LEAVES * (j + 1)] = g[f"L1_ffn_{s}_b2"]

    data = dict(
        x=g["x"], toep=toep, ctxT=ctxT.reshape(CTX, NB * KEYS), ctxiT=ctxT[:, :, TEXT:].reshape(CTX, NB * IPA),
        cols=cols, rows=rows, ident_in=np.eye(P, dtype=f32),
        sel24_in=sel24.astype(ml_dtypes.bfloat16), sel96_in=sel96.astype(ml_dtypes.bfloat16),
        sel48_in=sel48.astype(ml_dtypes.bfloat16),
        wq=g["L0_xattn_Wq"], wk=g["L0_xattn_Wk"], wv=g["L0_xattn_Wv"], wo=g["L0_xattn_Wo"],
        qdT=g["L0_xattn_q_down"].T, kdT=g["L0_xattn_k_down"].T, vdT=g["L0_xattn_v_down"].T, odT=g["L0_xattn_o_down"].T,
        qu=g["L0_xattn_q_up"], ku=g["L0_xattn_k_up"], vu=g["L0_xattn_v_up"], ou=g["L0_xattn_o_up"],
        wki=g["L0_xattn_Wk_ipa"], wvi=g["L0_xattn_Wv_ipa"],
        rw=g["L0_ffn_router_w"], w1=g["L0_ffn_W1"].transpose(1, 0, 2).reshape(D, EXPERTS * EF), w2=g["L0_ffn_W2"],
        b2=np.tile(g["L0_ffn_b2"], (3, 1)),
        win=g["L1_attn_in_w"].T, wsk=g["L1_attn_skip_w"].T,
        wdbc=np.concatenate([g["L1_attn_wd1"], g["L1_attn_wb"], g["L1_attn_wc"]]).T,
        wd2=g["L1_attn_wd2"].T, wout=g["L1_attn_out_w"].T,
        wq2=g["L1_xattn_Wq"], wk2=g["L1_xattn_Wk"], wv2=g["L1_xattn_Wv"], wo2=g["L1_xattn_Wo"],
        nw=np.concatenate([g[f"L1_ffn_{s}_node_w"] for s in "qkv"]).T,
        fw1=np.stack([g[f"L1_ffn_{s}_w1"].transpose(1, 0, 2).reshape(D, LEAVES * LW) for s in "qkv"]),
        fw2=np.stack([g[f"L1_ffn_{s}_w2"].reshape(LEAVES * LW, D) for s in "qkv"]),
        fb2=fb2,
    )
    nc = bacc.Bacc("TRN2", target_bir_lowering=False, num_devices=1)
    arrays, args = {}, {}
    for name, a in data.items():
        a = np.ascontiguousarray(a)
        arrays[f"in_{name}"] = a
        args[name] = nc.dram_tensor(f"in_{name}", a.shape, mybir.dt.from_np(a.dtype), kind="ExternalInput").ap()
    out = nc.dram_tensor("out_0_dram", (NB, T, D), mybir.dt.float32, kind="ExternalOutput").ap()
    decoder(nc, out=out, **args)
    r = run(nc, [arrays], core_ids=[0])
    return r.results[0]["out_0_dram"]
```

```python
import concourse.bass as bass
from concourse import mybir
from contextlib import ExitStack

NB, T, D = 8, 256, 256
P = 128
NT, ND = T // P, D // P
KEYS, IPA = 120, 4
TEXT = KEYS - IPA
CTX = 192
CH = CTX // 2
RANK = 32
H0, DH0 = 16, 64
M0 = H0 * DH0 // P
H1, DH1 = 16, 16
EXPERTS, EF = 8, 128
DI, NS, DTR, KC = 512, 16, 64, 4
NM = DI // P
LEAVES, LW, NODES = 16, 64, 15
MF = LEAVES * LW // P
EPS = 1e-5
BIG = float(2.0 ** 100)

COLS = {}
_at = 0
for _name, _n in (("moe_b1", EXPERTS), ("conv_w", NM * KC), ("conv_b", NM), ("wd2_b", NM), ("W_D", NM),
                  ("x_bq", ND), ("x_bk", ND), ("f_b1", 3 * MF), ("norm_w", ND), ("A_log", NM * NS),
                  ("alpha", 4)):
    COLS[_name] = (_at, _at + _n)
    _at += _n
NCOLS = _at
ROWS = {}
_at = 0
for _name, _n in (("x0_bo", D), ("router_b", EXPERTS), ("x1_bv", D), ("x1_bo", D), ("node_b", 3 * NODES),
                  ("iota", EXPERTS)):
    ROWS[_name] = (_at, _at + _n)
    _at += _n
NROWS = _at


class Ring:

    def __init__(self, fills):
        self.order = {name: n for n, (name, _) in enumerate(fills)}
        self.bank, self.use, self.uses = {}, {}, {}
        for name, bank in fills:
            self.bank[name] = bank
            self.use[name] = self.uses.get(bank, 0)
            self.uses[bank] = self.use[name] + 1

    def filled(self, name, i):
        return i * len(self.order) + (self.order[name] + 1)

    def turn(self, name, i):
        b = self.bank[name]
        return i * self.uses[b] + (self.use[name] + 1)


def numbered(names, banks=4):
    return [(name, n % banks) for n, name in enumerate(names)]


SROUND = [("S", t, g) for t in range(NT) for g in range(4)]
RING_A = Ring(numbered(
    ["conv", "x1T"] + [("q", g) for g in range(4)] + SROUND
    + [f for t in range(NT) for f in [("PT", t, g) for g in range(4)] + [("O", t, 0), ("O", t, 1)]]
    + ["y1", "x2T", "router"] + [("h", g) for g in range(4)] + ["maskT"] + [("mb", g) for g in range(4)] + ["y2"]))
RING_B = Ring(
    numbered(["xrT", ("u", 0), ("u", 1), "dbc", ("z", 0), ("z", 1)])
    + [(("bc", n), n % 2) for n in range(NS)] + [(("ysum", 0), 2), (("ysum", 1), 3)] + [(("skip", 0), 0), (("skip", 1), 1)]
    + numbered(["my", "x4T", "q2"] + SROUND + [f for t in range(NT) for f in [("PT", t, g) for g in range(4)] + [("o", t)]]
               + ["oT", "y3", "x5T", "node", "selT"]
               + [(s, j, g) for j in range(3) for s, n in (("hid", 4), ("out", 1)) for g in range(n)]
               + ["S3", "P3T", "y4"]))

def grid(s):
    return [f"{s}{t}{g}" for t in range(NT) for g in range(4)]


def four(s):
    return [f"{s}{g}" for g in range(4)]


SEGMENTS_A = (["conv", "x1", "x1T"] + four("q") + grid("S")[:5] + ["norm0"] + grid("S")[5:]
              + ["PT0", "norm1", "O0", "PT1", "O1", "y1", "x2", "x2T", "router", "h0", "gates", "h1", "h2", "h3", "maskT"]
              + four("mb") + ["y2", "x3"])
SEGMENTS_B = (["rms", "xr", "xrT", "u", "taps0", "taps1", "low rank", "delta", "dtx"] + [f"state{n}" for n in range(NS)]
              + ["skip", "ysum", "my", "x4", "x4T", "q2"] + grid("T")
              + ["QT0", "o0", "QT1", "o1", "oT", "y3", "x5", "x5T", "node", "tree", "selT"]
              + [s for j in range(3) for s in four(f"net{j}") + [f"out{j}"]] + ["S3", "P3", "y4", "x6"])
PAIRS = [("q3", "dtx"), ("O1", "state15"), ("gates", "o1"), ("x3", "x6")]


def schedule():
    order, a, b = [], 0, 0
    for stop_a, stop_b in PAIRS:
        na, nb = SEGMENTS_A.index(stop_a) + 1 - a, SEGMENTS_B.index(stop_b) + 1 - b
        for n in range(na + nb):
            if (n + 1) * na // (na + nb) > n * na // (na + nb):
                order.append(SEGMENTS_A[a])
                a += 1
            else:
                order.append(SEGMENTS_B[b])
                b += 1
    assert (a, b) == (len(SEGMENTS_A), len(SEGMENTS_B))
    return order


def write_out(order, *halves):
    coming = [next(half, None) for half in halves]
    for segment in order:
        for n, half in enumerate(halves):
            while coming[n] == segment:
                coming[n] = next(half, None)
    assert not any(coming), coming


MERGES = [("mk", c, f) for c in range(2) for f in range(2)] + [("mv", c, f) for c in range(2) for f in range(2)]
KV = ([("k", m, f) for m in range(M0) for f in range(2)] + [("v", b, f) for b in range(NB) for f in range(2)]
      + [("vi", f) for f in range(2)] + [("k2", m, f) for m in range(ND) for f in range(2)])
SETUP = (MERGES + KV + [("v2", b) for b in range(NB)] + [("mq", k, f) for k in range(ND) for f in range(2)]
         + [("mo", g) for g in range(4)])
BY_ACT = {name: n for n, name in enumerate(KV)}
BY_DVE = {name: n for n, name in enumerate([x for x in SETUP if x not in BY_ACT])}
STAGED = KV + [("v2", b) for b in range(NB)]
SLOT = {name: n for n, name in enumerate(STAGED)}
SLOTS = 4

LINKS_VEC_A, LINKS_VEC_B, LINKS_ACT_B = 26, 49, 2
LOADS = (3, 9)


def decoder(nc, x, toep, ctxT, ctxiT, cols, rows, ident_in, sel24_in, sel96_in, sel48_in,
            wq, wk, wv, wo, qdT, kdT, vdT, odT, qu, ku, vu, ou, wki, wvi,
            rw, w1, w2, b2, win, wsk, wdbc, wd2, wout, wq2, wk2, wv2, wo2, nw, fw1, fw2, fb2, out):
    fp32, bf16, u32 = mybir.dt.float32, mybir.dt.bfloat16, mybir.dt.uint32
    ALU, ACT, AX = mybir.AluOpType, mybir.ActivationFunctionType, mybir.AxisListType

    k0_all = nc.dram_tensor("k0_all", (NB, M0 * P, KEYS), fp32).ap()
    v0_all = nc.dram_tensor("v0_all", (NB, KEYS, H0 * DH0), fp32).ap()
    k2_all = nc.dram_tensor("k2_all", (NB, D, KEYS), fp32).ap()
    v2_all = nc.dram_tensor("v2_all", (NB, KEYS, H1 * (DH1 + 1)), fp32).ap()

    ctx = ExitStack()
    with ctx:
        def sb(name, shape, dt=fp32, stack=ctx):
            return stack.enter_context(nc.sbuf_tensor(name, shape, dt))

        def sem(name):
            return ctx.enter_context(nc.semaphore(name))

        Wq = sb("Wq", [P, ND, 1024]); Wo = sb("Wo", [P, M0, D])
        W1 = sb("W1", [P, ND, 1024]); W2 = sb("W2", [P, EXPERTS, D]); B2 = sb("B2", [24, D])
        Rw = sb("Rw", [P, ND, EXPERTS])
        Win = sb("Win", [P, ND, DI]); Wsk = sb("Wsk", [P, ND, DI]); Wdbc = sb("Wdbc", [P, NM, 96])
        Wd2 = sb("Wd2", [DTR, DI]); Wout = sb("Wout", [P, NM, D])
        Wq2 = sb("Wq2", [P, ND, D]); Wo2 = sb("Wo2", [P, ND, D])
        Nw = sb("Nw", [P, ND, 3 * NODES])
        FW1 = sb("FW1", [P, ND, 1024]); FW2 = sb("FW2", [P, MF, D])
        FB2 = sb("FB2", [48, 3, D])
        Toep = sb("Toep", [P, 2, P]); ident = sb("ident", [P, P])
        Sel24 = sb("Sel24", [24, EXPERTS], bf16); Sel96 = sb("Sel96", [96, 32], bf16)
        Sel48 = sb("Sel48", [48, 3, MF, P], bf16)
        Cols = sb("Cols", [P, NCOLS]); Rows = sb("Rows", [P, NROWS])
        Aneg = sb("Aneg", [P, NM, NS]); half = sb("half", [P, 4]); lora = sb("lora", [P, 4])
        xin = sb("xin", [P, NT, D])

        def col(name, n):
            a = COLS[name][0] + n
            return Cols[:, a:a + 1]

        def row(name):
            return Rows[:, ROWS[name][0]:ROWS[name][1]]

        psA = ctx.enter_context(nc.psum_tensor("psA", [P, 4, 512], fp32))
        psB = ctx.enter_context(nc.psum_tensor("psB", [P, 4, 512], fp32))

        with ExitStack() as st:
            Wk = sb("Wk", [CH, 2, 1024], stack=st); Wv = sb("Wv", [CH, 2, 1024], stack=st)
            Wki = sb("Wki", [CH, 2, 1024], stack=st); Wvi = sb("Wvi", [CH, 2, 1024], stack=st)
            Wk2 = sb("Wk2", [CH, 2, D], stack=st); Wv2 = sb("Wv2", [CH, 2, D], stack=st)
            Ct = sb("Ct", [CH, 2, NB * KEYS], stack=st); Ci = sb("Ci", [CH, 2, NB * IPA], stack=st)
            Up = sb("Up", [RANK, 3, 1024], stack=st); Ou = sb("Ou", [RANK, D], stack=st)
            Dn = sb("Dn", [RANK, 1024 + D + 2 * CTX], stack=st)
            Stage = sb("Stage", [P, SLOTS, 512], stack=st)
            V2s = sb("V2s", [KEYS, 2, H1, DH1 + 1], stack=st)
        DnO, DnQ, DnK, DnV = 0, 1024, 1024 + D, 1024 + D + CTX

        x3 = sb("x3", [P, NT, D])
        Kbd = sb("Kbd", [P, M0, 2 * KEYS]); V = sb("V", [KEYS, 1024])
        Kbd2 = sb("Kbd2", [P, ND, 8, KEYS]); V2 = sb("V2", [KEYS, H1, DH1 + 1])
        Uin = sb("Uin", [P, NM, KC - 1 + T])
        dA = sb("dA", [P, 2, NM, T])
        x6 = sb("x6", [P, NT, D])
        st = ctx
        if True:
            r = sb("r", [P, NT, D], stack=st)
            x1 = sb("x1", [P, NT, D], stack=st); x1b = sb("x1b", [P, NT, D], stack=st)
            x1T = sb("x1T", [P, ND, T], stack=st)
            qT = sb("qT", [P, M0, T], stack=st)
            Pr = sb("Pr", [P, NT, H0, KEYS], stack=st)
            PT = sb("PT", [KEYS, H0, P], stack=st)
            mx = sb("mx", [P, NT, 2, H0], stack=st); den = sb("den", [P, NT, 2, H0], stack=st)
            rden = sb("rden", [P, NT, 2, H0], stack=st)
            bn = sb("bn", [P, NT, 6], stack=st); mv = sb("mv", [P, NT, 2], stack=st)
            var = sb("var", [P, NT], stack=st); rstd = sb("rstd", [P, NT], stack=st)
            lg = sb("lg", [P, NT, EXPERTS], stack=st); lx = sb("lx", [P, NT], stack=st)
            pe_ = sb("pe_", [P, NT, EXPERTS], stack=st); top = sb("top", [P, NT, 8], stack=st)
            tix = sb("tix", [P, NT, 8], u32, stack=st); tif = sb("tif", [P, NT, 2], stack=st)
            tw = sb("tw", [P, NT, 2], stack=st); ts = sb("ts", [P, NT], stack=st); tr = sb("tr", [P, NT], stack=st)
            mk = sb("mk", [P, NT, 2, EXPERTS], stack=st); mask = sb("mask", [P, NT, EXPERTS], stack=st)
            mhi = sb("mhi", [P, NT, 2, EXPERTS], bf16, stack=st); mr = sb("mr", [P, NT, EXPERTS], stack=st)
            m3 = sb("m3", [P, NT, 3, EXPERTS], stack=st)
            mT = sb("mT", [24, T], stack=st); mTb = sb("mTb", [24, T], bf16, stack=st)
            x2 = x1b
            x2T = x1T
            OT = qT
            hT = Pr[:].rearrange("p t h j -> p (t h j)")[:, 0:EXPERTS * T].rearrange("p (e t) -> p e t", t=T)
        if True:
            rB = sb("rB", [P, NT, D], stack=st)
            x3d = sb("x3d", [P, NT, D], stack=st); xr = sb("xr", [P, NT, D], stack=st)
            sq = xr
            xrT = sb("xrT", [P, ND, T], stack=st)
            bnB = sb("bnB", [P, NT, 6], stack=st); mvB = sb("mvB", [P, NT, 2], stack=st)
            varB = sb("varB", [P, NT], stack=st); rstdB = sb("rstdB", [P, NT], stack=st)
            ssq = sb("ssq", [P, NT], stack=st)
            x4 = sb("x4", [P, NT, D], stack=st); x4b = sb("x4b", [P, NT, D], stack=st)
            x4T = xrT
            with ExitStack() as mm:
                xs = sb("xs", [P, NM, T], stack=mm)
                dbc = sb("dbc", [96, T], stack=mm); bcr = sb("bcr", [64, T], stack=mm)
                bc3 = sb("bc3", [96, T], bf16, stack=mm)
                dt_ = sb("dt_", [P, NM, T], stack=mm); dtx = sb("dtx", [P, NM, T], stack=mm)
                dBx = sb("dBx", [P, NM, T], stack=mm); hs = sb("hs", [P, NM, T], stack=mm)
                hC = sb("hC", [P, 2, NM, T], stack=mm)
                gate = dt_
                sp = hs
                yT = dBx
            with ExitStack() as mm:
                q2T = sb("q2T", [P, ND, T], stack=mm)
                Pr2 = sb("Pr2", [P, NT, H1, KEYS], stack=mm); PT2 = sb("PT2", [KEYS, H1, P], stack=mm)
                mx2 = sb("mx2", [P, NT, H1], stack=mm); rd2 = sb("rd2", [P, NT, H1], stack=mm)
                o2 = sb("o2", [P, NT, H1, DH1], stack=mm); o2T = sb("o2T", [P, ND, T], stack=mm)
            x5 = x3d; x5T = xrT
            with ExitStack() as mm:
                sc = sb("sc", [P, NT * 3, NODES], stack=mm); dec = sb("dec", [P, NT * 3, NODES], stack=mm)
                lv = [sb(f"lv{n}", [P, NT * 3, 2 ** (n + 1)], stack=mm) for n in range(4)]
                selT = sb("selT", [48, T], stack=mm); nsel = sb("nsel", [48, T], bf16, stack=mm)
                hid = sb("hid", [P, MF, T], stack=mm)
                qk3 = sb("qk3", [P, 2, ND, T], stack=mm); v3 = sb("v3", [P, NT, D], stack=mm)
                P3 = sb("P3", [P, NT, T], stack=mm); P3T = sb("P3T", [P, NT, T], stack=mm)
                mx3 = sb("mx3", [P, NT], stack=mm); nm3 = sb("nm3", [P, NT], stack=mm)
                den3 = sb("den3", [P, NT], stack=mm); rd3 = sb("rd3", [P, NT], stack=mm)

        weights_loaded = sem("weights_loaded"); kvw_loaded = sem("kvw_loaded")
        setup_full = sem("setup_full"); setup_act = sem("setup_act"); setup_dve = sem("setup_dve")
        setup_pool = sem("setup_pool"); setup_init = sem("setup_init")
        slot_stored = [sem(f"slot_stored{s}") for s in range(SLOTS)]
        v2_stored = [sem(f"v2_stored{s}") for s in range(2)]
        x_loaded = sem("x_loaded"); kv_loaded = sem("kv_loaded"); kv2_loaded = sem("kv2_loaded")
        out_stored = sem("out_stored")
        full_A = sem("full_A"); full_B = sem("full_B")
        free_A = [sem(f"free_A{b}") for b in range(4)]
        free_B = [sem(f"free_B{b}") for b in range(4)]
        links_vec_A = sem("links_vec_A"); links_vec_B = sem("links_vec_B"); links_act_B = sem("links_act_B")
        setup_vec = sem("setup_vec"); a_exp = sem("a_exp")
        fw1_loaded = sem("fw1_loaded"); fw2_loaded = sem("fw2_loaded")
        var_A = sem("var_A"); rstd_A = sem("rstd_A"); var_B = sem("var_B"); rstd_B = sem("rstd_B")
        x1_ready = sem("x1_ready"); x1b_ready = sem("x1b_ready")
        exp_done = sem("exp_done"); den_ready = sem("den_ready"); probs_ready = sem("probs_ready")
        x2_ready = sem("x2_ready"); logits_ready = sem("logits_ready"); gates_exp = sem("gates_exp")
        mask_ready = sem("mask_ready"); x3_ready = sem("x3_ready")
        sq_done = sem("sq_done"); xr_ready = sem("xr_ready"); conv_ready = sem("conv_ready")
        xs_ready = sem("xs_ready"); dbc_ready = sem("dbc_ready"); bc_hi = sem("bc_hi"); bc3_ready = sem("bc3_ready")
        dt_act = sem("dt_act"); dt_ready = sem("dt_ready"); dA_ready = sem("dA_ready")
        scan_done = sem("scan_done"); summed = sem("summed"); yT_ready = sem("yT_ready")
        x4_ready = sem("x4_ready"); x4b_ready = sem("x4b_ready"); exp2_done = sem("exp2_done")
        alone_vec = sem("alone_vec"); alone_pe = sem("alone_pe")
        x5_ready = sem("x5_ready"); sel_ready = sem("sel_ready"); selT_ready = sem("selT_ready")
        mx3_ready = sem("mx3_ready"); x6_ready = sem("x6_ready")

        def bA(name):
            return psA[:, RING_A.bank[name], :]

        def bB(name):
            return psB[:, RING_B.bank[name], :]

        weights = [
            (Rows[:], rows), (Cols[:], cols), (ident[:], ident_in),
            (Toep[:], toep.rearrange("k p t -> p k t")),
            (Wq[:], wq.rearrange("(k p) n -> p k n", p=P)), (Wo[:], wo.rearrange("(m p) n -> p m n", p=P)),
            (W1[:], w1.rearrange("(k p) n -> p k n", p=P)), (W2[:], w2.rearrange("e f n -> f e n")),
            (B2[:], b2), (Rw[:], rw.rearrange("(k p) n -> p k n", p=P)),
            (Win[:], win.rearrange("(k p) n -> p k n", p=P)), (Wsk[:], wsk.rearrange("(k p) n -> p k n", p=P)),
            (Wdbc[:], wdbc.rearrange("(k p) n -> p k n", p=P)), (Wd2[:], wd2),
            (Wout[:], wout.rearrange("(k p) n -> p k n", p=P)),
            (Wq2[:], wq2.rearrange("(k p) n -> p k n", p=P)), (Wo2[:], wo2.rearrange("(k p) n -> p k n", p=P)),
            (Nw[:], nw.rearrange("(k p) n -> p k n", p=P)),
            (FB2[:], fb2.rearrange("j r n -> r j n")),
            (Sel24[:], sel24_in), (Sel96[:], sel96_in), (Sel48[:], sel48_in),
            (Dn[:, DnO:DnQ], odT), (Dn[:, DnQ:DnK], qdT), (Up[:, 0], qu), (Ou[:], ou),
        ]
        N_WEIGHTS = len(weights)
        kv_weights = [
            (Dn[:, DnK:DnV], kdT), (Dn[:, DnV:DnV + CTX], vdT), (Up[:, 1], ku), (Up[:, 2], vu),
            (Wk[:], wk.rearrange("(c p) n -> p c n", p=CH)), (Wv[:], wv.rearrange("(c p) n -> p c n", p=CH)),
            (Ct[:], ctxT.rearrange("(c p) n -> p c n", p=CH)), (Ci[:], ctxiT.rearrange("(c p) n -> p c n", p=CH)),
            (Wki[:], wki.rearrange("(c p) n -> p c n", p=CH)), (Wvi[:], wvi.rearrange("(c p) n -> p c n", p=CH)),
            (Wk2[:], wk2.rearrange("(c p) n -> p c n", p=CH)), (Wv2[:], wv2.rearrange("(c p) n -> p c n", p=CH)),
        ]

        block = ctx.enter_context(nc.Block())

        def stored_by(n, s):
            return sum(16 * (NB if name[0] == "vi" else 1) for name in STAGED[:n]
                       if name[0] != "v2" and SLOT[name] % SLOTS == s)

        @block.sync
        def _(sp):
            def load_x(b):
                src = x[bass.ts(b, 1)] if not isinstance(b, int) else x[b:b + 1]
                sp.dma_start(xin[:], src.rearrange("o (t p) d -> p (o t) d", p=P)).then_inc(x_loaded, 16)

            def load_kv(b):
                k = k0_all[bass.ts(b, 1)] if not isinstance(b, int) else k0_all[b:b + 1]
                v = v0_all[bass.ts(b, 1)] if not isinstance(b, int) else v0_all[b:b + 1]
                for e in range(2):
                    sp.dma_start(Kbd[64 * e:64 * e + 64, :, e * KEYS:(e + 1) * KEYS],
                                 k.rearrange("o (m e p) j -> e p (o m) j", e=2, p=64)[e]).then_inc(kv_loaded, 16)
                sp.dma_start(V[:], v.rearrange("o j n -> j (o n)")).then_inc(kv_loaded, 16)

            def load_kv2(b):
                k = k2_all[bass.ts(b, 1)] if not isinstance(b, int) else k2_all[b:b + 1]
                v = v2_all[bass.ts(b, 1)] if not isinstance(b, int) else v2_all[b:b + 1]
                kk = k.rearrange("o (m h p) j -> h p (o m) j", h=8, p=DH1)
                for h in range(8):
                    sp.dma_start(Kbd2[DH1 * h:DH1 * (h + 1), :, h, :], kk[h]).then_inc(kv2_loaded, 16)
                sp.dma_start(V2[:].rearrange("j h d -> j (h d)"), v.rearrange("o j n -> j (o n)")).then_inc(kv2_loaded, 16)

            def load_fw1(j):
                sp.dma_start(FW1[:], fw1[j].rearrange("(k p) n -> p k n", p=P)).then_inc(fw1_loaded, 16)

            def load_fw2(j):
                sp.dma_start(FW2[:], fw2[j].rearrange("(m p) n -> p m n", p=P)).then_inc(fw2_loaded, 16)

            def store(b):
                dst = out[bass.ts(b, 1)] if not isinstance(b, int) else out[b:b + 1]
                sp.dma_start(dst.rearrange("o (t p) d -> p (o t) d", p=P), x6[:]).then_inc(out_stored, 16)

            for dst, src in kv_weights:
                sp.dma_start(dst, src).then_inc(kvw_loaded, 16)
            for dst, src in weights:
                sp.dma_start(dst, src).then_inc(weights_loaded, 16)
            load_x(0)
            load_fw1(0)
            load_fw2(0)
            for name in STAGED:
                s = SLOT[name] % SLOTS
                if name[0] == "v2":
                    b = name[1]
                    sp.wait_ge(setup_dve, BY_DVE[name] + 1)
                    sp.dma_start(v2_all[b], V2s[:, b % 2].rearrange("j h d -> j (h d)")).then_inc(v2_stored[b % 2], 16)
                    continue
                sp.wait_ge(setup_act, BY_ACT[name] + 1)
                if name[0] == "k":
                    _, m, f = name
                    sp.dma_start(k0_all[4 * f:4 * f + 4, m * P:(m + 1) * P, :].rearrange("b p j -> p b j"),
                                 Stage[:, s, 0:4 * KEYS].rearrange("p (b j) -> p b j", j=KEYS)).then_inc(slot_stored[s], 16)
                elif name[0] == "v":
                    _, b, f = name
                    sp.dma_start(v0_all[b, 0:TEXT, f * 512:(f + 1) * 512], Stage[0:TEXT, s, :]).then_inc(slot_stored[s], 16)
                elif name[0] == "vi":
                    f = name[1]
                    for b in range(NB):
                        sp.dma_start(v0_all[b, TEXT:KEYS, f * 512:(f + 1) * 512],
                                     Stage[IPA * b:IPA * (b + 1), s, :]).then_inc(slot_stored[s], 16)
                else:
                    _, m, f = name
                    sp.dma_start(k2_all[4 * f:4 * f + 4, m * P:(m + 1) * P, :].rearrange("b p j -> p b j"),
                                 Stage[:, s, 0:4 * KEYS].rearrange("p (b j) -> p b j", j=KEYS)).then_inc(slot_stored[s], 16)
            for s in range(SLOTS):
                sp.wait_ge(slot_stored[s], stored_by(len(SLOT), s))
            for s in range(2):
                sp.wait_ge(v2_stored[s], 16 * NB // 2)
            sp.wait_ge(setup_init, 1)
            load_kv(0)
            load_kv2(0)
            def nets(hid_taken, out_taken, again):
                for j in range(3):
                    if j < 2 or again:
                        sp.wait_ge(free_B[RING_B.bank["hid", j, 3]], hid_taken[j])
                        load_fw1((j + 1) % 3)
                        sp.wait_ge(free_B[RING_B.bank["out", j, 0]], out_taken[j])
                        load_fw2((j + 1) % 3)

            def around(a, b, fixed):
                value = (lambda v: v) if fixed else sp.snap
                nxt_a, nxt_b, x1_there, done = value(a + 1), value(b + 1), value(a + 1), value(b + 2)
                o_taken = value(RING_A.turn(("O", 1, 1), a) + 1)
                o2_taken = value(RING_B.turn(("o", 1), b) + 1)
                hid_taken = [value(RING_B.turn(("hid", j, 3), b) + 1) for j in range(3)]
                out_taken = [value(RING_B.turn(("out", j, 0), b) + 1) for j in range(3)]
                if not fixed or a < NB - 1:
                    sp.wait_ge(x1_ready, x1_there)
                    load_x(nxt_a)
                    sp.wait_ge(free_A[RING_A.bank["O", 1, 1]], o_taken)
                    load_kv(nxt_a)
                if b is not None and (not fixed or 0 <= b):
                    if not fixed or b < NB - 1:
                        sp.wait_ge(free_B[RING_B.bank["o", 1]], o2_taken)
                        load_kv2(nxt_b)
                    nets(hid_taken, out_taken, not fixed or b < NB - 1)
                    sp.wait_ge(x6_ready, done)
                    store(b)

            around(0, -1, True)
            with sp.Fori(0, NB - 2) as i:
                around(i + 1, i, False)
            around(NB - 1, NB - 2, True)
            around(NB, NB - 1, True)
            sp.wait_ge(out_stored, 16 * NB + 16)

        @block.gpsimd
        def _(po):
            for s in free_A + free_B:
                po.sem_inc(s, 1)
            po.sem_inc(out_stored, 16)
            po.sem_inc(x6_ready, 1)
            po.sem_inc(x3_ready, 1)
            nc.gpsimd.memset(half[:], -0.5).then_inc(setup_pool, 1)
            po.wait_ge(setup_pool, 1)
            nc.gpsimd.memset(V2s[:], 1.0).then_inc(setup_pool, 1)
            for s in range(2):
                po.wait_ge(v2_stored[s], 16 * NB // 2)
            for s in range(SLOTS):
                po.wait_ge(slot_stored[s], stored_by(len(SLOT), s))
            po.wait_ge(setup_dve, len(BY_DVE))
            nc.gpsimd.memset(Kbd[:], 0.0)
            nc.gpsimd.memset(Kbd2[:], 0.0)
            nc.gpsimd.memset(dA[:], 0.0)
            nc.gpsimd.memset(Uin[:], 0.0).then_inc(setup_init, 1)
            po.wait_ge(setup_init, 1)

            def rsqrt_A(n, i):
                po.wait_ge(var_A, i * 3 + (n + 1))
                nc.gpsimd.tensor_tensor(rstd[:], var[:], half[:, 0:NT], ALU.pow).then_inc(rstd_A, 1)

            def rsqrt_B(n, i):
                po.wait_ge(var_B, i * 4 + (n + 1))
                nc.gpsimd.tensor_tensor(rstdB[:], varB[:], half[:, 0:NT], ALU.pow).then_inc(rstd_B, 1)

            def pool_A(i):
                yield "conv"
                rsqrt_A(0, i)
                yield "x1"
                po.wait_ge(x1_ready, i + 1)
                nc.gpsimd.tensor_tensor(x1b[:], x1[:], row("x0_bo").unsqueeze(1).broadcast_to([P, NT, D]), ALU.add)\
                    .then_inc(x1b_ready, 1)
                for t in range(NT):
                    yield f"norm{t}"
                    po.wait_ge(den_ready, i * NT + (t + 1))
                    nc.gpsimd.tensor_tensor(Pr[:, t, :, 0:TEXT], Pr[:, t, :, 0:TEXT],
                                            rden[:, t, 0, :].unsqueeze(2).broadcast_to([P, H0, TEXT]), ALU.mult)
                    nc.gpsimd.tensor_tensor(Pr[:, t, :, TEXT:KEYS], Pr[:, t, :, TEXT:KEYS],
                                            rden[:, t, 1, :].unsqueeze(2).broadcast_to([P, H0, IPA]), ALU.mult)\
                        .then_inc(probs_ready, 1)
                yield "y1"
                rsqrt_A(1, i)
                yield "y2"
                rsqrt_A(2, i)

            def pool_B(i):
                yield "rms"
                rsqrt_B(0, i)
                yield "my"
                rsqrt_B(1, i)
                yield "x4"
                po.wait_ge(x4_ready, i + 1)
                nc.gpsimd.tensor_tensor(x4b[:], x4[:], row("x1_bo").unsqueeze(1).broadcast_to([P, NT, D]), ALU.add)\
                    .then_inc(x4b_ready, 1)
                yield "y3"
                rsqrt_B(2, i)
                yield "y4"
                rsqrt_B(3, i)

            po.wait_ge(weights_loaded, 16 * N_WEIGHTS)
            write_out(SEGMENTS_A, pool_A(0))
            with po.Fori(0, NB - 1) as i:
                write_out(schedule(), pool_A(i + 1), pool_B(i))
            write_out(SEGMENTS_B, pool_B(NB - 1))

        @block.scalar
        def _(act):
            act.wait_ge(weights_loaded, 16 * N_WEIGHTS)
            a0, a1 = COLS["A_log"]
            nc.scalar.activation(Aneg[:], Cols[:, a0:a1].rearrange("p (m n) -> p m n", n=NS), ACT.Exp)\
                .then_inc(a_exp, 1)
            for name in KV:
                n = BY_ACT[name]
                s = SLOT[name] % SLOTS
                bank = SETUP.index(name) % 8
                ps = (psA if bank < 4 else psB)[:, bank % 4, :]
                act.wait_ge(setup_full, SETUP.index(name) + 1)
                if SLOT[name] >= SLOTS:
                    act.wait_ge(slot_stored[s], stored_by(SLOT[name], s))
                if name[0] == "k":
                    nc.scalar.activation(Stage[:, s, 0:480], ps[:, 0:480], ACT.Copy).then_inc(setup_act, 1)
                elif name[0] == "v":
                    nc.scalar.activation(Stage[0:KEYS, s, :], ps[0:KEYS, :], ACT.Copy).then_inc(setup_act, 1)
                elif name[0] == "vi":
                    nc.scalar.activation(Stage[0:NB * IPA, s, :], ps[0:NB * IPA, :], ACT.Copy).then_inc(setup_act, 1)
                else:
                    nc.scalar.activation(Stage[:, s, 0:480], ps[:, 0:480], ACT.Identity,
                                         bias=col("x_bk", name[1])).then_inc(setup_act, 1)
            act.wait_ge(setup_init, 1)
            act.wait_ge(setup_vec, 1)

            def take_A(name, i):
                act.wait_ge(full_A, RING_A.filled(name, i))

            def take_B(name, i):
                act.wait_ge(full_B, RING_B.filled(name, i))

            def act_A(i):
                yield "x1T"
                take_A("x1T", i)
                nc.scalar.activation(x1T[:].rearrange("p k t -> p (k t)"), bA("x1T"), ACT.Copy)\
                    .then_inc(free_A[RING_A.bank["x1T"]], 1)
                for g in range(4):
                    yield f"q{g}"
                    take_A(("q", g), i)
                    nc.scalar.activation(qT[:, 2 * g:2 * g + 2, :].rearrange("p m t -> p (m t)"), bA(("q", g)), ACT.Copy)\
                        .then_inc(free_A[RING_A.bank["q", g]], 1)
                for t in range(NT):
                    yield f"S{t}3"
                    act.wait_ge(free_A[RING_A.bank["S", t, 3]], RING_A.turn(("S", t, 3), i) + 1)
                    nc.scalar.activation(Pr[:, t].rearrange("p h j -> p (h j)"), Pr[:, t].rearrange("p h j -> p (h j)"),
                                         ACT.Exp, scale=DH0 ** -0.5).then_inc(exp_done, 1)
                for t in range(NT):
                    yield f"PT{t}"
                    for g in range(4):
                        take_A(("PT", t, g), i)
                        nc.scalar.activation(PT[:, 4 * g:4 * g + 4],
                                             bA(("PT", t, g))[0:KEYS].rearrange("j (h t) -> j h t", t=P), ACT.Copy)\
                            .then_inc(free_A[RING_A.bank["PT", t, g]], 1)
                    yield f"O{t}"
                    for f in range(2):
                        take_A(("O", t, f), i)
                        nc.scalar.activation(OT[:, 4 * f:4 * f + 4, t * P:(t + 1) * P],
                                             bA(("O", t, f)).rearrange("p (m t) -> p m t", t=P), ACT.Copy)\
                            .then_inc(free_A[RING_A.bank["O", t, f]], 1)
                yield "x2T"
                take_A("x2T", i)
                nc.scalar.activation(x2T[:].rearrange("p k t -> p (k t)"), bA("x2T"), ACT.Copy)\
                    .then_inc(free_A[RING_A.bank["x2T"]], 1)
                for g in range(4):
                    if g == 1:
                        yield "gates"
                        act.wait_ge(logits_ready, i + 1)
                        nc.scalar.activation(pe_[:], lg[:], ACT.Exp).then_inc(gates_exp, 1)
                    yield f"h{g}"
                    take_A(("h", g), i)
                    for e in (2 * g, 2 * g + 1):
                        last = nc.scalar.activation(hT[:, e, :], bA(("h", g))[:, (e % 2) * T:(e % 2 + 1) * T],
                                                    ACT.Gelu, bias=col("moe_b1", e))
                    last.then_inc(free_A[RING_A.bank["h", g]], 1)

            def act_B(i):
                c = 0

                def link(ins):
                    nonlocal c
                    c += 1
                    ins.then_inc(links_act_B, 1)
                    act.wait_ge(links_act_B, i * LINKS_ACT_B + c)

                yield "rms"
                act.wait_ge(x3_ready, i + 2)
                nc.scalar.activation(sq[:, 0], x3[:, 0], ACT.Square, accum_out=ssq[:, 0:1])
                nc.scalar.activation(sq[:, 1], x3[:, 1], ACT.Square, accum_out=ssq[:, 1:2]).then_inc(sq_done, 1)
                yield "xrT"
                take_B("xrT", i)
                nc.scalar.activation(xrT[:].rearrange("p k t -> p (k t)"), bB("xrT"), ACT.Copy)\
                    .then_inc(free_B[RING_B.bank["xrT"]], 1)
                yield "u"
                for g in range(2):
                    take_B(("u", g), i)
                    nc.scalar.activation(Uin[:, 2 * g:2 * g + 2, KC - 1:],
                                         bB(("u", g)).rearrange("p (m t) -> p m t", t=T), ACT.Copy)\
                        .then_inc(free_B[RING_B.bank["u", g]], 1)
                for g in range(2):
                    yield f"taps{g}"
                    act.wait_ge(conv_ready, i * 2 + (g + 1))
                    nc.scalar.activation(xs[:, 2 * g:2 * g + 2], xs[:, 2 * g:2 * g + 2], ACT.Silu).then_inc(xs_ready, 1)
                yield "low rank"
                take_B("dbc", i)
                nc.scalar.activation(bc3[0:32], bB("dbc")[64:96, 0:T], ACT.Copy).then_inc(bc_hi, 1)
                act.wait_ge(bc_hi, i + 1)
                nc.scalar.activation(dbc[0:DTR], bB("dbc")[0:DTR, 0:T], ACT.Copy).then_inc(dbc_ready, 1)
                yield "delta"
                for m in range(NM):
                    if m % 2 == 0:
                        take_B(("z", m // 2), i)
                    ins = nc.scalar.activation(dt_[:, m], bB(("z", m // 2))[:, (m % 2) * T:(m % 2 + 1) * T],
                                               ACT.Identity, bias=col("wd2_b", m))
                    if m % 2:
                        ins.then_inc(free_B[RING_B.bank["z", m // 2]], 1)
                act.wait_ge(free_B[RING_B.bank["z", 1]], RING_B.turn(("z", 1), i) + 1)
                link(nc.scalar.activation(sp[:], dt_[:], ACT.Abs))
                link(nc.scalar.activation(sp[:], sp[:], ACT.Exp, scale=-1.0))
                nc.scalar.activation(sp[:], sp[:], ACT.Ln, bias=1.0).then_inc(dt_act, 1)
                act.wait_ge(dt_ready, i + 1)
                for n in range(NS):
                    yield f"state{n}"
                    if n >= 2:
                        act.wait_ge(scan_done, i * NS + (n - 1))
                    for m in range(NM):
                        last = nc.scalar.activation(dA[:, n % 2, m, 1:T], dt_[:, m, 1:T], ACT.Exp,
                                                    scale=Aneg[:, m, n:n + 1])
                    last.then_inc(dA_ready, 1)
                yield "skip"
                act.wait_ge(dA_ready, i * NS + NS)
                for g in range(2):
                    take_B(("skip", g), i)
                    nc.scalar.activation(gate[:, 2 * g:2 * g + 2, :].rearrange("p m t -> p (m t)"), bB(("skip", g)),
                                         ACT.Silu).then_inc(free_B[RING_B.bank["skip", g]], 1)
                yield "x4T"
                take_B("x4T", i)
                nc.scalar.activation(x4T[:].rearrange("p k t -> p (k t)"), bB("x4T"), ACT.Copy)\
                    .then_inc(free_B[RING_B.bank["x4T"]], 1)
                yield "q2"
                take_B("q2", i)
                for m in range(ND):
                    last = nc.scalar.activation(q2T[:, m], bB("q2")[:, m * T:(m + 1) * T], ACT.Identity,
                                                bias=col("x_bq", m))
                last.then_inc(free_B[RING_B.bank["q2"]], 1)
                for t in range(NT):
                    yield f"T{t}3"
                    act.wait_ge(free_B[RING_B.bank["S", t, 3]], RING_B.turn(("S", t, 3), i) + 1)
                    nc.scalar.activation(Pr2[:, t].rearrange("p h j -> p (h j)"), Pr2[:, t].rearrange("p h j -> p (h j)"),
                                         ACT.Exp, scale=DH1 ** -0.5).then_inc(exp2_done, 1)
                for t in range(NT):
                    yield f"QT{t}"
                    if t:
                        take_B(("o", t - 1), i)
                    for g in range(4):
                        take_B(("PT", t, g), i)
                        nc.scalar.activation(PT2[:, 4 * g:4 * g + 4],
                                             bB(("PT", t, g))[0:KEYS].rearrange("j (h t) -> j h t", t=P), ACT.Copy)\
                            .then_inc(free_B[RING_B.bank["PT", t, g]], 1)
                yield "oT"
                take_B("oT", i)
                nc.scalar.activation(o2T[:].rearrange("p k t -> p (k t)"), bB("oT"), ACT.Copy)\
                    .then_inc(free_B[RING_B.bank["oT"]], 1)
                yield "x5T"
                take_B("x5T", i)
                nc.scalar.activation(x5T[:].rearrange("p k t -> p (k t)"), bB("x5T"), ACT.Copy)\
                    .then_inc(free_B[RING_B.bank["x5T"]], 1)
                yield "selT"
                take_B("selT", i)
                nc.scalar.activation(selT[:], bB("selT")[0:48, 0:T], ACT.Copy).then_inc(selT_ready, 1)
                for j in range(3):
                    for g in (0, 2):
                        yield f"net{j}{g}"
                        take_B(("hid", j, g), i)
                        for m in (2 * g, 2 * g + 1):
                            last = nc.scalar.activation(hid[:, m], bB(("hid", j, g))[:, (m % 2) * T:(m % 2 + 1) * T],
                                                        ACT.Relu, bias=col("f_b1", MF * j + m))
                        last.then_inc(free_B[RING_B.bank["hid", j, g]], 1)
                    yield f"out{j}"
                    take_B(("out", j, 0), i)
                    dst = qk3[:, j].rearrange("p k t -> p (k t)") if j < 2 else v3[:].rearrange("p t d -> p (t d)")
                    nc.scalar.activation(dst, bB(("out", j, 0)), ACT.Copy).then_inc(free_B[RING_B.bank["out", j, 0]], 1)
                yield "S3"
                act.wait_ge(mx3_ready, i + 1)
                for t in range(NT):
                    last = nc.scalar.activation(P3[:, t], bB("S3")[:, t * T:(t + 1) * T], ACT.Exp, bias=nm3[:, t:t + 1],
                                                scale=D ** -0.5, accum_out=den3[:, t:t + 1])
                last.then_inc(free_B[RING_B.bank["S3"]], 1)
                yield "P3"
                take_B("P3T", i)
                nc.scalar.activation(P3T[:].rearrange("p k t -> p (k t)"), bB("P3T"), ACT.Copy)\
                    .then_inc(free_B[RING_B.bank["P3T"]], 1)
                assert c == LINKS_ACT_B, c

            write_out(SEGMENTS_A, act_A(0))
            with act.Fori(0, NB - 1) as i:
                write_out(schedule(), act_A(i + 1), act_B(i))
            write_out(SEGMENTS_B, act_B(NB - 1))

        @block.vector
        def _(dve):
            vec = nc.vector

            dve.wait_ge(weights_loaded, 16 * N_WEIGHTS)
            dve.wait_ge(kvw_loaded, 16 * len(kv_weights))
            vec.tensor_scalar(lora[:], Cols[:, COLS["alpha"][0]:COLS["alpha"][1]], 1.0 / RANK, None, ALU.mult)\
                .then_inc(setup_vec, 1)
            dve.wait_ge(setup_vec, 1)
            merged = {"mq": (0, Wq), "mk": (1, Wk), "mv": (2, Wv), "mo": (3, Wo)}
            for name in BY_DVE:
                at = SETUP.index(name)
                ps = (psA if at % 8 < 4 else psB)[:, at % 4, :]
                dve.wait_ge(setup_full, at + 1)
                kind, f = name[0], name[-1]
                if kind == "v2":
                    if f == 0:
                        dve.wait_ge(setup_pool, 2)
                    if f >= 2:
                        dve.wait_ge(v2_stored[f % 2], 16 * (f // 2))
                    vec.tensor_tensor(V2s[:, f % 2, :, 0:DH1], ps[0:KEYS, 0:D].rearrange("j (h d) -> j h d", d=DH1),
                                      row("x1_bv")[0:KEYS].rearrange("j (h d) -> j h d", d=DH1), ALU.add)\
                        .then_inc(setup_dve, 1)
                    continue
                n, W = merged[kind]
                if kind == "mo":
                    w = W[:, 2 * f:2 * f + 2, :].rearrange("p m n -> p (m n)")
                else:
                    w = W[:, name[1], f * 512:(f + 1) * 512]
                h = CH if kind in ("mk", "mv") else P
                vec.scalar_tensor_tensor(w, ps[0:h], lora[0:h, n:n + 1], w, ALU.mult, ALU.add).then_inc(setup_dve, 1)
            for W in (Win, Wsk):
                for k in range(ND):
                    vec.tensor_scalar(W[:, k], W[:, k], col("norm_w", k), None, ALU.mult)
            dve.wait_ge(a_exp, 1)
            vec.tensor_scalar(Aneg[:], Aneg[:], -1.0, None, ALU.mult).then_inc(setup_vec, 1)
            dve.wait_ge(setup_init, 1)

            def dve_A(i):
                c = 0

                def link(ins):
                    nonlocal c
                    c += 1
                    ins.then_inc(links_vec_A, 1)
                    dve.wait_ge(links_vec_A, i * LINKS_VEC_A + c)

                def take(name):
                    dve.wait_ge(full_A, RING_A.filled(name, i))

                def give(ins, name):
                    ins.then_inc(free_A[RING_A.bank[name]], 1)

                def given(name):
                    dve.wait_ge(free_A[RING_A.bank[name]], RING_A.turn(name, i) + 1)

                def statistics():
                    for t in range(NT):
                        last = vec.bn_stats(bn[:, t], r[:, t])
                    link(last)
                    dve.sem_inc(alone_vec, 1)
                    for t in range(NT):
                        last = vec.bn_aggr(mv[:, t], bn[:, t])
                    link(last)
                    vec.tensor_scalar(var[:], mv[:, :, 1], EPS, None, ALU.add).then_inc(var_A, 1)

                def scale(n, dst, ready):
                    dve.wait_ge(rstd_A, i * 3 + (n + 1))
                    for t in range(NT):
                        last = vec.tensor_scalar(dst[:, t], r[:, t], mv[:, t, 0:1], rstd[:, t:t + 1], ALU.subtract, ALU.mult)
                    last.then_inc(ready, 1)

                yield "conv"
                dve.wait_ge(x3_ready, i + 1)
                take("conv")
                give(vec.tensor_tensor(r[:].rearrange("p t d -> p (t d)"), bA("conv"),
                                       xin[:].rearrange("p t d -> p (t d)"), ALU.add), "conv")
                given("conv")
                statistics()
                yield "x1"
                scale(0, x1, x1_ready)
                def normalisers(t):
                    dve.wait_ge(exp_done, i * NT + (t + 1))
                    vec.tensor_reduce(den[:, t, 0], Pr[:, t, :, 0:TEXT], AX.X, ALU.add)
                    link(vec.tensor_reduce(den[:, t, 1], Pr[:, t, :, TEXT:KEYS], AX.X, ALU.add))
                    vec.reciprocal(rden[:, t], den[:, t]).then_inc(den_ready, 1)

                for _, t, g in SROUND:
                    if (t, g) == (1, 1):
                        yield "norm0"
                        normalisers(0)
                    yield f"S{t}{g}"
                    take(("S", t, g))
                    hs4 = slice(4 * g, 4 * g + 4)
                    s4 = bA(("S", t, g))[:, 0:4 * KEYS].rearrange("p (h j) -> p h j", j=KEYS)
                    vec.tensor_reduce(mx[:, t, 0, hs4], s4[:, :, 0:TEXT], AX.X, ALU.max)
                    link(vec.tensor_reduce(mx[:, t, 1, hs4], s4[:, :, TEXT:KEYS], AX.X, ALU.max))
                    vec.tensor_tensor(Pr[:, t, hs4, 0:TEXT], s4[:, :, 0:TEXT],
                                      mx[:, t, 0, hs4].unsqueeze(2).broadcast_to([P, 4, TEXT]), ALU.subtract)
                    give(vec.tensor_tensor(Pr[:, t, hs4, TEXT:KEYS], s4[:, :, TEXT:KEYS],
                                           mx[:, t, 1, hs4].unsqueeze(2).broadcast_to([P, 4, IPA]), ALU.subtract),
                         ("S", t, g))
                yield "norm1"
                normalisers(1)
                yield "y1"
                take("y1")
                dve.wait_ge(x1b_ready, i + 1)
                give(vec.tensor_tensor(r[:].rearrange("p t d -> p (t d)"), bA("y1"),
                                       x1b[:].rearrange("p t d -> p (t d)"), ALU.add), "y1")
                given("y1")
                statistics()
                yield "x2"
                scale(1, x2, x2_ready)
                yield "router"
                take("router")
                give(vec.tensor_tensor(lg[:], bA("router")[:, 0:NT * EXPERTS].rearrange("p (t e) -> p t e", e=EXPERTS),
                                       row("router_b").unsqueeze(1).broadcast_to([P, NT, EXPERTS]), ALU.add), "router")
                given("router")
                link(vec.tensor_reduce(lx[:], lg[:], AX.X, ALU.max))
                vec.tensor_tensor(lg[:], lg[:], lx[:].unsqueeze(2).broadcast_to([P, NT, EXPERTS]), ALU.subtract)\
                    .then_inc(logits_ready, 1)
                yield "gates"
                dve.wait_ge(gates_exp, i + 1)
                dve.sem_inc(alone_vec, 1)
                for t in range(NT):
                    last = vec.max(top[:, t], pe_[:, t])
                link(last)
                dve.sem_inc(alone_vec, 1)
                for t in range(NT):
                    vec.max_index(tix[:, t], top[:, t], pe_[:, t])
                link(vec.tensor_tensor(ts[:], top[:, :, 0], top[:, :, 1], ALU.add))
                vec.tensor_copy(tif[:], tix[:, :, 0:2])
                link(vec.reciprocal(tr[:], ts[:]))
                link(vec.tensor_tensor(tw[:], top[:, :, 0:2], tr[:].unsqueeze(2).broadcast_to([P, NT, 2]), ALU.mult))
                for t in range(NT):
                    for s in range(2):
                        last = vec.tensor_scalar(mk[:, t, s], row("iota"), tif[:, t, s:s + 1], tw[:, t, s:s + 1],
                                                 ALU.is_equal, ALU.mult)
                link(last)
                link(vec.tensor_tensor(mask[:], mk[:, :, 0], mk[:, :, 1], ALU.add))
                link(vec.tensor_copy(mhi[:, :, 0], mask[:]))
                vec.tensor_copy(m3[:, :, 0], mhi[:, :, 0])
                link(vec.tensor_tensor(mr[:], mask[:], mhi[:, :, 0], ALU.subtract))
                link(vec.tensor_copy(mhi[:, :, 1], mr[:]))
                vec.tensor_copy(m3[:, :, 1], mhi[:, :, 1])
                vec.tensor_tensor(m3[:, :, 2], mr[:], mhi[:, :, 1], ALU.subtract).then_inc(mask_ready, 1)
                yield "maskT"
                take("maskT")
                vec.tensor_copy(mT[:], bA("maskT")[0:24, 0:T])
                give(vec.tensor_copy(mTb[:], bA("maskT")[0:24, 0:T]), "maskT")
                for g in range(4):
                    yield f"mb{g}"
                    given(("h", g))
                    take(("mb", g))
                    h2 = hT[:, 2 * g:2 * g + 2, :].rearrange("p e t -> p (e t)")
                    give(vec.tensor_tensor(h2, h2, bA(("mb", g)), ALU.mult), ("mb", g))
                yield "y2"
                take("y2")
                give(vec.tensor_tensor(r[:].rearrange("p t d -> p (t d)"), bA("y2"),
                                       x2[:].rearrange("p t d -> p (t d)"), ALU.add), "y2")
                given("y2")
                statistics()
                yield "x3"
                scale(2, x3, x3_ready)
                assert c == LINKS_VEC_A, ("LINKS_VEC_A", c)

            def dve_B(i):
                c = 0

                def link(ins):
                    nonlocal c
                    c += 1
                    ins.then_inc(links_vec_B, 1)
                    dve.wait_ge(links_vec_B, i * LINKS_VEC_B + c)

                def take(name):
                    dve.wait_ge(full_B, RING_B.filled(name, i))

                def give(ins, name):
                    ins.then_inc(free_B[RING_B.bank[name]], 1)

                def given(name):
                    dve.wait_ge(free_B[RING_B.bank[name]], RING_B.turn(name, i) + 1)

                def statistics():
                    for t in range(NT):
                        last = vec.bn_stats(bnB[:, t], rB[:, t])
                    link(last)
                    dve.sem_inc(alone_vec, 1)
                    for t in range(NT):
                        last = vec.bn_aggr(mvB[:, t], bnB[:, t])
                    link(last)
                    vec.tensor_scalar(varB[:], mvB[:, :, 1], EPS, None, ALU.add).then_inc(var_B, 1)

                def scale(n, dst, ready):
                    dve.wait_ge(rstd_B, i * 4 + (n + 1))
                    for t in range(NT):
                        last = vec.tensor_scalar(dst[:, t], rB[:, t], mvB[:, t, 0:1], rstdB[:, t:t + 1],
                                                 ALU.subtract, ALU.mult)
                    last.then_inc(ready, 1)

                yield "rms"
                dve.wait_ge(x6_ready, i + 1)
                dve.wait_ge(x3_ready, i + 2)
                vec.tensor_scalar(x3d[:], x3[:], 2.0, None, ALU.mult)
                dve.wait_ge(sq_done, i + 1)
                vec.tensor_scalar(varB[:], ssq[:], 1.0 / D, EPS, ALU.mult, ALU.add).then_inc(var_B, 1)
                yield "xr"
                dve.wait_ge(rstd_B, i * 4 + 1)
                for t in range(NT):
                    last = vec.tensor_scalar(xr[:, t], x3[:, t], rstdB[:, t:t + 1], None, ALU.mult)
                last.then_inc(xr_ready, 1)
                for g in range(2):
                    yield f"taps{g}"
                    given(("u", g))
                    ms = (2 * g, 2 * g + 1)
                    for m in ms:
                        last = vec.tensor_scalar(xs[:, m], Uin[:, m, 0:T], col("conv_w", KC * m), col("conv_b", m),
                                                 ALU.mult, ALU.add)
                    link(last)
                    for k in range(1, KC):
                        for m in ms:
                            last = vec.scalar_tensor_tensor(xs[:, m], Uin[:, m, k:k + T], col("conv_w", KC * m + k),
                                                            xs[:, m], ALU.mult, ALU.add)
                        if k < KC - 1:
                            link(last)
                    last.then_inc(conv_ready, 1)
                yield "low rank"
                dve.wait_ge(dbc_ready, i + 1)
                give(vec.tensor_tensor(bcr[32:64], bB("dbc")[64:96, 0:T], bc3[0:32], ALU.subtract), "dbc")
                given("dbc")
                link(vec.tensor_copy(bc3[32:64], bcr[32:64]))
                vec.tensor_tensor(bc3[64:96], bcr[32:64], bc3[32:64], ALU.subtract).then_inc(bc3_ready, 1)
                yield "dtx"
                dve.wait_ge(dt_act, i + 1)
                vec.scalar_tensor_tensor(dt_[:].rearrange("p m t -> p (m t)"), dt_[:].rearrange("p m t -> p (m t)"), 0.0,
                                         sp[:].rearrange("p m t -> p (m t)"), ALU.max, ALU.add).then_inc(dt_ready, 1)
                dve.wait_ge(dt_ready, i + 1)
                link(vec.tensor_tensor(dtx[:], dt_[:], xs[:], ALU.mult))
                for n in range(NS):
                    yield f"state{n}"
                    take(("bc", n))
                    bc = bB(("bc", n)).rearrange("p (s t) -> p s t", s=2)
                    link(vec.tensor_tensor(dBx[:], dtx[:], bc[:, 0:1, :].broadcast_to([P, NM, T]), ALU.mult))
                    dve.wait_ge(dA_ready, i * NS + (n + 1))
                    vec.tensor_tensor_scan(hs[:].rearrange("p m t -> p (m t)"),
                                           dA[:, n % 2].rearrange("p m t -> p (m t)"),
                                           dBx[:].rearrange("p m t -> p (m t)"), 0.0, ALU.mult, ALU.add)\
                        .then_inc(scan_done, 1)
                    dve.wait_ge(scan_done, i * NS + (n + 1))
                    if n >= 2:
                        dve.wait_ge(summed, i * (NS - 1) + (n - 1))
                    give(vec.tensor_tensor(hC[:, n % 2], hs[:], bc[:, 1:2, :].broadcast_to([P, NM, T]), ALU.mult),
                         ("bc", n))
                yield "ysum"
                given(("skip", 1))
                for g in range(2):
                    take(("ysum", g))
                    for m in (2 * g, 2 * g + 1):
                        last = vec.scalar_tensor_tensor(yT[:, m], xs[:, m], col("W_D", m),
                                                        bB(("ysum", g))[:, (m % 2) * T:(m % 2 + 1) * T],
                                                        ALU.mult, ALU.add)
                    give(last, ("ysum", g))
                    given(("ysum", g))
                vec.tensor_tensor(yT[:], yT[:], gate[:], ALU.mult).then_inc(yT_ready, 1)
                yield "my"
                take("my")
                give(vec.tensor_tensor(rB[:].rearrange("p t d -> p (t d)"), bB("my"),
                                       x3d[:].rearrange("p t d -> p (t d)"), ALU.add), "my")
                given("my")
                statistics()
                yield "x4"
                scale(1, x4, x4_ready)
                for _, t, g in SROUND:
                    yield f"T{t}{g}"
                    take(("S", t, g))
                    hs4 = slice(4 * g, 4 * g + 4)
                    s4 = bB(("S", t, g))[:, 0:4 * KEYS].rearrange("p (h j) -> p h j", j=KEYS)
                    link(vec.tensor_reduce(mx2[:, t, hs4], s4, AX.X, ALU.max))
                    give(vec.tensor_tensor(Pr2[:, t, hs4], s4, mx2[:, t, hs4].unsqueeze(2).broadcast_to([P, 4, KEYS]),
                                           ALU.subtract), ("S", t, g))
                for t in range(NT):
                    yield f"o{t}"
                    take(("o", t))
                    o = bB(("o", t))[:, 0:H1 * (DH1 + 1)].rearrange("p (h d) -> p h d", d=DH1 + 1)
                    link(vec.reciprocal(rd2[:, t], o[:, :, DH1]))
                    give(vec.tensor_tensor(o2[:, t], o[:, :, 0:DH1], rd2[:, t].unsqueeze(2).broadcast_to([P, H1, DH1]),
                                           ALU.mult), ("o", t))
                yield "y3"
                take("y3")
                dve.wait_ge(x4b_ready, i + 1)
                give(vec.tensor_tensor(rB[:].rearrange("p t d -> p (t d)"), bB("y3"),
                                       x4b[:].rearrange("p t d -> p (t d)"), ALU.add), "y3")
                given("y3")
                statistics()
                yield "x5"
                scale(2, x5, x5_ready)
                yield "node"
                take("node")
                give(vec.tensor_tensor(sc[:].rearrange("p (t j) n -> p t (j n)", t=NT),
                                       bB("node")[:, 0:NT * 3 * NODES].rearrange("p (t n) -> p t n", t=NT),
                                       row("node_b").unsqueeze(1).broadcast_to([P, NT, 3 * NODES]), ALU.add), "node")
                given("node")
                link(vec.tensor_scalar(dec[:], sc[:], 0.0, None, ALU.is_ge))
                vec.tensor_copy(lv[0][:, :, 1], dec[:, :, 0])
                link(vec.tensor_scalar(lv[0][:, :, 0], dec[:, :, 0], -1.0, 1.0, ALU.mult, ALU.add))
                for n in range(1, 4):
                    w = 2 ** n
                    pair = lv[n][:].rearrange("p j (w c) -> p j w c", c=2)
                    link(vec.tensor_tensor(pair[:, :, :, 1], lv[n - 1][:], dec[:, :, w - 1:2 * w - 1], ALU.mult))
                    last = vec.tensor_tensor(pair[:, :, :, 0], lv[n - 1][:], pair[:, :, :, 1], ALU.subtract)
                    if n < 3:
                        link(last)
                last.then_inc(sel_ready, 1)
                yield "selT"
                dve.wait_ge(selT_ready, i + 1)
                give(vec.tensor_scalar(nsel[:], bB("selT")[0:48, 0:T], BIG, -BIG, ALU.mult, ALU.add), "selT")
                for j in range(3):
                    for g in (1, 3):
                        yield f"net{j}{g}"
                        take(("hid", j, g))
                        for m in (2 * g, 2 * g + 1):
                            last = vec.tensor_scalar(hid[:, m], bB(("hid", j, g))[:, (m % 2) * T:(m % 2 + 1) * T],
                                                     col("f_b1", MF * j + m), 0.0, ALU.add, ALU.max)
                        give(last, ("hid", j, g))
                yield "S3"
                take("S3")
                link(vec.tensor_reduce(mx3[:], bB("S3").rearrange("p (t k) -> p t k", t=NT), AX.X, ALU.max))
                vec.tensor_scalar(nm3[:], mx3[:], -(D ** -0.5), None, ALU.mult).then_inc(mx3_ready, 1)
                yield "P3"
                given("S3")
                link(vec.reciprocal(rd3[:], den3[:]))
                yield "y4"
                take("y4")
                for t in range(NT):
                    last = vec.scalar_tensor_tensor(rB[:, t], bB("y4")[:, t * D:(t + 1) * D], rd3[:, t:t + 1], x5[:, t],
                                                    ALU.mult, ALU.add)
                give(last, "y4")
                given("y4")
                statistics()
                yield "x6"
                dve.wait_ge(out_stored, i * 16 + 16)
                scale(3, x6, x6_ready)
                assert c == LINKS_VEC_B, ("LINKS_VEC_B", c)

            write_out(SEGMENTS_A, dve_A(0))
            with dve.Fori(0, NB - 1) as i:
                write_out(schedule(), dve_A(i + 1), dve_B(i))
            write_out(SEGMENTS_B, dve_B(NB - 1))

        @block.tensor
        def _(pe):
            mm, tp = nc.tensor.matmul, nc.tensor.transpose

            pe.wait_ge(kvw_loaded, 16 * len(kv_weights))
            pe.wait_ge(weights_loaded, 16 * N_WEIGHTS)
            for at, name in enumerate(SETUP):
                ps = (psA if at % 8 < 4 else psB)[:, at % 4, :]
                if at >= 8:
                    before = SETUP[at - 8]
                    if before in BY_ACT:
                        pe.wait_ge(setup_act, BY_ACT[before] + 1)
                    else:
                        pe.wait_ge(setup_dve, BY_DVE[before] + 1)
                kind = name[0]
                if kind in ("mk", "mv", "mq"):
                    _, c, f = name
                    d0, w, u = {"mk": (DnK, CH, 1), "mv": (DnV, CH, 2), "mq": (DnQ, P, 0)}[kind]
                    last = mm(ps[0:w], Dn[:, d0 + w * c:d0 + w * (c + 1)], Up[:, u, f * 512:(f + 1) * 512],
                              start=True, stop=True)
                elif kind == "mo":
                    for m in (2 * name[1], 2 * name[1] + 1):
                        last = mm(ps[:, (m % 2) * D:(m % 2 + 1) * D], Dn[:, DnO + m * P:DnO + (m + 1) * P], Ou[:],
                                  start=True, stop=True)
                elif kind == "k":
                    _, m, f = name
                    if m == f == 0:
                        pe.wait_ge(setup_dve, 4)
                    for c in range(2):
                        mm(ps[:, 0:480], Wk[:, c, m * P:(m + 1) * P], Ct[:, c, f * 480:(f + 1) * 480],
                           start=c == 0, stop=c == 1)
                    ipa = ps[:, 0:480].rearrange("p (b j) -> p b j", j=KEYS)[:, :, TEXT:KEYS]
                    for c in range(2):
                        last = mm(ipa, Wki[:, c, m * P:(m + 1) * P],
                                  Ci[:, c, f * 4 * IPA:(f + 1) * 4 * IPA].rearrange("p (b j) -> p b j", j=IPA),
                                  start=c == 0, stop=c == 1)
                elif kind == "v":
                    _, b, f = name
                    if b == f == 0:
                        pe.wait_ge(setup_dve, 8)
                    for c in range(2):
                        last = mm(ps[0:KEYS], Ct[:, c, b * KEYS:(b + 1) * KEYS], Wv[:, c, f * 512:(f + 1) * 512],
                                  start=c == 0, stop=c == 1)
                elif kind == "vi":
                    for c in range(2):
                        last = mm(ps[0:NB * IPA], Ci[:, c, :], Wvi[:, c, name[1] * 512:(name[1] + 1) * 512],
                                  start=c == 0, stop=c == 1)
                elif kind == "k2":
                    _, m, f = name
                    for c in range(2):
                        last = mm(ps[:, 0:480], Wk2[:, c, m * P:(m + 1) * P], Ct[:, c, f * 480:(f + 1) * 480],
                                  start=c == 0, stop=c == 1)
                else:
                    b = name[1]
                    for c in range(2):
                        last = mm(ps[0:KEYS, 0:D], Ct[:, c, b * KEYS:(b + 1) * KEYS], Wv2[:, c, :],
                                  start=c == 0, stop=c == 1)
                last.then_inc(setup_full, 1)
            pe.wait_ge(setup_act, len(BY_ACT))
            pe.wait_ge(setup_dve, len(BY_DVE))
            pe.wait_ge(setup_vec, 2)

            def pe_A(i):
                def room(name):
                    pe.wait_ge(free_A[RING_A.bank[name]], RING_A.turn(name, i))

                def taken(name):
                    pe.wait_ge(free_A[RING_A.bank[name]], RING_A.turn(name, i) + 1)

                def full(ins):
                    ins.then_inc(full_A, 1)

                def to_cols(name, rows_):
                    room(name)
                    for k in range(ND):
                        for t in range(NT):
                            last = tp(bA(name)[:, k * T + t * P:k * T + (t + 1) * P], rows_[:, t, k * P:(k + 1) * P],
                                      ident[:])
                    full(last)

                yield "conv"
                room("conv")
                pe.wait_ge(x_loaded, i * 16 + 16)
                mm(bA("conv")[:, 0:D], Toep[:, 0], xin[:, 0], start=True, stop=False)
                mm(bA("conv")[:, 0:D], Toep[:, 1], xin[:, 1], start=False, stop=True)
                full(mm(bA("conv")[:, D:2 * D], Toep[:, 0], xin[:, 1], start=True, stop=True))
                yield "x1T"
                pe.wait_ge(x1_ready, i + 1)
                to_cols("x1T", x1)
                for g in range(4):
                    yield f"q{g}"
                    if g == 0:
                        taken("x1T")
                    room(("q", g))
                    for m in (2 * g, 2 * g + 1):
                        for k in range(ND):
                            last = mm(bA(("q", g))[:, (m % 2) * T:(m % 2 + 1) * T], Wq[:, k, m * P:(m + 1) * P],
                                      x1T[:, k], start=k == 0, stop=k == 1)
                    full(last)
                for _, t, g in SROUND:
                    yield f"S{t}{g}"
                    if t == g == 0:
                        pe.wait_ge(kv_loaded, i * 16 * LOADS[0] + 16 * LOADS[0])
                    if t == 0:
                        taken(("q", g))
                    room(("S", t, g))
                    for m in (2 * g, 2 * g + 1):
                        last = mm(bA(("S", t, g))[:, (m % 2) * 2 * KEYS:(m % 2 + 1) * 2 * KEYS],
                                  qT[:, m, t * P:(t + 1) * P], Kbd[:, m], start=True, stop=True)
                    full(last)
                for t in range(NT):
                    yield f"PT{t}"
                    pe.wait_ge(probs_ready, i * NT + (t + 1))
                    for g in range(4):
                        room(("PT", t, g))
                        for h in range(4):
                            last = tp(bA(("PT", t, g))[0:KEYS, h * P:(h + 1) * P], Pr[:, t, 4 * g + h], ident[:])
                        full(last)
                    yield f"O{t}"
                    for f in range(2):
                        for g in (2 * f, 2 * f + 1):
                            taken(("PT", t, g))
                        room(("O", t, f))
                        for h in range(8 * f, 8 * f + 8):
                            m = h // 2
                            last = mm(bA(("O", t, f))[64 * (h % 2):64 * (h % 2) + 64, (m % 4) * P:(m % 4 + 1) * P],
                                      V[:, h * DH0:(h + 1) * DH0], PT[:, h], start=True, stop=True)
                        full(last)
                yield "y1"
                taken(("O", 1, 1))
                room("y1")
                for t in range(NT):
                    for m in range(M0):
                        last = mm(bA("y1")[:, t * D:(t + 1) * D], OT[:, m, t * P:(t + 1) * P], Wo[:, m],
                                  start=m == 0, stop=m == M0 - 1)
                full(last)
                yield "x2T"
                pe.wait_ge(x2_ready, i + 1)
                to_cols("x2T", x2)
                yield "router"
                taken("x2T")
                room("router")
                for t in range(NT):
                    for k in range(ND):
                        last = mm(bA("router")[:, t * EXPERTS:(t + 1) * EXPERTS], x2T[:, k, t * P:(t + 1) * P], Rw[:, k],
                                  start=k == 0, stop=k == 1)
                full(last)
                for g in range(4):
                    yield f"h{g}"
                    room(("h", g))
                    for e in (2 * g, 2 * g + 1):
                        for k in range(ND):
                            last = mm(bA(("h", g))[:, (e % 2) * T:(e % 2 + 1) * T], W1[:, k, e * EF:(e + 1) * EF],
                                      x2T[:, k], start=k == 0, stop=k == 1)
                    full(last)
                yield "maskT"
                room("maskT")
                pe.wait_ge(mask_ready, i + 1)
                for t in range(NT):
                    last = tp(bA("maskT")[0:24, t * P:(t + 1) * P], m3[:, t].rearrange("p s e -> p (s e)"), ident[:])
                full(last)
                for g in range(4):
                    yield f"mb{g}"
                    if g == 0:
                        taken("maskT")
                    room(("mb", g))
                    for e in (2 * g, 2 * g + 1):
                        last = mm(bA(("mb", g))[:, (e % 2) * T:(e % 2 + 1) * T], Sel24[:, e:e + 1].broadcast_to([24, P]), mTb[:], start=True, stop=True)
                    full(last)
                yield "y2"
                taken(("mb", 3))
                room("y2")
                for t in range(NT):
                    for e in range(EXPERTS):
                        mm(bA("y2")[:, t * D:(t + 1) * D], hT[:, e, t * P:(t + 1) * P], W2[:, e],
                           start=e == 0, stop=False)
                    last = mm(bA("y2")[:, t * D:(t + 1) * D], mT[:, t * P:(t + 1) * P], B2[:], start=False, stop=True)
                full(last)

            def pe_B(i):
                def room(name):
                    pe.wait_ge(free_B[RING_B.bank[name]], RING_B.turn(name, i))

                def taken(name):
                    pe.wait_ge(free_B[RING_B.bank[name]], RING_B.turn(name, i) + 1)

                def full(ins):
                    ins.then_inc(full_B, 1)

                def to_cols(name, rows_):
                    room(name)
                    for k in range(ND):
                        for t in range(NT):
                            last = tp(bB(name)[:, k * T + t * P:k * T + (t + 1) * P], rows_[:, t, k * P:(k + 1) * P],
                                      ident[:])
                    full(last)

                yield "xrT"
                pe.wait_ge(xr_ready, i + 1)
                to_cols("xrT", xr)
                yield "u"
                taken("xrT")
                def inward(s, W):
                    for g in range(2):
                        room((s, g))
                        for m in (2 * g, 2 * g + 1):
                            for k in range(ND):
                                last = mm(bB((s, g))[:, (m % 2) * T:(m % 2 + 1) * T], W[:, k, m * P:(m + 1) * P],
                                          xrT[:, k], start=k == 0, stop=k == 1)
                        full(last)

                inward("u", Win)
                yield "low rank"
                room("dbc")
                for m in range(NM):
                    if m % 2 == 0:
                        pe.wait_ge(xs_ready, i * 2 + (m // 2 + 1))
                    last = mm(bB("dbc")[0:96, 0:T], Wdbc[:, m], xs[:, m], start=m == 0, stop=m == NM - 1)
                full(last)
                yield "delta"
                pe.wait_ge(dbc_ready, i + 1)
                for g in range(2):
                    room(("z", g))
                    for m in (2 * g, 2 * g + 1):
                        last = mm(bB(("z", g))[:, (m % 2) * T:(m % 2 + 1) * T], Wd2[:, m * P:(m + 1) * P], dbc[0:DTR],
                                  start=True, stop=True)
                    full(last)
                pe.wait_ge(bc3_ready, i + 1)

                def broadcast(n):
                    room(("bc", n))
                    mm(bB(("bc", n))[:, 0:T], Sel96[:, n:n + 1].broadcast_to([96, P]), bc3[:], start=True, stop=True)
                    full(mm(bB(("bc", n))[:, T:2 * T], Sel96[:, NS + n:NS + n + 1].broadcast_to([96, P]), bc3[:], start=True, stop=True))

                broadcast(0)
                broadcast(1)

                def sum_up(n):
                    taken(("bc", n))
                    for g in range(2):
                        if n == 0:
                            room(("ysum", g))
                        last = mm(bB(("ysum", g)), ident[:], hC[:, n % 2, 2 * g:2 * g + 2].rearrange("p m t -> p (m t)"),
                                  start=n == 0, stop=n == NS - 1, skip_group_check=True)
                        if n == NS - 1:
                            full(last)
                    if n < NS - 1:
                        last.then_inc(summed, 1)

                for n in range(1, NS):
                    yield f"state{n}"
                    sum_up(n - 1)
                    if n + 1 < NS:
                        broadcast(n + 1)
                yield "skip"
                sum_up(NS - 1)
                inward("skip", Wsk)
                yield "my"
                pe.wait_ge(yT_ready, i + 1)
                room("my")
                for t in range(NT):
                    for m in range(NM):
                        last = mm(bB("my")[:, t * D:(t + 1) * D], yT[:, m, t * P:(t + 1) * P], Wout[:, m],
                                  start=m == 0, stop=m == NM - 1)
                full(last)
                yield "x4T"
                pe.wait_ge(x4_ready, i + 1)
                to_cols("x4T", x4)
                yield "q2"
                taken("x4T")
                room("q2")
                for m in range(ND):
                    for k in range(ND):
                        last = mm(bB("q2")[:, m * T:(m + 1) * T], Wq2[:, k, m * P:(m + 1) * P], x4T[:, k],
                                  start=k == 0, stop=k == 1)
                full(last)
                for _, t, g in SROUND:
                    yield f"T{t}{g}"
                    if t == g == 0:
                        taken("q2")
                        pe.wait_ge(kv2_loaded, i * 16 * LOADS[1] + 16 * LOADS[1])
                    room(("S", t, g))
                    full(mm(bB(("S", t, g))[:, 0:4 * KEYS], q2T[:, g // 2, t * P:(t + 1) * P],
                            Kbd2[:, g // 2, 4 * (g % 2):4 * (g % 2) + 4].rearrange("p h j -> p (h j)"),
                            start=True, stop=True))
                for t in range(NT):
                    yield f"QT{t}"
                    pe.wait_ge(exp2_done, i * NT + (t + 1))
                    for g in range(4):
                        room(("PT", t, g))
                        for h in range(4):
                            last = tp(bB(("PT", t, g))[0:KEYS, h * P:(h + 1) * P], Pr2[:, t, 4 * g + h], ident[:])
                        full(last)
                    yield f"o{t}"
                    taken(("PT", t, 3))
                    room(("o", t))
                    for h in range(H1):
                        last = mm(bB(("o", t))[:, h * (DH1 + 1):(h + 1) * (DH1 + 1)], PT2[:, h],
                                  V2[:, h], start=True, stop=True)
                    full(last)
                yield "oT"
                taken(("o", 1))
                room("oT")
                for k in range(ND):
                    for t in range(NT):
                        last = tp(bB("oT")[:, k * T + t * P:k * T + (t + 1) * P],
                                  o2[:, t, 8 * k:8 * k + 8].rearrange("p h d -> p (h d)"), ident[:])
                full(last)
                yield "y3"
                taken("oT")
                room("y3")
                for t in range(NT):
                    for k in range(ND):
                        last = mm(bB("y3")[:, t * D:(t + 1) * D], o2T[:, k, t * P:(t + 1) * P], Wo2[:, k],
                                  start=k == 0, stop=k == 1)
                full(last)
                yield "x5T"
                pe.wait_ge(x5_ready, i + 1)
                to_cols("x5T", x5)
                yield "node"
                taken("x5T")
                room("node")
                for t in range(NT):
                    for k in range(ND):
                        last = mm(bB("node")[:, t * 3 * NODES:(t + 1) * 3 * NODES], x5T[:, k, t * P:(t + 1) * P],
                                  Nw[:, k], start=k == 0, stop=k == 1)
                full(last)
                yield "selT"
                room("selT")
                pe.wait_ge(sel_ready, i + 1)
                pe.sem_inc(alone_pe, 1)
                for t in range(NT):
                    last = tp(bB("selT")[0:48, t * P:(t + 1) * P],
                              lv[3][:, 3 * t:3 * t + 3].rearrange("p j l -> p (j l)"), ident[:])
                full(last)
                for j in range(3):
                    for g in range(4):
                        yield f"net{j}{g}"
                        if g == 0:
                            pe.wait_ge(fw1_loaded, i * 48 + 16 * (j + 1))
                            if j == 0:
                                taken("selT")
                        room(("hid", j, g))
                        for m in (2 * g, 2 * g + 1):
                            h = bB(("hid", j, g))[:, (m % 2) * T:(m % 2 + 1) * T]
                            for k in range(ND):
                                mm(h, FW1[:, k, m * P:(m + 1) * P], x5T[:, k], start=k == 0, stop=False)
                            last = mm(h, Sel48[:, j, m], nsel[:], start=False, stop=True)
                        full(last)
                    yield f"out{j}"
                    pe.wait_ge(fw2_loaded, i * 48 + 16 * (j + 1))
                    taken(("hid", j, 2))
                    taken(("hid", j, 3))
                    room(("out", j, 0))
                    for o in range(2):
                        dst = bB(("out", j, 0))[:, o * T:(o + 1) * T]
                        for m in range(MF):
                            if j < 2:
                                mm(dst, FW2[:, m, o * P:(o + 1) * P], hid[:, m], start=m == 0, stop=False)
                            else:
                                mm(dst, hid[:, m, o * P:(o + 1) * P], FW2[:, m], start=m == 0, stop=False)
                        if j < 2:
                            last = mm(dst, FB2[:, j, o * P:(o + 1) * P], selT[:], start=False, stop=True)
                        else:
                            last = mm(dst, selT[:, o * P:(o + 1) * P], FB2[:, j], start=False, stop=True)
                    full(last)
                yield "S3"
                taken(("out", 1, 0))
                room("S3")
                for t in range(NT):
                    for k in range(ND):
                        last = mm(bB("S3")[:, t * T:(t + 1) * T], qk3[:, 0, k, t * P:(t + 1) * P], qk3[:, 1, k],
                                  start=k == 0, stop=k == 1)
                full(last)
                yield "P3"
                taken("S3")
                room("P3T")
                for k in range(NT):
                    for t in range(NT):
                        last = tp(bB("P3T")[:, k * T + t * P:k * T + (t + 1) * P], P3[:, t, k * P:(k + 1) * P], ident[:])
                full(last)
                yield "y4"
                taken("P3T")
                taken(("out", 2, 0))
                room("y4")
                for t in range(NT):
                    for k in range(NT):
                        last = mm(bB("y4")[:, t * D:(t + 1) * D], P3T[:, k, t * P:(t + 1) * P], v3[:, k],
                                  start=k == 0, stop=k == 1)
                full(last)

            write_out(SEGMENTS_A, pe_A(0))
            with pe.Fori(0, NB - 1) as i:
                write_out(schedule(), pe_A(i + 1), pe_B(i))
            write_out(SEGMENTS_B, pe_B(NB - 1))


def kernel(**inputs):
    import numpy as np
    import ml_dtypes
    import concourse.bacc as bacc
    from concourse.bass_utils import run_bass_kernel_spmd as run

    g = {k: np.asarray(v) for k, v in inputs.items()}
    f32 = np.float32

    padded = np.concatenate([np.zeros(P - 1, f32), g["L0_attn_filt"][:T]])
    k, t = np.arange(P)[:, None], np.arange(P)[None, :]
    toep = np.stack([padded[k - t + P - 1], padded[k - t + 2 * P - 1]])

    def vec(a):
        return np.asarray(a).reshape(-1, P).T

    cols = np.concatenate([
        vec(g["L0_ffn_b1"]),
        g["L1_attn_conv_w"].reshape(NM, P, KC).transpose(1, 0, 2).reshape(P, NM * KC),
        vec(g["L1_attn_conv_b"]), vec(g["L1_attn_wd2_b"]), vec(g["L1_attn_W_D"]),
        vec(g["L1_xattn_bq"]), vec(g["L1_xattn_bk"]),
        vec(g["L1_ffn_q_b1"]), vec(g["L1_ffn_k_b1"]), vec(g["L1_ffn_v_b1"]),
        vec(g["L1_attn_norm_w"]),
        g["L1_attn_A_log"].reshape(NM, P, NS).transpose(1, 0, 2).reshape(P, NM * NS),
        np.broadcast_to(np.concatenate([g[f"L0_xattn_{s}_alpha"] for s in "qkvo"])[None], (P, 4)),
    ], axis=1)
    rows = np.broadcast_to(np.concatenate([
        g["L0_xattn_bo"], g["L0_ffn_router_b"], g["L1_xattn_bv"], g["L1_xattn_bo"],
        g["L1_ffn_q_node_b"], g["L1_ffn_k_node_b"], g["L1_ffn_v_node_b"],
        np.arange(EXPERTS).astype(f32)])[None], (P, NROWS))

    ctxT = g["ctx_768"].transpose(2, 0, 1)
    sel24 = np.tile(np.eye(EXPERTS, dtype=f32), (3, 1))
    sel96 = np.tile(np.eye(32, dtype=f32), (3, 1))
    sel48 = np.zeros((48, 3, MF, P), f32)
    for j in range(3):
        for m in range(MF):
            for a in range(2):
                sel48[LEAVES * j + 2 * m + a, j, m, LW * a:LW * (a + 1)] = 1
    fb2 = np.zeros((3, 48, D), f32)
    for j, s in enumerate("qkv"):
        fb2[j, LEAVES * j:LEAVES * (j + 1)] = g[f"L1_ffn_{s}_b2"]

    data = dict(
        x=g["x"], toep=toep, ctxT=ctxT.reshape(CTX, NB * KEYS), ctxiT=ctxT[:, :, TEXT:].reshape(CTX, NB * IPA),
        cols=cols, rows=rows, ident_in=np.eye(P, dtype=f32),
        sel24_in=sel24.astype(ml_dtypes.bfloat16), sel96_in=sel96.astype(ml_dtypes.bfloat16),
        sel48_in=sel48.astype(ml_dtypes.bfloat16),
        wq=g["L0_xattn_Wq"], wk=g["L0_xattn_Wk"], wv=g["L0_xattn_Wv"], wo=g["L0_xattn_Wo"],
        qdT=g["L0_xattn_q_down"].T, kdT=g["L0_xattn_k_down"].T, vdT=g["L0_xattn_v_down"].T, odT=g["L0_xattn_o_down"].T,
        qu=g["L0_xattn_q_up"], ku=g["L0_xattn_k_up"], vu=g["L0_xattn_v_up"], ou=g["L0_xattn_o_up"],
        wki=g["L0_xattn_Wk_ipa"], wvi=g["L0_xattn_Wv_ipa"],
        rw=g["L0_ffn_router_w"], w1=g["L0_ffn_W1"].transpose(1, 0, 2).reshape(D, EXPERTS * EF), w2=g["L0_ffn_W2"],
        b2=np.tile(g["L0_ffn_b2"], (3, 1)),
        win=g["L1_attn_in_w"].T, wsk=g["L1_attn_skip_w"].T,
        wdbc=np.concatenate([g["L1_attn_wd1"], g["L1_attn_wb"], g["L1_attn_wc"]]).T,
        wd2=g["L1_attn_wd2"].T, wout=g["L1_attn_out_w"].T,
        wq2=g["L1_xattn_Wq"], wk2=g["L1_xattn_Wk"], wv2=g["L1_xattn_Wv"], wo2=g["L1_xattn_Wo"],
        nw=np.concatenate([g[f"L1_ffn_{s}_node_w"] for s in "qkv"]).T,
        fw1=np.stack([g[f"L1_ffn_{s}_w1"].transpose(1, 0, 2).reshape(D, LEAVES * LW) for s in "qkv"]),
        fw2=np.stack([g[f"L1_ffn_{s}_w2"].reshape(LEAVES * LW, D) for s in "qkv"]),
        fb2=fb2,
    )
    nc = bacc.Bacc("TRN2", target_bir_lowering=False, num_devices=1)
    arrays, args = {}, {}
    for name, a in data.items():
        a = np.ascontiguousarray(a)
        arrays[f"in_{name}"] = a
        args[name] = nc.dram_tensor(f"in_{name}", a.shape, mybir.dt.from_np(a.dtype), kind="ExternalInput").ap()
    out = nc.dram_tensor("out_0_dram", (NB, T, D), mybir.dt.float32, kind="ExternalOutput").ap()
    decoder(nc, out=out, **args)
    r = run(nc, [arrays], core_ids=[0])
    return r.results[0]["out_0_dram"]
```

```python
import concourse.bass as bass
from concourse import mybir
from contextlib import ExitStack

NB, T, D = 8, 256, 256
P = 128
NT, ND = T // P, D // P
KEYS, IPA = 120, 4
TEXT = KEYS - IPA
CTX = 192
CH = CTX // 2
RANK = 32
H0, DH0 = 16, 64
M0 = H0 * DH0 // P
H1, DH1 = 16, 16
EXPERTS, EF = 8, 128
DI, NS, DTR, KC = 512, 16, 64, 4
NM = DI // P
LEAVES, LW, NODES = 16, 64, 15
MF = LEAVES * LW // P
EPS = 1e-5
BIG = float(2.0 ** 100)

COLS = {}
_at = 0
for _name, _n in (("moe_b1", EXPERTS), ("conv_w", NM * KC), ("conv_b", NM), ("wd2_b", NM), ("W_D", NM),
                  ("x_bq", ND), ("x_bk", ND), ("f_b1", 3 * MF), ("norm_w", ND), ("A_log", NM * NS),
                  ("alpha", 4)):
    COLS[_name] = (_at, _at + _n)
    _at += _n
NCOLS = _at
ROWS = {}
_at = 0
for _name, _n in (("x0_bo", D), ("router_b", EXPERTS), ("x1_bv", D), ("x1_bo", D), ("node_b", 3 * NODES),
                  ("iota", EXPERTS)):
    ROWS[_name] = (_at, _at + _n)
    _at += _n
NROWS = _at


class Ring:

    def __init__(self, leading, trailing, banks=4):
        self.order, self.bank, self.use = {}, {}, {}
        self.trails = {name: False for name in leading} | {name: True for name in trailing}
        self.fills = (len(leading), len(trailing))
        self.uses = [[0, 0] for _ in range(banks)]
        for names in (leading, trailing):
            for n, name in enumerate(names):
                self.order[name], self.bank[name] = n, n % banks
                self.use[name] = self.uses[n % banks][self.trails[name]]
                self.uses[n % banks][self.trails[name]] += 1

    def before(self, name, i):
        if self.trails[name]:
            return min(i + 2, NB) if isinstance(i, int) else i + 2, i
        return i, max(i - 1, 0) if isinstance(i, int) else i - 1

    def filled(self, name, i):
        a, b = self.before(name, i)
        return a * self.fills[0] + b * self.fills[1] + (self.order[name] + 1)

    def turn(self, name, i):
        a, b = self.before(name, i)
        uses = self.uses[self.bank[name]]
        return a * uses[0] + b * uses[1] + (self.use[name] + 1)


def rounds(s):
    return [(s, t, g) for t in range(NT) for g in range(4)]


RING_A = Ring(
    ["conv", "x1T"] + [("q", g) for g in range(4)] + rounds("S")
    + [f for t in range(NT) for f in [("PT", t, g) for g in range(4)] + [("O", t, 0), ("O", t, 1)]]
    + ["y1", "x2T", "router"] + [("h", g) for g in range(4)] + ["maskT"] + [("mb", g) for g in range(4)] + ["y2"],
    ["x4T", "q2"] + rounds("S2") + [f for t in range(NT) for f in [("PT2", t, g) for g in range(4)] + [("o", t)]]
    + ["oT", "y3"])
RING_B = Ring(
    ["xrT", ("u", 0), ("u", 1), ("skip", 0), ("skip", 1), "dbc", ("z", 0), ("z", 1)] + [("bc", n) for n in range(NS)]
    + ["my"],
    ["x5T", "node", "selT"] + [(s, j, g) for j in range(3) for s, n in (("hid", 4), ("out", 1)) for g in range(n)]
    + ["S3", "P3T", "y4"])

TILES = [(t, g) for t in range(NT) for g in range(4)]

def grid(s):
    return [f"{s}{t}{g}" for t in range(NT) for g in range(4)]


def four(s):
    return [f"{s}{g}" for g in range(4)]


SEGMENTS_A = (["conv", "x1", "x1T"] + four("q") + grid("S")[:5] + ["norm0"] + grid("S")[5:]
              + ["PT0", "norm1", "O0", "PT1", "O1", "y1a", "y1", "x2", "x2T", "router", "h0", "gates", "h1", "h2", "h3", "gelu", "maskT"]
              + four("mb") + ["y2a", "y2", "x3"])
SEGMENTS_M = (["rms", "xr", "xrT", "u", "skip", "taps0", "taps1", "gate", "low rank", "delta", "dtx"]
              + [s for n in range(NS) for s in ((f"state{n}", f"add{n-1}") if n else ("state0",))] + ["add15", "y", "my", "x4"])
SEGMENTS_X = ["x4T", "qx"] + grid("T") + ["QT0", "o0", "QT1", "o1", "oT", "y3", "x5"]
SEGMENTS_F = (["x5T", "node", "tree", "selT"]
              + [s for j in range(3) for s in four(f"net{j}") + [f"out{j}a", f"out{j}"]] + ["S3", "P3", "y4", "x6"])
PAIRS = [("x4T", "x5T"), ("T01", "selT"), ("T12", "out0"), ("S00", "y4"), ("gates", "add3"), ("mb2", "state12"), ("x3", "x4")]
OPENING_PAIRS = [("conv", "late3"), ("y1", "late25")]
FIRST_PAIRS = [("S11", "dtx"), ("mb3", "state14"), ("x3", "x4")]
SECOND_PAIRS = [("QT0", "skip"), ("y3", "state0"), ("S00", "add5"), ("x3", "x4")]
LAST_PAIRS = [("x5", "P3")]


def interleaved(ours, theirs, pairs):
    order, a, b = [], 0, 0
    for stop_a, stop_b in pairs:
        na, nb = ours.index(stop_a, a) + 1 - a, theirs.index(stop_b, b) + 1 - b
        for n in range(na + nb):
            if (n + 1) * na // (na + nb) > n * na // (na + nb):
                order.append(ours[a])
                a += 1
            else:
                order.append(theirs[b])
                b += 1
    return order + theirs[b:] + ours[a:]


FIRST = interleaved(SEGMENTS_A, SEGMENTS_M, FIRST_PAIRS)
SECOND = interleaved(SEGMENTS_X + SEGMENTS_A, SEGMENTS_M, SECOND_PAIRS)
STEADY = interleaved(SEGMENTS_X + SEGMENTS_A, SEGMENTS_F + SEGMENTS_M, PAIRS)
LAST = interleaved(SEGMENTS_X, SEGMENTS_F, LAST_PAIRS)


def write_out(order, *halves):
    coming = [next(half, None) for half in halves]
    for segment in order:
        for n, half in enumerate(halves):
            while coming[n] == segment:
                coming[n] = next(half, None)
    assert not any(coming), coming


MERGES = [("mk", c, f) for c in range(2) for f in range(2)] + [("mv", c, f) for c in range(2) for f in range(2)]
EARLY = (MERGES + [("ki",)] + [("k", m, f) for m in range(M0) for f in range(2)] + [("v", 0, f) for f in range(2)]
         + [("vi", f) for f in range(2)] + [("mq", k, f) for k in range(ND) for f in range(2)] + [("mo", g) for g in range(4)])
LATE = ([("v", b, f) for b in range(1, NB) for f in range(2)] + [("k2", m, f) for m in range(ND) for f in range(2)]
        + [("v2", b) for b in range(NB)])
SETUP = EARLY + LATE
BANK = {name: n % 8 for n, name in enumerate(EARLY)} | {name: 4 + n % 4 for n, name in enumerate(LATE)}
BY_ACT = {name: n for n, name in enumerate([x for x in SETUP if x[0] in ("ki", "k", "v", "vi", "k2")])}
BY_DVE = {name: n for n, name in enumerate([x for x in SETUP if x not in BY_ACT])}
EARLY_ACT, EARLY_DVE = len([x for x in EARLY if x in BY_ACT]), len([x for x in EARLY if x in BY_DVE])
STAGED = [x for x in SETUP if x[0] in ("k", "v", "vi", "k2", "v2")]
SLOT = {name: n for n, name in enumerate(STAGED)}
EARLY_STAGED = len([x for x in STAGED if x in EARLY])
SLOTS = 4
OPENING = interleaved(SEGMENTS_A, [f"late{n}" for n in range(len(LATE))], OPENING_PAIRS)

LINKS_VEC = {"A": 26, "M": 26, "X": 12, "F": 11}
LINKS_ACT_M = 2
LOADS = (3, 9)


def decoder(nc, x, toep, ctxT, ctxiT, cols, rows, ident_in, sel24_in, sel96_in, sel48_in,
            wq, wk, wv, wo, qdT, kdT, vdT, odT, qu, ku, vu, ou, wki, wvi,
            rw, w1, w2, b2, win, wsk, wdbc, wd2, wout, wq2, wk2, wv2, wo2, nw, fw1, fw2, fb2, out):
    fp32, bf16, u32 = mybir.dt.float32, mybir.dt.bfloat16, mybir.dt.uint32
    ALU, ACT, AX = mybir.AluOpType, mybir.ActivationFunctionType, mybir.AxisListType

    k0_all = nc.dram_tensor("k0_all", (NB, M0 * P, KEYS), fp32).ap()
    v0_all = nc.dram_tensor("v0_all", (NB, KEYS, H0 * DH0), fp32).ap()
    k2_all = nc.dram_tensor("k2_all", (NB, D, KEYS), fp32).ap()
    v2_all = nc.dram_tensor("v2_all", (NB, KEYS, H1 * (DH1 + 1)), fp32).ap()

    ctx = ExitStack()
    with ctx:
        def sb(name, shape, dt=fp32, stack=ctx):
            return stack.enter_context(nc.sbuf_tensor(name, shape, dt))

        def sem(name):
            return ctx.enter_context(nc.semaphore(name))

        Wq = sb("Wq", [P, ND, 1024]); Wo = sb("Wo", [P, M0, D])
        W1 = sb("W1", [P, ND, 1024]); W2 = sb("W2", [P, EXPERTS, D]); B2 = sb("B2", [24, D])
        Rw = sb("Rw", [P, ND, EXPERTS])
        Win = sb("Win", [P, ND, DI]); Wsk = sb("Wsk", [P, ND, DI]); Wdbc = sb("Wdbc", [P, NM, 96])
        Wd2 = sb("Wd2", [DTR, DI]); Wout = sb("Wout", [P, NM, D])
        Wq2 = sb("Wq2", [P, ND, D]); Wo2 = sb("Wo2", [P, ND, D])
        Nw = sb("Nw", [P, ND, 3 * NODES])
        FW1 = sb("FW1", [P, ND, 1024]); FW2 = sb("FW2", [P, MF, D])
        FB2 = sb("FB2", [48, 3, D])
        Toep = sb("Toep", [P, 2, P]); ident = sb("ident", [P, P])
        Sel24 = sb("Sel24", [24, EXPERTS], bf16); Sel96 = sb("Sel96", [96, 32], bf16)
        Sel48 = sb("Sel48", [48, 3, MF, P], bf16)
        Cols = sb("Cols", [P, NCOLS]); Rows = sb("Rows", [P, NROWS])
        Aneg = sb("Aneg", [P, NM, NS]); half = sb("half", [P, 4]); lora = sb("lora", [P, 4])
        xin = sb("xin", [P, NT, D])

        def col(name, n):
            a = COLS[name][0] + n
            return Cols[:, a:a + 1]

        def row(name):
            return Rows[:, ROWS[name][0]:ROWS[name][1]]

        psA = ctx.enter_context(nc.psum_tensor("psA", [P, 4, 512], fp32))
        psB = ctx.enter_context(nc.psum_tensor("psB", [P, 4, 512], fp32))

        with ExitStack() as st:
            Wk = sb("Wk", [CH, 2, 1024], stack=st)
            Wki = sb("Wki", [CH, 2, 1024], stack=st); Wvi = sb("Wvi", [CH, 2, 1024], stack=st)
            Ci = sb("Ci", [CH, 2, NB * IPA], stack=st)
            Up = sb("Up", [RANK, 3, 1024], stack=st); Ou = sb("Ou", [RANK, D], stack=st)
            Dn = sb("Dn", [RANK, 1024 + D + 2 * CTX], stack=st)
            Kip = sb("Kip", [P, M0, NB, IPA], stack=st)
        DnO, DnQ, DnK, DnV = 0, 1024, 1024 + D, 1024 + D + CTX

        x3 = sb("x3", [P, NT, D])
        x5 = sb("x5", [P, NT, D])
        x5r = sb("x5r", [P, NT, D])
        Kbd = sb("Kbd", [P, M0, 2 * KEYS]); V = sb("V", [KEYS, 1024])
        Kbd2 = sb("Kbd2", [P, ND, 8, KEYS]); V2 = sb("V2", [KEYS, H1, DH1 + 1])
        Uin = sb("Uin", [P, NM, KC - 1 + T])
        dA = sb("dA", [P, 2, NM, T])
        st = ctx
        if True:
            r = sb("r", [P, NT, D], stack=st)
            x1 = sb("x1", [P, NT, D], stack=st); x1b = sb("x1b", [P, NT, D], stack=st)
            x1T = sb("x1T", [P, ND, T], stack=st)
            qT = sb("qT", [P, M0, T], stack=st)
            Pr = sb("Pr", [P, NT, H0, KEYS], stack=st)
            PT = sb("PT", [KEYS, H0, P], stack=st)
            mx = sb("mx", [P, NT, 2, H0], stack=st); den = sb("den", [P, NT, 2, H0], stack=st)
            rden = sb("rden", [P, NT, 2, H0], stack=st)
            bn = sb("bn", [P, NT, 6], stack=st); mv = sb("mv", [P, NT, 2], stack=st)
            var_A = sb("var_A", [P, NT], stack=st); rstd_A = sb("rstd_A", [P, NT], stack=st)
            lg = sb("lg", [P, NT, EXPERTS], stack=st); lx = sb("lx", [P, NT], stack=st)
            pe_ = sb("pe_", [P, NT, EXPERTS], stack=st); top = sb("top", [P, NT, 8], stack=st)
            tix = sb("tix", [P, NT, 8], u32, stack=st); tif = sb("tif", [P, NT, 2], stack=st)
            tw = sb("tw", [P, NT, 2], stack=st); ts = sb("ts", [P, NT], stack=st); tr = sb("tr", [P, NT], stack=st)
            mk = sb("mk", [P, NT, 2, EXPERTS], stack=st); mask = sb("mask", [P, NT, EXPERTS], stack=st)
            mhi = sb("mhi", [P, NT, 2, EXPERTS], bf16, stack=st); mr = sb("mr", [P, NT, EXPERTS], stack=st)
            m3 = sb("m3", [P, NT, 3, EXPERTS], stack=st)
            mT = sb("mT", [24, T], stack=st); mTb = sb("mTb", [24, T], bf16, stack=st)
            x2 = x1b
            x2T = x1T
            OT = qT
            x4T, x4b, q2T, o2T = x1T, x1b, qT[:, 0:ND], qT[:, ND:2 * ND]
            Pr2, PT2 = Pr, PT
            o2 = x1[:].rearrange("p t (h d) -> p t h d", d=DH1)
            mx2 = sb("mx2", [P, NT, H1], stack=st); rd2 = sb("rd2", [P, NT, H1], stack=st)
            hT = Pr[:].rearrange("p t h j -> p (t h j)")[:, 0:EXPERTS * T].rearrange("p (e t) -> p e t", t=T)
        if True:
            rB = sb("rB", [P, NT, D], stack=st)
            xrT = sb("xrT", [P, ND, T], stack=st)
            bnB = sb("bnB", [P, NT, 6], stack=st); mvB = sb("mvB", [P, NT, 2], stack=st)
            var_B = sb("var_B", [P, NT], stack=st); rstd_B = sb("rstd_B", [P, NT], stack=st)
            ssq = sb("ssq", [P, NT], stack=st)
            x4 = sb("x4", [P, NT, D], stack=st)
            x6 = rB
            with ExitStack() as late:
                Wv = sb("Wv", [CH, 2, 1024], stack=late); Ct = sb("Ct", [CH, 2, NB * KEYS], stack=late)
                Wk2 = sb("Wk2", [CH, 2, D], stack=late); Wv2 = sb("Wv2", [CH, 2, D], stack=late)
                Stage = sb("Stage", [P, SLOTS, 512], stack=late)
                V2s = sb("V2s", [KEYS, 2, H1, DH1 + 1], stack=late)
            with ExitStack() as mm:
                xs = sb("xs", [P, NM, T], stack=mm)
                bc3 = sb("bc3", [96, T], bf16, stack=mm)
                dt_ = sb("dt_", [P, NM, T], stack=mm); dtx = sb("dtx", [P, NM, T], stack=mm)
                hs = sb("hs", [P, 3, NM, T], stack=mm)
                acc = sb("acc", [P, NM, T], stack=mm)
                xr = acc[:, 0:NT]
                sq = xr
                gate = sb("gate", [P, NM, T], stack=mm)
                bcr, dbc = hs[0:64, 0, 0], hs[0:DTR, 2, 0]
                sp = hs[:, 1]
                yT = hs[:, 1]
            x5T = xrT
            with ExitStack() as mm:
                sc = sb("sc", [P, NT * 3, NODES], stack=mm); dec = sb("dec", [P, NT * 3, NODES], stack=mm)
                lv = [sb(f"lv{n}", [P, NT * 3, 2 ** (n + 1)], stack=mm) for n in range(4)]
                selT = sb("selT", [48, T], stack=mm); nsel = sb("nsel", [48, T], bf16, stack=mm)
                hid = sb("hid", [P, MF, T], stack=mm)
                qk3 = sb("qk3", [P, 2, ND, T], stack=mm); v3 = sb("v3", [P, NT, D], stack=mm)
                P3 = sb("P3", [P, NT, T], stack=mm); P3T = sb("P3T", [P, NT, T], stack=mm)
                mx3 = sb("mx3", [P, NT], stack=mm); nm3 = sb("nm3", [P, NT], stack=mm)
                den3 = sb("den3", [P, NT], stack=mm); rd3 = sb("rd3", [P, NT], stack=mm)

        weights_loaded = sem("weights_loaded"); setup_loaded = {s: sem(f"{s}_loaded") for s in ("lora", "keys", "values", "second")}
        setup_full = sem("setup_full"); setup_act = sem("setup_act"); setup_dve = sem("setup_dve")
        setup_pool = sem("setup_pool"); setup_init = sem("setup_init")
        slot_stored = [sem(f"slot_stored{s}") for s in range(SLOTS)]
        v2_stored = [sem(f"v2_stored{s}") for s in range(2)]
        x_loaded = sem("x_loaded"); kv_loaded = sem("kv_loaded"); kv2_loaded = sem("kv2_loaded")
        out_stored = sem("out_stored")
        full_A = sem("full_A"); full_B = sem("full_B")
        free_A = [sem(f"free_A{b}") for b in range(4)]
        free_B = [sem(f"free_B{b}") for b in range(4)]
        links_vec = {part: sem(f"links_vec_{part}") for part in LINKS_VEC}; links_act_M = sem("links_act_M")
        setup_vec = sem("setup_vec"); a_exp = sem("a_exp")
        fw1_loaded = sem("fw1_loaded"); fw2_loaded = sem("fw2_loaded")
        var_ready = {part: sem(f"var_ready_{part}") for part in "AMXF"}
        rstd_ready = {part: sem(f"rstd_ready_{part}") for part in "AMXF"}
        x1_ready = sem("x1_ready"); x1b_ready = sem("x1b_ready")
        exp_done = sem("exp_done"); den_ready = sem("den_ready"); probs_ready = sem("probs_ready")
        x2_ready = sem("x2_ready"); logits_ready = sem("logits_ready"); gates_exp = sem("gates_exp")
        mask_ready = sem("mask_ready"); x3_ready = sem("x3_ready")
        sq_done = sem("sq_done"); xr_ready = sem("xr_ready"); conv_ready = sem("conv_ready")
        xs_ready = sem("xs_ready"); dbc_ready = sem("dbc_ready"); bc_hi = sem("bc_hi"); bc3_ready = sem("bc3_ready")
        dt_act = sem("dt_act"); dt_ready = sem("dt_ready"); dA_ready = sem("dA_ready")
        scan_done = sem("scan_done"); added = sem("added"); acc_ready = sem("acc_ready"); yT_ready = sem("yT_ready")
        x4_ready = sem("x4_ready"); x4b_ready = sem("x4b_ready"); exp2_done = sem("exp2_done")
        alone_vec = sem("alone_vec"); alone_pe = sem("alone_pe")
        x5_ready = sem("x5_ready"); x5r_ready = sem("x5r_ready"); sel_ready = sem("sel_ready"); selT_ready = sem("selT_ready")
        mx3_ready = sem("mx3_ready"); x6_ready = sem("x6_ready")

        def bA(name):
            return psA[:, RING_A.bank[name], :]

        def bB(name):
            return psB[:, RING_B.bank[name], :]

        weights = [
            (ident[:], ident_in),
            (Toep[:], toep.rearrange("k p t -> p k t")),
            (Wq[:], wq.rearrange("(k p) n -> p k n", p=P)), (Wo[:], wo.rearrange("(m p) n -> p m n", p=P)),
            (W1[:], w1.rearrange("(k p) n -> p k n", p=P)), (W2[:], w2.rearrange("e f n -> f e n")),
            (B2[:], b2), (Rw[:], rw.rearrange("(k p) n -> p k n", p=P)),
            (Win[:], win.rearrange("(k p) n -> p k n", p=P)), (Wsk[:], wsk.rearrange("(k p) n -> p k n", p=P)),
            (Wdbc[:], wdbc.rearrange("(k p) n -> p k n", p=P)), (Wd2[:], wd2),
            (Wout[:], wout.rearrange("(k p) n -> p k n", p=P)),
            (Wq2[:], wq2.rearrange("(k p) n -> p k n", p=P)), (Wo2[:], wo2.rearrange("(k p) n -> p k n", p=P)),
            (Nw[:], nw.rearrange("(k p) n -> p k n", p=P)),
            (FB2[:], fb2.rearrange("j r n -> r j n")),
            (Sel24[:], sel24_in), (Sel96[:], sel96_in), (Sel48[:], sel48_in),
            (Dn[:, DnO:DnQ], odT), (Dn[:, DnQ:DnK], qdT), (Up[:, 0], qu), (Ou[:], ou),
        ]
        N_WEIGHTS = len(weights)
        setup_loads = {
            "lora": [(Cols[:], cols), (Dn[:, DnK:DnV], kdT), (Dn[:, DnV:DnV + CTX], vdT), (Up[:, 1], ku), (Up[:, 2], vu)],
            "keys": [(Ci[:], ctxiT.rearrange("(c p) n -> p c n", p=CH)), (Wki[:], wki.rearrange("(c p) n -> p c n", p=CH)),
                     (Wk[:], wk.rearrange("(c p) n -> p c n", p=CH)), (Ct[:], ctxT.rearrange("(c p) n -> p c n", p=CH))],
            "values": [(Wv[:], wv.rearrange("(c p) n -> p c n", p=CH)), (Wvi[:], wvi.rearrange("(c p) n -> p c n", p=CH))],
            "second": [(Rows[:], rows), (Wk2[:], wk2.rearrange("(c p) n -> p c n", p=CH)),
                       (Wv2[:], wv2.rearrange("(c p) n -> p c n", p=CH))],
        }

        block = ctx.enter_context(nc.Block())

        def stored_by(n, s):
            return sum(16 * (NB if name[0] == "vi" else 1) for name in STAGED[:n]
                       if name[0] != "v2" and SLOT[name] % SLOTS == s)

        @block.sync
        def _(sp):
            def load_x(b):
                src = x[bass.ts(b, 1)] if not isinstance(b, int) else x[b:b + 1]
                sp.dma_start(xin[:], src.rearrange("o (t p) d -> p (o t) d", p=P)).then_inc(x_loaded, 16)

            def load_kv(b):
                k = k0_all[bass.ts(b, 1)] if not isinstance(b, int) else k0_all[b:b + 1]
                v = v0_all[bass.ts(b, 1)] if not isinstance(b, int) else v0_all[b:b + 1]
                for e in range(2):
                    sp.dma_start(Kbd[64 * e:64 * e + 64, :, e * KEYS:(e + 1) * KEYS],
                                 k.rearrange("o (m e p) j -> e p (o m) j", e=2, p=64)[e]).then_inc(kv_loaded, 16)
                sp.dma_start(V[:], v.rearrange("o j n -> j (o n)")).then_inc(kv_loaded, 16)

            def load_kv2(b):
                k = k2_all[bass.ts(b, 1)] if not isinstance(b, int) else k2_all[b:b + 1]
                v = v2_all[bass.ts(b, 1)] if not isinstance(b, int) else v2_all[b:b + 1]
                kk = k.rearrange("o (m h p) j -> h p (o m) j", h=8, p=DH1)
                for h in range(8):
                    sp.dma_start(Kbd2[DH1 * h:DH1 * (h + 1), :, h, :], kk[h]).then_inc(kv2_loaded, 16)
                sp.dma_start(V2[:].rearrange("j h d -> j (h d)"), v.rearrange("o j n -> j (o n)")).then_inc(kv2_loaded, 16)

            def load_fw1(j):
                sp.dma_start(FW1[:], fw1[j].rearrange("(k p) n -> p k n", p=P)).then_inc(fw1_loaded, 16)

            def load_fw2(j):
                sp.dma_start(FW2[:], fw2[j].rearrange("(m p) n -> p m n", p=P)).then_inc(fw2_loaded, 16)

            def store(b):
                dst = out[bass.ts(b, 1)] if not isinstance(b, int) else out[b:b + 1]
                sp.dma_start(dst.rearrange("o (t p) d -> p (o t) d", p=P), x6[:]).then_inc(out_stored, 16)

            for s, loads in setup_loads.items():
                for dst, src in loads:
                    sp.dma_start(dst, src).then_inc(setup_loaded[s], 16)
            for dst, src in weights:
                sp.dma_start(dst, src).then_inc(weights_loaded, 16)
            load_x(0)
            load_fw1(0)
            load_fw2(0)
            def store_piece(name):
                s = SLOT[name] % SLOTS
                if name[0] == "v2":
                    b = name[1]
                    sp.wait_ge(setup_dve, BY_DVE[name] + 1)
                    sp.dma_start(v2_all[b], V2s[:, b % 2].rearrange("j h d -> j (h d)")).then_inc(v2_stored[b % 2], 16)
                    return
                sp.wait_ge(setup_act, BY_ACT[name] + 1)
                if name[0] == "k":
                    _, m, f = name
                    sp.dma_start(k0_all[4 * f:4 * f + 4, m * P:(m + 1) * P, :].rearrange("b p j -> p b j"),
                                 Stage[:, s, 0:4 * KEYS].rearrange("p (b j) -> p b j", j=KEYS)).then_inc(slot_stored[s], 16)
                elif name[0] == "v":
                    _, b, f = name
                    sp.dma_start(v0_all[b, 0:TEXT, f * 512:(f + 1) * 512], Stage[0:TEXT, s, :]).then_inc(slot_stored[s], 16)
                elif name[0] == "vi":
                    f = name[1]
                    for b in range(NB):
                        sp.dma_start(v0_all[b, TEXT:KEYS, f * 512:(f + 1) * 512],
                                     Stage[IPA * b:IPA * (b + 1), s, :]).then_inc(slot_stored[s], 16)
                else:
                    _, m, f = name
                    sp.dma_start(k2_all[4 * f:4 * f + 4, m * P:(m + 1) * P, :].rearrange("b p j -> p b j"),
                                 Stage[:, s, 0:4 * KEYS].rearrange("p (b j) -> p b j", j=KEYS)).then_inc(slot_stored[s], 16)

            for name in STAGED[:EARLY_STAGED]:
                store_piece(name)
            for s in range(SLOTS):
                sp.wait_ge(slot_stored[s], stored_by(EARLY_STAGED, s))
            sp.wait_ge(setup_init, 1)
            load_kv(0)
            for name in STAGED[EARLY_STAGED:]:
                store_piece(name)
            for s in range(SLOTS):
                sp.wait_ge(slot_stored[s], stored_by(len(SLOT), s))
            for s in range(2):
                sp.wait_ge(v2_stored[s], 16 * NB // 2)
            sp.wait_ge(setup_act, len(BY_ACT))
            sp.wait_ge(setup_dve, len(BY_DVE))
            load_kv2(0)

            def first_half(x1_there, nxt):
                sp.wait_ge(x1_ready, x1_there)
                load_x(nxt)

            def first_attention(o_taken, nxt):
                sp.wait_ge(free_A[RING_A.bank["O", 1, 1]], o_taken)
                load_kv(nxt)

            def second_attention(o2_taken, nxt):
                sp.wait_ge(free_A[RING_A.bank["o", 1]], o2_taken)
                load_kv2(nxt)

            def nets(hid_taken, out_taken, again):
                for j in range(3):
                    if j < 2 or again:
                        sp.wait_ge(free_B[RING_B.bank["hid", j, 3]], hid_taken[j])
                        load_fw1((j + 1) % 3)
                        sp.wait_ge(free_B[RING_B.bank["out", j, 0]], out_taken[j])
                        load_fw2((j + 1) % 3)

            def o_counts(a):
                return RING_A.turn(("O", 1, 1), a) + 1

            def rest_counts(b):
                return (RING_A.turn(("o", 1), b) + 1, [RING_B.turn(("hid", j, 3), b) + 1 for j in range(3)],
                        [RING_B.turn(("out", j, 0), b) + 1 for j in range(3)])

            for a in range(2):
                first_half(a + 1, a + 1)
                first_attention(o_counts(a), a + 1)
            second_attention(rest_counts(0)[0], 1)
            first_half(3, 3)
            first_attention(o_counts(2), 3)

            with sp.Fori(0, NB - 4) as b:
                nxt_b, nxt_a, x1_there, done = sp.snap(b + 2), sp.snap(b + 4), sp.snap(b + 4), sp.snap(b + 2)
                o_taken, o2_taken = sp.snap(o_counts(b + 3)), sp.snap(rest_counts(b + 1)[0])
                hid_taken, out_taken = [[sp.snap(v) for v in vs] for vs in rest_counts(b)[1:]]
                nets(hid_taken, out_taken, True)
                sp.wait_ge(x6_ready, done)
                store(b)
                second_attention(o2_taken, nxt_b)
                first_half(x1_there, nxt_a)
                first_attention(o_taken, nxt_a)
            for b in range(NB - 4, NB):
                _, hid_taken, out_taken = rest_counts(b)
                nets(hid_taken, out_taken, b < NB - 1)
                sp.wait_ge(x6_ready, b + 2)
                store(b)
                if b < NB - 2:
                    second_attention(rest_counts(b + 1)[0], b + 2)
            sp.wait_ge(out_stored, 16 * NB + 16)

        @block.gpsimd
        def _(po):
            for s in free_A + free_B:
                po.sem_inc(s, 1)
            po.sem_inc(out_stored, 16)
            po.sem_inc(x6_ready, 1)
            po.sem_inc(x3_ready, 1)
            nc.gpsimd.memset(half[:], -0.5).then_inc(setup_pool, 1)
            po.wait_ge(setup_pool, 1)
            nc.gpsimd.memset(V2s[:], 1.0).then_inc(setup_pool, 1)
            po.wait_ge(setup_act, EARLY_ACT)
            po.wait_ge(setup_dve, EARLY_DVE)
            nc.gpsimd.memset(Kbd[:], 0.0)
            nc.gpsimd.memset(Kbd2[:], 0.0)
            nc.gpsimd.memset(dA[:], 0.0)
            nc.gpsimd.memset(Uin[:], 0.0).then_inc(setup_init, 1)
            po.wait_ge(setup_init, 1)

            def rsqrt(part, n):
                v, d = (var_A, rstd_A) if part in "AX" else (var_B, rstd_B)
                po.wait_ge(var_ready[part], n + 1)
                nc.gpsimd.tensor_tensor(d[:], v[:], half[:, 0:NT], ALU.pow).then_inc(rstd_ready[part], 1)

            def pool_A(i):
                yield "conv"
                rsqrt("A", i * 3)
                yield "x1"
                po.wait_ge(x1_ready, i + 1)
                nc.gpsimd.tensor_tensor(x1b[:], x1[:], row("x0_bo").unsqueeze(1).broadcast_to([P, NT, D]), ALU.add)\
                    .then_inc(x1b_ready, 1)
                for t in range(NT):
                    yield f"norm{t}"
                    po.wait_ge(den_ready, i * NT + (t + 1))
                    nc.gpsimd.tensor_tensor(Pr[:, t, :, 0:TEXT], Pr[:, t, :, 0:TEXT],
                                            rden[:, t, 0, :].unsqueeze(2).broadcast_to([P, H0, TEXT]), ALU.mult)
                    nc.gpsimd.tensor_tensor(Pr[:, t, :, TEXT:KEYS], Pr[:, t, :, TEXT:KEYS],
                                            rden[:, t, 1, :].unsqueeze(2).broadcast_to([P, H0, IPA]), ALU.mult)\
                        .then_inc(probs_ready, 1)
                yield "y1"
                rsqrt("A", i * 3 + 1)
                yield "y2"
                rsqrt("A", i * 3 + 2)

            def pool_M(i):
                yield "rms"
                rsqrt("M", i * 2)
                yield "low rank"
                po.wait_ge(xs_ready, i * 2 + 2)
                wd = Cols[:, COLS["W_D"][0]:COLS["W_D"][1]].unsqueeze(2).broadcast_to([P, NM, T])
                nc.gpsimd.tensor_tensor(acc[:], xs[:], wd, ALU.mult).then_inc(acc_ready, 1)
                for n in range(NS):
                    yield f"add{n}"
                    if n == 0:
                        po.wait_ge(acc_ready, i + 1)
                    po.wait_ge(free_B[RING_B.bank["bc", n]], RING_B.turn(("bc", n), i) + 1)
                    for h in range(2):
                        if n:
                            po.wait_ge(added, i * 2 * NS + (2 * n + h - 1))
                        if h == 0 and n + 1 < NS:
                            po.wait_ge(scan_done, i * NS + (n + 2))
                        a2 = acc[:, 2 * h:2 * h + 2]
                        nc.gpsimd.tensor_tensor(a2, a2, hs[:, n % 3, 2 * h:2 * h + 2], ALU.add).then_inc(added, 1)
                yield "my"
                rsqrt("M", i * 2 + 1)

            def pool_X(i):
                yield "x4T"
                po.wait_ge(x4_ready, i + 1)
                nc.gpsimd.tensor_tensor(x4b[:], x4[:], row("x1_bo").unsqueeze(1).broadcast_to([P, NT, D]), ALU.add)\
                    .then_inc(x4b_ready, 1)
                yield "y3"
                rsqrt("X", i)

            def pool_F(i):
                yield "y4"
                rsqrt("F", i)

            po.wait_ge(setup_loaded["second"], 16 * len(setup_loads["second"]))
            write_out(SEGMENTS_A, pool_A(0))
            po.wait_ge(kv2_loaded, 16 * LOADS[1])
            write_out(FIRST, pool_A(1), pool_M(0))
            write_out(SECOND, pool_X(0), pool_A(2), pool_M(1))
            with po.Fori(0, NB - 3) as i:
                write_out(STEADY, pool_X(i + 1), pool_A(i + 3), pool_F(i), pool_M(i + 2))
            write_out(LAST + SEGMENTS_M, pool_X(NB - 2), pool_F(NB - 3), pool_M(NB - 1))
            write_out(LAST, pool_X(NB - 1), pool_F(NB - 2))
            write_out(SEGMENTS_F, pool_F(NB - 1))

        @block.scalar
        def _(act):
            act.wait_ge(setup_loaded["lora"], 16 * len(setup_loads["lora"]))
            a0, a1 = COLS["A_log"]
            nc.scalar.activation(Aneg[:], Cols[:, a0:a1].rearrange("p (m n) -> p m n", n=NS), ACT.Exp)\
                .then_inc(a_exp, 1)
            def take_out(name):
                s = SLOT.get(name, 0) % SLOTS
                ps = (psA if BANK[name] < 4 else psB)[:, BANK[name] % 4, :]
                act.wait_ge(setup_full, SETUP.index(name) + 1)
                if SLOT.get(name, 0) >= SLOTS:
                    act.wait_ge(slot_stored[s], stored_by(SLOT[name], s))
                if name[0] == "ki":
                    nc.scalar.activation(Kip[:], ps[:, 0:M0 * NB * IPA].rearrange("p (m b j) -> p m b j", m=M0, b=NB),
                                         ACT.Copy).then_inc(setup_act, 1)
                    act.wait_ge(setup_act, 1)
                elif name[0] == "k":
                    _, m, f = name
                    k = Stage[:, s, 0:480].rearrange("p (b j) -> p b j", j=KEYS)
                    nc.scalar.activation(k[:, :, 0:TEXT], ps[:, 0:480].rearrange("p (b j) -> p b j", j=KEYS)[:, :, 0:TEXT],
                                         ACT.Copy)
                    nc.scalar.activation(k[:, :, TEXT:KEYS], Kip[:, m, 4 * f:4 * f + 4], ACT.Copy).then_inc(setup_act, 1)
                elif name[0] == "v":
                    nc.scalar.activation(Stage[0:KEYS, s, :], ps[0:KEYS, :], ACT.Copy).then_inc(setup_act, 1)
                elif name[0] == "vi":
                    nc.scalar.activation(Stage[0:NB * IPA, s, :], ps[0:NB * IPA, :], ACT.Copy).then_inc(setup_act, 1)
                else:
                    nc.scalar.activation(Stage[:, s, 0:480], ps[:, 0:480], ACT.Identity,
                                         bias=col("x_bk", name[1])).then_inc(setup_act, 1)

            def late():
                for n, name in enumerate(LATE):
                    if name in BY_ACT:
                        yield f"late{n}"
                        take_out(name)

            for name in BY_ACT:
                if name in EARLY:
                    take_out(name)
            act.wait_ge(setup_init, 1)
            act.wait_ge(setup_vec, 1)

            def take_A(name, i):
                act.wait_ge(full_A, RING_A.filled(name, i))

            def take_B(name, i):
                act.wait_ge(full_B, RING_B.filled(name, i))

            def act_A(i):
                yield "x1T"
                take_A("x1T", i)
                nc.scalar.activation(x1T[:].rearrange("p k t -> p (k t)"), bA("x1T"), ACT.Copy)\
                    .then_inc(free_A[RING_A.bank["x1T"]], 1)
                for g in range(4):
                    yield f"q{g}"
                    take_A(("q", g), i)
                    nc.scalar.activation(qT[:, 2 * g:2 * g + 2, :].rearrange("p m t -> p (m t)"), bA(("q", g)), ACT.Copy)\
                        .then_inc(free_A[RING_A.bank["q", g]], 1)
                for t in range(NT):
                    yield f"S{t}3"
                    act.wait_ge(free_A[RING_A.bank["S", t, 3]], RING_A.turn(("S", t, 3), i) + 1)
                    nc.scalar.activation(Pr[:, t].rearrange("p h j -> p (h j)"), Pr[:, t].rearrange("p h j -> p (h j)"),
                                         ACT.Exp, scale=DH0 ** -0.5).then_inc(exp_done, 1)
                for t in range(NT):
                    yield f"PT{t}"
                    for g in range(4):
                        take_A(("PT", t, g), i)
                        nc.scalar.activation(PT[:, 4 * g:4 * g + 4],
                                             bA(("PT", t, g))[0:KEYS].rearrange("j (h t) -> j h t", t=P), ACT.Copy)\
                            .then_inc(free_A[RING_A.bank["PT", t, g]], 1)
                    yield f"O{t}"
                    for f in range(2):
                        take_A(("O", t, f), i)
                        nc.scalar.activation(OT[:, 4 * f:4 * f + 4, t * P:(t + 1) * P],
                                             bA(("O", t, f)).rearrange("p (m t) -> p m t", t=P), ACT.Copy)\
                            .then_inc(free_A[RING_A.bank["O", t, f]], 1)
                yield "x2T"
                take_A("x2T", i)
                nc.scalar.activation(x2T[:].rearrange("p k t -> p (k t)"), bA("x2T"), ACT.Copy)\
                    .then_inc(free_A[RING_A.bank["x2T"]], 1)
                yield "gates"
                act.wait_ge(logits_ready, i + 1)
                nc.scalar.activation(pe_[:], lg[:], ACT.Exp).then_inc(gates_exp, 1)
                yield "gelu"
                for g in range(4):
                    take_A(("h", g), i)
                    for e in (2 * g, 2 * g + 1):
                        last = nc.scalar.activation(hT[:, e, :], bA(("h", g))[:, (e % 2) * T:(e % 2 + 1) * T],
                                                    ACT.Gelu, bias=col("moe_b1", e))
                    last.then_inc(free_A[RING_A.bank["h", g]], 1)

            def act_M(i):
                c = 0

                def link(ins):
                    nonlocal c
                    c += 1
                    ins.then_inc(links_act_M, 1)
                    act.wait_ge(links_act_M, i * LINKS_ACT_M + c)

                yield "rms"
                act.wait_ge(x3_ready, i + 2)
                nc.scalar.activation(sq[:, 0], x3[:, 0], ACT.Square, accum_out=ssq[:, 0:1])
                nc.scalar.activation(sq[:, 1], x3[:, 1], ACT.Square, accum_out=ssq[:, 1:2]).then_inc(sq_done, 1)
                yield "xrT"
                take_B("xrT", i)
                nc.scalar.activation(xrT[:].rearrange("p k t -> p (k t)"), bB("xrT"), ACT.Copy)\
                    .then_inc(free_B[RING_B.bank["xrT"]], 1)
                yield "u"
                for g in range(2):
                    take_B(("u", g), i)
                    nc.scalar.activation(Uin[:, 2 * g:2 * g + 2, KC - 1:],
                                         bB(("u", g)).rearrange("p (m t) -> p m t", t=T), ACT.Copy)\
                        .then_inc(free_B[RING_B.bank["u", g]], 1)
                for g in range(2):
                    yield f"taps{g}"
                    act.wait_ge(conv_ready, i * 2 + (g + 1))
                    nc.scalar.activation(xs[:, 2 * g:2 * g + 2], xs[:, 2 * g:2 * g + 2], ACT.Silu).then_inc(xs_ready, 1)
                yield "gate"
                for g in range(2):
                    take_B(("skip", g), i)
                    nc.scalar.activation(gate[:, 2 * g:2 * g + 2, :].rearrange("p m t -> p (m t)"), bB(("skip", g)),
                                         ACT.Silu).then_inc(free_B[RING_B.bank["skip", g]], 1)
                yield "low rank"
                take_B("dbc", i)
                nc.scalar.activation(bc3[0:32], bB("dbc")[64:96, 0:T], ACT.Copy).then_inc(bc_hi, 1)
                act.wait_ge(bc_hi, i + 1)
                nc.scalar.activation(dbc, bB("dbc")[0:DTR, 0:T], ACT.Copy).then_inc(dbc_ready, 1)
                yield "delta"
                for m in range(NM):
                    if m % 2 == 0:
                        take_B(("z", m // 2), i)
                    ins = nc.scalar.activation(dt_[:, m], bB(("z", m // 2))[:, (m % 2) * T:(m % 2 + 1) * T],
                                               ACT.Identity, bias=col("wd2_b", m))
                    if m % 2:
                        ins.then_inc(free_B[RING_B.bank["z", m // 2]], 1)
                act.wait_ge(free_B[RING_B.bank["z", 1]], RING_B.turn(("z", 1), i) + 1)
                link(nc.scalar.activation(sp[:], dt_[:], ACT.Abs))
                link(nc.scalar.activation(sp[:], sp[:], ACT.Exp, scale=-1.0))
                nc.scalar.activation(sp[:], sp[:], ACT.Ln, bias=1.0).then_inc(dt_act, 1)
                act.wait_ge(dt_ready, i + 1)
                for n in range(NS):
                    yield f"state{n}"
                    if n >= 2:
                        act.wait_ge(scan_done, i * NS + (n - 1))
                    for m in range(NM):
                        last = nc.scalar.activation(dA[:, n % 2, m, 1:T], dt_[:, m, 1:T], ACT.Exp,
                                                    scale=Aneg[:, m, n:n + 1])
                    last.then_inc(dA_ready, 1)
                assert c == LINKS_ACT_M, c

            def act_X(i):
                yield "x4T"
                take_A("x4T", i)
                nc.scalar.activation(x4T[:].rearrange("p k t -> p (k t)"), bA("x4T"), ACT.Copy)\
                    .then_inc(free_A[RING_A.bank["x4T"]], 1)
                yield "qx"
                take_A("q2", i)
                for m in range(ND):
                    last = nc.scalar.activation(q2T[:, m], bA("q2")[:, m * T:(m + 1) * T], ACT.Identity,
                                                bias=col("x_bq", m))
                last.then_inc(free_A[RING_A.bank["q2"]], 1)
                for t in range(NT):
                    yield f"T{t}3"
                    act.wait_ge(free_A[RING_A.bank["S2", t, 3]], RING_A.turn(("S2", t, 3), i) + 1)
                    nc.scalar.activation(Pr2[:, t].rearrange("p h j -> p (h j)"), Pr2[:, t].rearrange("p h j -> p (h j)"),
                                         ACT.Exp, scale=DH1 ** -0.5).then_inc(exp2_done, 1)
                for t in range(NT):
                    yield f"QT{t}"
                    if t:
                        take_A(("o", t - 1), i)
                    for g in range(4):
                        take_A(("PT2", t, g), i)
                        nc.scalar.activation(PT2[:, 4 * g:4 * g + 4],
                                             bA(("PT2", t, g))[0:KEYS].rearrange("j (h t) -> j h t", t=P), ACT.Copy)\
                            .then_inc(free_A[RING_A.bank["PT2", t, g]], 1)
                yield "oT"
                take_A("oT", i)
                nc.scalar.activation(o2T[:].rearrange("p k t -> p (k t)"), bA("oT"), ACT.Copy)\
                    .then_inc(free_A[RING_A.bank["oT"]], 1)

            def act_F(i):
                yield "x5T"
                act.wait_ge(x5_ready, i + 1)
                if not isinstance(i, int) or i > 0:
                    act.wait_ge(x6_ready, i + 1)
                nc.scalar.activation(x5r[:], x5[:], ACT.Copy).then_inc(x5r_ready, 1)
                take_B("x5T", i)
                nc.scalar.activation(x5T[:].rearrange("p k t -> p (k t)"), bB("x5T"), ACT.Copy)\
                    .then_inc(free_B[RING_B.bank["x5T"]], 1)
                yield "selT"
                take_B("selT", i)
                nc.scalar.activation(selT[:], bB("selT")[0:48, 0:T], ACT.Copy).then_inc(selT_ready, 1)
                for j in range(3):
                    for g in (0, 2):
                        yield f"net{j}{g}"
                        take_B(("hid", j, g), i)
                        for m in (2 * g, 2 * g + 1):
                            last = nc.scalar.activation(hid[:, m], bB(("hid", j, g))[:, (m % 2) * T:(m % 2 + 1) * T],
                                                        ACT.Relu, bias=col("f_b1", MF * j + m))
                        last.then_inc(free_B[RING_B.bank["hid", j, g]], 1)
                    yield f"out{j}"
                    take_B(("out", j, 0), i)
                    dst = qk3[:, j].rearrange("p k t -> p (k t)") if j < 2 else v3[:].rearrange("p t d -> p (t d)")
                    nc.scalar.activation(dst, bB(("out", j, 0)), ACT.Copy).then_inc(free_B[RING_B.bank["out", j, 0]], 1)
                yield "S3"
                act.wait_ge(mx3_ready, i + 1)
                for t in range(NT):
                    last = nc.scalar.activation(P3[:, t], bB("S3")[:, t * T:(t + 1) * T], ACT.Exp, bias=nm3[:, t:t + 1],
                                                scale=D ** -0.5, accum_out=den3[:, t:t + 1])
                last.then_inc(free_B[RING_B.bank["S3"]], 1)
                yield "P3"
                take_B("P3T", i)
                nc.scalar.activation(P3T[:].rearrange("p k t -> p (k t)"), bB("P3T"), ACT.Copy)\
                    .then_inc(free_B[RING_B.bank["P3T"]], 1)

            write_out(OPENING, act_A(0), late())
            act.wait_ge(kv2_loaded, 16 * LOADS[1])
            write_out(FIRST, act_A(1), act_M(0))
            write_out(SECOND, act_X(0), act_A(2), act_M(1))
            with act.Fori(0, NB - 3) as i:
                write_out(STEADY, act_X(i + 1), act_A(i + 3), act_F(i), act_M(i + 2))
            write_out(LAST + SEGMENTS_M, act_X(NB - 2), act_F(NB - 3), act_M(NB - 1))
            write_out(LAST, act_X(NB - 1), act_F(NB - 2))
            write_out(SEGMENTS_F, act_F(NB - 1))

        @block.vector
        def _(dve):
            vec = nc.vector

            dve.wait_ge(setup_loaded["lora"], 16 * len(setup_loads["lora"]))
            vec.tensor_scalar(lora[:], Cols[:, COLS["alpha"][0]:COLS["alpha"][1]], 1.0 / RANK, None, ALU.mult)\
                .then_inc(setup_vec, 1)
            dve.wait_ge(setup_vec, 1)
            merged = {"mq": (0, Wq), "mk": (1, Wk), "mv": (2, Wv), "mo": (3, Wo)}

            def take_out(name):
                ps = (psA if BANK[name] < 4 else psB)[:, BANK[name] % 4, :]
                dve.wait_ge(setup_full, SETUP.index(name) + 1)
                kind, f = name[0], name[-1]
                if name in (("mk", 0, 0), ("mv", 0, 0), ("v2", 0)):
                    s = {"mk": "keys", "mv": "values", "v2": "second"}[kind]
                    dve.wait_ge(setup_loaded[s], 16 * len(setup_loads[s]))
                elif name == ("mq", 0, 0):
                    dve.wait_ge(weights_loaded, 16 * N_WEIGHTS)
                if kind == "v2":
                    if f == 0:
                        dve.wait_ge(setup_pool, 2)
                    if f >= 2:
                        dve.wait_ge(v2_stored[f % 2], 16 * (f // 2))
                    vec.tensor_tensor(V2s[:, f % 2, :, 0:DH1], ps[0:KEYS, 0:D].rearrange("j (h d) -> j h d", d=DH1),
                                      row("x1_bv")[0:KEYS].rearrange("j (h d) -> j h d", d=DH1), ALU.add)\
                        .then_inc(setup_dve, 1)
                    return
                n, W = merged[kind]
                if kind == "mo":
                    w = W[:, 2 * f:2 * f + 2, :].rearrange("p m n -> p (m n)")
                else:
                    w = W[:, name[1], f * 512:(f + 1) * 512]
                h = CH if kind in ("mk", "mv") else P
                vec.scalar_tensor_tensor(w, ps[0:h], lora[0:h, n:n + 1], w, ALU.mult, ALU.add).then_inc(setup_dve, 1)

            def late():
                for n, name in enumerate(LATE):
                    if name in BY_DVE:
                        yield f"late{n}"
                        take_out(name)

            for name in BY_DVE:
                if name in EARLY:
                    take_out(name)
            for W in (Win, Wsk):
                for k in range(ND):
                    vec.tensor_scalar(W[:, k], W[:, k], col("norm_w", k), None, ALU.mult)
            dve.wait_ge(a_exp, 1)
            vec.tensor_scalar(Aneg[:], Aneg[:], -1.0, None, ALU.mult).then_inc(setup_vec, 1)
            dve.wait_ge(setup_init, 1)

            def tools(part, i):
                if part in "AX":
                    full, free, ring, rows_, bns, mvs, variance, rstd = full_A, free_A, RING_A, r, bn, mv, var_A, rstd_A
                else:
                    full, free, ring, rows_, bns, mvs, variance, rstd = full_B, free_B, RING_B, rB, bnB, mvB, var_B, rstd_B
                c = 0

                def link(ins):
                    nonlocal c
                    c += 1
                    ins.then_inc(links_vec[part], 1)
                    dve.wait_ge(links_vec[part], i * LINKS_VEC[part] + c)

                def take(name):
                    dve.wait_ge(full, ring.filled(name, i))

                def give(ins, name):
                    ins.then_inc(free[ring.bank[name]], 1)

                def given(name):
                    dve.wait_ge(free[ring.bank[name]], ring.turn(name, i) + 1)

                def statistics():
                    for t in range(NT):
                        last = vec.bn_stats(bns[:, t], rows_[:, t])
                    link(last)
                    dve.sem_inc(alone_vec, 1)
                    for t in range(NT):
                        last = vec.bn_aggr(mvs[:, t], bns[:, t])
                    link(last)
                    vec.tensor_scalar(variance[:], mvs[:, :, 1], EPS, None, ALU.add).then_inc(var_ready[part], 1)

                def scale(n, dst, ready):
                    dve.wait_ge(rstd_ready[part], n)
                    for t in range(NT):
                        last = vec.tensor_scalar(dst[:, t], rows_[:, t], mvs[:, t, 0:1], rstd[:, t:t + 1],
                                                 ALU.subtract, ALU.mult)
                    last.then_inc(ready, 1)

                return link, lambda: c, take, give, given, statistics, scale

            def dve_A(i):
                link, linked, take, give, given, statistics, scale = tools("A", i)
                yield "conv"
                dve.wait_ge(x3_ready, i + 1)
                if not isinstance(i, int) or i > 1:
                    dve.wait_ge(x5_ready, i - 1)
                take("conv")
                give(vec.tensor_tensor(r[:].rearrange("p t d -> p (t d)"), bA("conv"),
                                       xin[:].rearrange("p t d -> p (t d)"), ALU.add), "conv")
                given("conv")
                statistics()
                yield "x1"
                scale(i * 3 + 1, x1, x1_ready)
                def normalisers(t):
                    dve.wait_ge(exp_done, i * NT + (t + 1))
                    vec.tensor_reduce(den[:, t, 0], Pr[:, t, :, 0:TEXT], AX.X, ALU.add)
                    link(vec.tensor_reduce(den[:, t, 1], Pr[:, t, :, TEXT:KEYS], AX.X, ALU.add))
                    vec.reciprocal(rden[:, t], den[:, t]).then_inc(den_ready, 1)

                for t, g in TILES:
                    if (t, g) == (1, 1):
                        yield "norm0"
                        normalisers(0)
                    yield f"S{t}{g}"
                    take(("S", t, g))
                    hs4 = slice(4 * g, 4 * g + 4)
                    s4 = bA(("S", t, g))[:, 0:4 * KEYS].rearrange("p (h j) -> p h j", j=KEYS)
                    vec.tensor_reduce(mx[:, t, 0, hs4], s4[:, :, 0:TEXT], AX.X, ALU.max)
                    link(vec.tensor_reduce(mx[:, t, 1, hs4], s4[:, :, TEXT:KEYS], AX.X, ALU.max))
                    vec.tensor_tensor(Pr[:, t, hs4, 0:TEXT], s4[:, :, 0:TEXT],
                                      mx[:, t, 0, hs4].unsqueeze(2).broadcast_to([P, 4, TEXT]), ALU.subtract)
                    give(vec.tensor_tensor(Pr[:, t, hs4, TEXT:KEYS], s4[:, :, TEXT:KEYS],
                                           mx[:, t, 1, hs4].unsqueeze(2).broadcast_to([P, 4, IPA]), ALU.subtract),
                         ("S", t, g))
                yield "norm1"
                normalisers(1)
                yield "y1"
                take("y1")
                dve.wait_ge(x1b_ready, i + 1)
                give(vec.tensor_tensor(r[:].rearrange("p t d -> p (t d)"), bA("y1"),
                                       x1b[:].rearrange("p t d -> p (t d)"), ALU.add), "y1")
                given("y1")
                statistics()
                yield "x2"
                scale(i * 3 + 2, x2, x2_ready)
                yield "router"
                take("router")
                give(vec.tensor_tensor(lg[:], bA("router")[:, 0:NT * EXPERTS].rearrange("p (t e) -> p t e", e=EXPERTS),
                                       row("router_b").unsqueeze(1).broadcast_to([P, NT, EXPERTS]), ALU.add), "router")
                given("router")
                link(vec.tensor_reduce(lx[:], lg[:], AX.X, ALU.max))
                vec.tensor_tensor(lg[:], lg[:], lx[:].unsqueeze(2).broadcast_to([P, NT, EXPERTS]), ALU.subtract)\
                    .then_inc(logits_ready, 1)
                yield "gates"
                dve.wait_ge(gates_exp, i + 1)
                dve.sem_inc(alone_vec, 1)
                for t in range(NT):
                    last = vec.max(top[:, t], pe_[:, t])
                link(last)
                dve.sem_inc(alone_vec, 1)
                for t in range(NT):
                    vec.max_index(tix[:, t], top[:, t], pe_[:, t])
                link(vec.tensor_tensor(ts[:], top[:, :, 0], top[:, :, 1], ALU.add))
                vec.tensor_copy(tif[:], tix[:, :, 0:2])
                link(vec.reciprocal(tr[:], ts[:]))
                link(vec.tensor_tensor(tw[:], top[:, :, 0:2], tr[:].unsqueeze(2).broadcast_to([P, NT, 2]), ALU.mult))
                for t in range(NT):
                    for s in range(2):
                        last = vec.tensor_scalar(mk[:, t, s], row("iota"), tif[:, t, s:s + 1], tw[:, t, s:s + 1],
                                                 ALU.is_equal, ALU.mult)
                link(last)
                link(vec.tensor_tensor(mask[:], mk[:, :, 0], mk[:, :, 1], ALU.add))
                link(vec.tensor_copy(mhi[:, :, 0], mask[:]))
                vec.tensor_copy(m3[:, :, 0], mhi[:, :, 0])
                link(vec.tensor_tensor(mr[:], mask[:], mhi[:, :, 0], ALU.subtract))
                link(vec.tensor_copy(mhi[:, :, 1], mr[:]))
                vec.tensor_copy(m3[:, :, 1], mhi[:, :, 1])
                vec.tensor_tensor(m3[:, :, 2], mr[:], mhi[:, :, 1], ALU.subtract).then_inc(mask_ready, 1)
                yield "maskT"
                take("maskT")
                vec.tensor_copy(mT[:], bA("maskT")[0:24, 0:T])
                give(vec.tensor_copy(mTb[:], bA("maskT")[0:24, 0:T]), "maskT")
                for g in range(4):
                    yield f"mb{g}"
                    given(("h", g))
                    take(("mb", g))
                    h2 = hT[:, 2 * g:2 * g + 2, :].rearrange("p e t -> p (e t)")
                    give(vec.tensor_tensor(h2, h2, bA(("mb", g)), ALU.mult), ("mb", g))
                yield "y2"
                take("y2")
                give(vec.tensor_tensor(r[:].rearrange("p t d -> p (t d)"), bA("y2"),
                                       x2[:].rearrange("p t d -> p (t d)"), ALU.add), "y2")
                given("y2")
                statistics()
                yield "x3"
                scale(i * 3 + 3, x3, x3_ready)
                assert linked() == LINKS_VEC["A"], linked()

            def dve_M(i):
                link, linked, take, give, given, statistics, scale = tools("M", i)
                yield "rms"
                if not isinstance(i, int) or i > 0:
                    dve.wait_ge(x6_ready, i)
                dve.wait_ge(x3_ready, i + 2)
                dve.wait_ge(sq_done, i + 1)
                vec.tensor_scalar(var_B[:], ssq[:], 1.0 / D, EPS, ALU.mult, ALU.add).then_inc(var_ready["M"], 1)
                yield "xr"
                dve.wait_ge(rstd_ready["M"], i * 2 + 1)
                for t in range(NT):
                    last = vec.tensor_scalar(xr[:, t], x3[:, t], rstd_B[:, t:t + 1], None, ALU.mult)
                last.then_inc(xr_ready, 1)
                for g in range(2):
                    yield f"taps{g}"
                    given(("u", g))
                    ms = (2 * g, 2 * g + 1)
                    for m in ms:
                        last = vec.tensor_scalar(xs[:, m], Uin[:, m, 0:T], col("conv_w", KC * m), col("conv_b", m),
                                                 ALU.mult, ALU.add)
                    link(last)
                    for k in range(1, KC):
                        for m in ms:
                            last = vec.scalar_tensor_tensor(xs[:, m], Uin[:, m, k:k + T], col("conv_w", KC * m + k),
                                                            xs[:, m], ALU.mult, ALU.add)
                        if k < KC - 1:
                            link(last)
                    last.then_inc(conv_ready, 1)
                yield "low rank"
                dve.wait_ge(dbc_ready, i + 1)
                give(vec.tensor_tensor(bcr[32:64], bB("dbc")[64:96, 0:T], bc3[0:32], ALU.subtract), "dbc")
                given("dbc")
                link(vec.tensor_copy(bc3[32:64], bcr[32:64]))
                vec.tensor_tensor(bc3[64:96], bcr[32:64], bc3[32:64], ALU.subtract).then_inc(bc3_ready, 1)
                yield "dtx"
                dve.wait_ge(dt_act, i + 1)
                vec.scalar_tensor_tensor(dt_[:].rearrange("p m t -> p (m t)"), dt_[:].rearrange("p m t -> p (m t)"), 0.0,
                                         sp[:].rearrange("p m t -> p (m t)"), ALU.max, ALU.add).then_inc(dt_ready, 1)
                dve.wait_ge(dt_ready, i + 1)
                link(vec.tensor_tensor(dtx[:], dt_[:], xs[:], ALU.mult))

                def bc(n):
                    return bB(("bc", n)).rearrange("p (s t) -> p s t", s=2)

                def states_input(n):
                    take(("bc", n))
                    if n >= 3:
                        dve.wait_ge(added, i * 2 * NS + 2 * (n - 2))
                    link(vec.tensor_tensor(hs[:, n % 3], dtx[:], bc(n)[:, 0:1, :].broadcast_to([P, NM, T]), ALU.mult))

                states_input(0)
                for n in range(NS):
                    yield f"state{n}"
                    h = hs[:, n % 3]
                    dve.wait_ge(dA_ready, i * NS + (n + 1))
                    h1 = h.rearrange("p m t -> p (m t)")
                    vec.tensor_tensor_scan(h1, dA[:, n % 2].rearrange("p m t -> p (m t)"), h1, 0.0, ALU.mult, ALU.add)\
                        .then_inc(scan_done, 1)
                    if n + 1 < NS:
                        states_input(n + 1)
                    dve.wait_ge(scan_done, i * NS + (n + 1))
                    give(vec.tensor_tensor(h, h, bc(n)[:, 1:2, :].broadcast_to([P, NM, T]), ALU.mult), ("bc", n))
                yield "y"
                dve.wait_ge(free_B[RING_B.bank["skip", 1]], RING_B.turn(("skip", 1), i) + 1)
                dve.wait_ge(added, (i + 1) * 2 * NS)
                vec.tensor_tensor(yT, acc[:], gate[:], ALU.mult).then_inc(yT_ready, 1)
                yield "my"
                take("my")
                if not isinstance(i, int) or i > 0:
                    dve.wait_ge(out_stored, i * 16)
                give(vec.scalar_tensor_tensor(rB[:].rearrange("p t d -> p (t d)"), x3[:].rearrange("p t d -> p (t d)"),
                                              2.0, bB("my"), ALU.mult, ALU.add), "my")
                given("my")
                statistics()
                yield "x4"
                scale(i * 2 + 2, x4, x4_ready)
                assert linked() == LINKS_VEC["M"], linked()

            def dve_X(i):
                link, linked, take, give, given, statistics, scale = tools("X", i)
                for t, g in TILES:
                    yield f"T{t}{g}"
                    take(("S2", t, g))
                    hs4 = slice(4 * g, 4 * g + 4)
                    s4 = bA(("S2", t, g))[:, 0:4 * KEYS].rearrange("p (h j) -> p h j", j=KEYS)
                    link(vec.tensor_reduce(mx2[:, t, hs4], s4, AX.X, ALU.max))
                    give(vec.tensor_tensor(Pr2[:, t, hs4], s4, mx2[:, t, hs4].unsqueeze(2).broadcast_to([P, 4, KEYS]),
                                           ALU.subtract), ("S2", t, g))
                for t in range(NT):
                    yield f"o{t}"
                    take(("o", t))
                    o = bA(("o", t))[:, 0:H1 * (DH1 + 1)].rearrange("p (h d) -> p h d", d=DH1 + 1)
                    link(vec.reciprocal(rd2[:, t], o[:, :, DH1]))
                    give(vec.tensor_tensor(o2[:, t], o[:, :, 0:DH1], rd2[:, t].unsqueeze(2).broadcast_to([P, H1, DH1]),
                                           ALU.mult), ("o", t))
                yield "y3"
                take("y3")
                dve.wait_ge(x4b_ready, i + 1)
                give(vec.tensor_tensor(r[:].rearrange("p t d -> p (t d)"), bA("y3"),
                                       x4b[:].rearrange("p t d -> p (t d)"), ALU.add), "y3")
                given("y3")
                statistics()
                yield "x5"
                if not isinstance(i, int) or i > 0:
                    dve.wait_ge(x5r_ready, i)
                scale(i + 1, x5, x5_ready)
                assert linked() == LINKS_VEC["X"], linked()

            def dve_F(i):
                link, linked, take, give, given, statistics, scale = tools("F", i)
                yield "node"
                take("node")
                give(vec.tensor_tensor(sc[:].rearrange("p (t j) n -> p t (j n)", t=NT),
                                       bB("node")[:, 0:NT * 3 * NODES].rearrange("p (t n) -> p t n", t=NT),
                                       row("node_b").unsqueeze(1).broadcast_to([P, NT, 3 * NODES]), ALU.add), "node")
                given("node")
                link(vec.tensor_scalar(dec[:], sc[:], 0.0, None, ALU.is_ge))
                vec.tensor_copy(lv[0][:, :, 1], dec[:, :, 0])
                link(vec.tensor_scalar(lv[0][:, :, 0], dec[:, :, 0], -1.0, 1.0, ALU.mult, ALU.add))
                for n in range(1, 4):
                    w = 2 ** n
                    pair = lv[n][:].rearrange("p j (w c) -> p j w c", c=2)
                    link(vec.tensor_tensor(pair[:, :, :, 1], lv[n - 1][:], dec[:, :, w - 1:2 * w - 1], ALU.mult))
                    last = vec.tensor_tensor(pair[:, :, :, 0], lv[n - 1][:], pair[:, :, :, 1], ALU.subtract)
                    if n < 3:
                        link(last)
                last.then_inc(sel_ready, 1)
                yield "selT"
                dve.wait_ge(selT_ready, i + 1)
                give(vec.tensor_scalar(nsel[:], bB("selT")[0:48, 0:T], BIG, -BIG, ALU.mult, ALU.add), "selT")
                for j in range(3):
                    for g in (1, 3):
                        yield f"net{j}{g}"
                        take(("hid", j, g))
                        for m in (2 * g, 2 * g + 1):
                            last = vec.tensor_scalar(hid[:, m], bB(("hid", j, g))[:, (m % 2) * T:(m % 2 + 1) * T],
                                                     col("f_b1", MF * j + m), 0.0, ALU.add, ALU.max)
                        give(last, ("hid", j, g))
                yield "S3"
                take("S3")
                link(vec.tensor_reduce(mx3[:], bB("S3").rearrange("p (t k) -> p t k", t=NT), AX.X, ALU.max))
                vec.tensor_scalar(nm3[:], mx3[:], -(D ** -0.5), None, ALU.mult).then_inc(mx3_ready, 1)
                yield "P3"
                given("S3")
                link(vec.reciprocal(rd3[:], den3[:]))
                yield "y4"
                dve.wait_ge(x5r_ready, i + 1)
                take("y4")
                for t in range(NT):
                    last = vec.scalar_tensor_tensor(rB[:, t], bB("y4")[:, t * D:(t + 1) * D], rd3[:, t:t + 1], x5r[:, t],
                                                    ALU.mult, ALU.add)
                give(last, "y4")
                given("y4")
                statistics()
                yield "x6"
                scale(i + 1, x6, x6_ready)
                assert linked() == LINKS_VEC["F"], linked()

            write_out(OPENING, dve_A(0), late())
            dve.wait_ge(kv2_loaded, 16 * LOADS[1])
            write_out(FIRST, dve_A(1), dve_M(0))
            write_out(SECOND, dve_X(0), dve_A(2), dve_M(1))
            with dve.Fori(0, NB - 3) as i:
                write_out(STEADY, dve_X(i + 1), dve_A(i + 3), dve_F(i), dve_M(i + 2))
            write_out(LAST + SEGMENTS_M, dve_X(NB - 2), dve_F(NB - 3), dve_M(NB - 1))
            write_out(LAST, dve_X(NB - 1), dve_F(NB - 2))
            write_out(SEGMENTS_F, dve_F(NB - 1))

        @block.tensor
        def _(pe):
            mm, tp = nc.tensor.matmul, nc.tensor.transpose

            first_of = {("mk", 0, 0): "lora", ("ki",): "keys", ("v", 0, 0): "values", ("k2", 0, 0): "second"}

            def put(name):
                ps = (psA if BANK[name] < 4 else psB)[:, BANK[name] % 4, :]
                before = [x for x in SETUP[:SETUP.index(name)] if BANK[x] == BANK[name]]
                if before:
                    if before[-1] in BY_ACT:
                        pe.wait_ge(setup_act, BY_ACT[before[-1]] + 1)
                    else:
                        pe.wait_ge(setup_dve, BY_DVE[before[-1]] + 1)
                if name in first_of:
                    pe.wait_ge(setup_loaded[first_of[name]], 16 * len(setup_loads[first_of[name]]))
                elif name == ("mq", 0, 0):
                    pe.wait_ge(weights_loaded, 16 * N_WEIGHTS)
                kind = name[0]
                if kind == "ki":
                    for m in range(M0):
                        for c in range(2):
                            last = mm(ps[:, m * NB * IPA:(m + 1) * NB * IPA], Wki[:, c, m * P:(m + 1) * P], Ci[:, c],
                                      start=c == 0, stop=c == 1)
                elif kind in ("mk", "mv", "mq"):
                    _, c, f = name
                    d0, w, u = {"mk": (DnK, CH, 1), "mv": (DnV, CH, 2), "mq": (DnQ, P, 0)}[kind]
                    last = mm(ps[0:w], Dn[:, d0 + w * c:d0 + w * (c + 1)], Up[:, u, f * 512:(f + 1) * 512],
                              start=True, stop=True)
                elif kind == "mo":
                    for m in (2 * name[1], 2 * name[1] + 1):
                        last = mm(ps[:, (m % 2) * D:(m % 2 + 1) * D], Dn[:, DnO + m * P:DnO + (m + 1) * P], Ou[:],
                                  start=True, stop=True)
                elif kind == "k":
                    _, m, f = name
                    if m == f == 0:
                        pe.wait_ge(setup_dve, 4)
                    for c in range(2):
                        last = mm(ps[:, 0:480], Wk[:, c, m * P:(m + 1) * P], Ct[:, c, f * 480:(f + 1) * 480],
                                  start=c == 0, stop=c == 1)
                elif kind == "v":
                    _, b, f = name
                    if b == f == 0:
                        pe.wait_ge(setup_dve, 8)
                    for c in range(2):
                        last = mm(ps[0:KEYS], Ct[:, c, b * KEYS:(b + 1) * KEYS], Wv[:, c, f * 512:(f + 1) * 512],
                                  start=c == 0, stop=c == 1)
                elif kind == "vi":
                    for c in range(2):
                        last = mm(ps[0:NB * IPA], Ci[:, c, :], Wvi[:, c, name[1] * 512:(name[1] + 1) * 512],
                                  start=c == 0, stop=c == 1)
                elif kind == "k2":
                    _, m, f = name
                    for c in range(2):
                        last = mm(ps[:, 0:480], Wk2[:, c, m * P:(m + 1) * P], Ct[:, c, f * 480:(f + 1) * 480],
                                  start=c == 0, stop=c == 1)
                else:
                    b = name[1]
                    for c in range(2):
                        last = mm(ps[0:KEYS, 0:D], Ct[:, c, b * KEYS:(b + 1) * KEYS], Wv2[:, c, :],
                                  start=c == 0, stop=c == 1)
                last.then_inc(setup_full, 1)

            def late():
                for n, name in enumerate(LATE):
                    yield f"late{n}"
                    put(name)

            for name in EARLY:
                put(name)
            pe.wait_ge(setup_act, EARLY_ACT)
            pe.wait_ge(setup_dve, EARLY_DVE)
            pe.wait_ge(setup_vec, 2)

            def tools(part, i):
                fulls, free, ring, bank = (full_A, free_A, RING_A, bA) if part in "AX" else (full_B, free_B, RING_B, bB)

                def room(name):
                    pe.wait_ge(free[ring.bank[name]], ring.turn(name, i))

                def taken(name):
                    pe.wait_ge(free[ring.bank[name]], ring.turn(name, i) + 1)

                def full(ins):
                    ins.then_inc(fulls, 1)

                def to_cols(name, rows_):
                    room(name)
                    for k in range(ND):
                        for t in range(NT):
                            last = tp(bank(name)[:, k * T + t * P:k * T + (t + 1) * P], rows_[:, t, k * P:(k + 1) * P],
                                      ident[:])
                    full(last)

                return room, taken, full, to_cols

            def pe_A(i):
                room, taken, full, to_cols = tools("A", i)
                yield "conv"
                room("conv")
                pe.wait_ge(x_loaded, i * 16 + 16)
                mm(bA("conv")[:, 0:D], Toep[:, 0], xin[:, 0], start=True, stop=False)
                mm(bA("conv")[:, 0:D], Toep[:, 1], xin[:, 1], start=False, stop=True)
                full(mm(bA("conv")[:, D:2 * D], Toep[:, 0], xin[:, 1], start=True, stop=True))
                yield "x1T"
                pe.wait_ge(x1_ready, i + 1)
                to_cols("x1T", x1)
                for g in range(4):
                    yield f"q{g}"
                    if g == 0:
                        taken("x1T")
                    room(("q", g))
                    for m in (2 * g, 2 * g + 1):
                        for k in range(ND):
                            last = mm(bA(("q", g))[:, (m % 2) * T:(m % 2 + 1) * T], Wq[:, k, m * P:(m + 1) * P],
                                      x1T[:, k], start=k == 0, stop=k == 1)
                    full(last)
                for t, g in TILES:
                    yield f"S{t}{g}"
                    if t == g == 0:
                        pe.wait_ge(kv_loaded, i * 16 * LOADS[0] + 16 * LOADS[0])
                    if t == 0:
                        taken(("q", g))
                    room(("S", t, g))
                    for m in (2 * g, 2 * g + 1):
                        last = mm(bA(("S", t, g))[:, (m % 2) * 2 * KEYS:(m % 2 + 1) * 2 * KEYS],
                                  qT[:, m, t * P:(t + 1) * P], Kbd[:, m], start=True, stop=True)
                    full(last)
                for t in range(NT):
                    yield f"PT{t}"
                    pe.wait_ge(probs_ready, i * NT + (t + 1))
                    for g in range(4):
                        room(("PT", t, g))
                        for h in range(4):
                            last = tp(bA(("PT", t, g))[0:KEYS, h * P:(h + 1) * P], Pr[:, t, 4 * g + h], ident[:])
                        full(last)
                    yield f"O{t}"
                    for f in range(2):
                        for g in (2 * f, 2 * f + 1):
                            taken(("PT", t, g))
                        room(("O", t, f))
                        for h in range(8 * f, 8 * f + 8):
                            m = h // 2
                            last = mm(bA(("O", t, f))[64 * (h % 2):64 * (h % 2) + 64, (m % 4) * P:(m % 4 + 1) * P],
                                      V[:, h * DH0:(h + 1) * DH0], PT[:, h], start=True, stop=True)
                        full(last)
                yield "y1a"
                taken(("O", 1, 1))
                room("y1")
                for t in range(NT):
                    if t:
                        yield "y1"
                    for m in range(M0):
                        last = mm(bA("y1")[:, t * D:(t + 1) * D], OT[:, m, t * P:(t + 1) * P], Wo[:, m],
                                  start=m == 0, stop=m == M0 - 1)
                full(last)
                yield "x2T"
                pe.wait_ge(x2_ready, i + 1)
                to_cols("x2T", x2)
                yield "router"
                taken("x2T")
                room("router")
                for t in range(NT):
                    for k in range(ND):
                        last = mm(bA("router")[:, t * EXPERTS:(t + 1) * EXPERTS], x2T[:, k, t * P:(t + 1) * P], Rw[:, k],
                                  start=k == 0, stop=k == 1)
                full(last)
                for g in range(4):
                    yield f"h{g}"
                    room(("h", g))
                    for e in (2 * g, 2 * g + 1):
                        for k in range(ND):
                            last = mm(bA(("h", g))[:, (e % 2) * T:(e % 2 + 1) * T], W1[:, k, e * EF:(e + 1) * EF],
                                      x2T[:, k], start=k == 0, stop=k == 1)
                    full(last)
                yield "maskT"
                room("maskT")
                pe.wait_ge(mask_ready, i + 1)
                for t in range(NT):
                    last = tp(bA("maskT")[0:24, t * P:(t + 1) * P], m3[:, t].rearrange("p s e -> p (s e)"), ident[:])
                full(last)
                for g in range(4):
                    yield f"mb{g}"
                    if g == 0:
                        taken("maskT")
                    room(("mb", g))
                    for e in (2 * g, 2 * g + 1):
                        last = mm(bA(("mb", g))[:, (e % 2) * T:(e % 2 + 1) * T], Sel24[:, e:e + 1].broadcast_to([24, P]), mTb[:], start=True, stop=True)
                    full(last)
                yield "y2a"
                taken(("mb", 3))
                room("y2")
                for t in range(NT):
                    if t:
                        yield "y2"
                    for e in range(EXPERTS):
                        mm(bA("y2")[:, t * D:(t + 1) * D], hT[:, e, t * P:(t + 1) * P], W2[:, e],
                           start=e == 0, stop=False)
                    last = mm(bA("y2")[:, t * D:(t + 1) * D], mT[:, t * P:(t + 1) * P], B2[:], start=False, stop=True)
                full(last)

            def pe_M(i):
                room, taken, full, to_cols = tools("M", i)
                yield "xrT"
                pe.wait_ge(xr_ready, i + 1)
                to_cols("xrT", xr)
                yield "u"
                taken("xrT")
                def inward(s, W):
                    for g in range(2):
                        room((s, g))
                        for m in (2 * g, 2 * g + 1):
                            for k in range(ND):
                                last = mm(bB((s, g))[:, (m % 2) * T:(m % 2 + 1) * T], W[:, k, m * P:(m + 1) * P],
                                          xrT[:, k], start=k == 0, stop=k == 1)
                        full(last)

                inward("u", Win)
                yield "skip"
                inward("skip", Wsk)
                yield "low rank"
                room("dbc")
                for m in range(NM):
                    if m % 2 == 0:
                        pe.wait_ge(xs_ready, i * 2 + (m // 2 + 1))
                    last = mm(bB("dbc")[0:96, 0:T], Wdbc[:, m], xs[:, m], start=m == 0, stop=m == NM - 1)
                full(last)
                yield "delta"
                pe.wait_ge(dbc_ready, i + 1)
                for g in range(2):
                    room(("z", g))
                    for m in (2 * g, 2 * g + 1):
                        last = mm(bB(("z", g))[:, (m % 2) * T:(m % 2 + 1) * T], Wd2[:, m * P:(m + 1) * P], dbc,
                                  start=True, stop=True)
                    full(last)
                pe.wait_ge(bc3_ready, i + 1)

                def broadcast(n):
                    room(("bc", n))
                    mm(bB(("bc", n))[:, 0:T], Sel96[:, n:n + 1].broadcast_to([96, P]), bc3[:], start=True, stop=True)
                    full(mm(bB(("bc", n))[:, T:2 * T], Sel96[:, NS + n:NS + n + 1].broadcast_to([96, P]), bc3[:], start=True, stop=True))

                broadcast(0)
                broadcast(1)
                for n in range(NS - 2):
                    yield f"state{n}"
                    broadcast(n + 2)
                yield "my"
                pe.wait_ge(yT_ready, i + 1)
                room("my")
                for t in range(NT):
                    for m in range(NM):
                        last = mm(bB("my")[:, t * D:(t + 1) * D], yT[:, m, t * P:(t + 1) * P], Wout[:, m],
                                  start=m == 0, stop=m == NM - 1)
                full(last)

            def pe_X(i):
                room, taken, full, to_cols = tools("X", i)
                yield "x4T"
                pe.wait_ge(x4_ready, i + 1)
                to_cols("x4T", x4)
                yield "qx"
                taken("x4T")
                room("q2")
                for m in range(ND):
                    for k in range(ND):
                        last = mm(bA("q2")[:, m * T:(m + 1) * T], Wq2[:, k, m * P:(m + 1) * P], x4T[:, k],
                                  start=k == 0, stop=k == 1)
                full(last)
                for t, g in TILES:
                    yield f"T{t}{g}"
                    if t == g == 0:
                        taken("q2")
                        pe.wait_ge(kv2_loaded, i * 16 * LOADS[1] + 16 * LOADS[1])
                    room(("S2", t, g))
                    full(mm(bA(("S2", t, g))[:, 0:4 * KEYS], q2T[:, g // 2, t * P:(t + 1) * P],
                            Kbd2[:, g // 2, 4 * (g % 2):4 * (g % 2) + 4].rearrange("p h j -> p (h j)"),
                            start=True, stop=True))
                for t in range(NT):
                    yield f"QT{t}"
                    pe.wait_ge(exp2_done, i * NT + (t + 1))
                    for g in range(4):
                        room(("PT2", t, g))
                        for h in range(4):
                            last = tp(bA(("PT2", t, g))[0:KEYS, h * P:(h + 1) * P], Pr2[:, t, 4 * g + h], ident[:])
                        full(last)
                    yield f"o{t}"
                    taken(("PT2", t, 3))
                    room(("o", t))
                    for h in range(H1):
                        last = mm(bA(("o", t))[:, h * (DH1 + 1):(h + 1) * (DH1 + 1)], PT2[:, h],
                                  V2[:, h], start=True, stop=True)
                    full(last)
                yield "oT"
                taken(("o", 1))
                room("oT")
                for k in range(ND):
                    for t in range(NT):
                        last = tp(bA("oT")[:, k * T + t * P:k * T + (t + 1) * P],
                                  o2[:, t, 8 * k:8 * k + 8].rearrange("p h d -> p (h d)"), ident[:])
                full(last)
                yield "y3"
                taken("oT")
                room("y3")
                for t in range(NT):
                    for k in range(ND):
                        last = mm(bA("y3")[:, t * D:(t + 1) * D], o2T[:, k, t * P:(t + 1) * P], Wo2[:, k],
                                  start=k == 0, stop=k == 1)
                full(last)

            def pe_F(i):
                room, taken, full, to_cols = tools("F", i)
                yield "x5T"
                pe.wait_ge(x5_ready, i + 1)
                to_cols("x5T", x5)
                yield "node"
                taken("x5T")
                room("node")
                for t in range(NT):
                    for k in range(ND):
                        last = mm(bB("node")[:, t * 3 * NODES:(t + 1) * 3 * NODES], x5T[:, k, t * P:(t + 1) * P],
                                  Nw[:, k], start=k == 0, stop=k == 1)
                full(last)
                yield "selT"
                room("selT")
                pe.wait_ge(sel_ready, i + 1)
                pe.sem_inc(alone_pe, 1)
                for t in range(NT):
                    last = tp(bB("selT")[0:48, t * P:(t + 1) * P],
                              lv[3][:, 3 * t:3 * t + 3].rearrange("p j l -> p (j l)"), ident[:])
                full(last)
                for j in range(3):
                    for g in range(4):
                        yield f"net{j}{g}"
                        if g == 0:
                            pe.wait_ge(fw1_loaded, i * 48 + 16 * (j + 1))
                            if j == 0:
                                taken("selT")
                        room(("hid", j, g))
                        for m in (2 * g, 2 * g + 1):
                            h = bB(("hid", j, g))[:, (m % 2) * T:(m % 2 + 1) * T]
                            for k in range(ND):
                                mm(h, FW1[:, k, m * P:(m + 1) * P], x5T[:, k], start=k == 0, stop=False)
                            last = mm(h, Sel48[:, j, m], nsel[:], start=False, stop=True)
                        full(last)
                    yield f"out{j}a"
                    pe.wait_ge(fw2_loaded, i * 48 + 16 * (j + 1))
                    taken(("hid", j, 2))
                    taken(("hid", j, 3))
                    room(("out", j, 0))
                    for o in range(2):
                        if o:
                            yield f"out{j}"
                        dst = bB(("out", j, 0))[:, o * T:(o + 1) * T]
                        for m in range(MF):
                            if j < 2:
                                mm(dst, FW2[:, m, o * P:(o + 1) * P], hid[:, m], start=m == 0, stop=False)
                            else:
                                mm(dst, hid[:, m, o * P:(o + 1) * P], FW2[:, m], start=m == 0, stop=False)
                        if j < 2:
                            last = mm(dst, FB2[:, j, o * P:(o + 1) * P], selT[:], start=False, stop=True)
                        else:
                            last = mm(dst, selT[:, o * P:(o + 1) * P], FB2[:, j], start=False, stop=True)
                    full(last)
                yield "S3"
                taken(("out", 1, 0))
                room("S3")
                for t in range(NT):
                    for k in range(ND):
                        last = mm(bB("S3")[:, t * T:(t + 1) * T], qk3[:, 0, k, t * P:(t + 1) * P], qk3[:, 1, k],
                                  start=k == 0, stop=k == 1)
                full(last)
                yield "P3"
                taken("S3")
                room("P3T")
                for k in range(NT):
                    for t in range(NT):
                        last = tp(bB("P3T")[:, k * T + t * P:k * T + (t + 1) * P], P3[:, t, k * P:(k + 1) * P], ident[:])
                full(last)
                yield "y4"
                taken("P3T")
                taken(("out", 2, 0))
                room("y4")
                for t in range(NT):
                    for k in range(NT):
                        last = mm(bB("y4")[:, t * D:(t + 1) * D], P3T[:, k, t * P:(t + 1) * P], v3[:, k],
                                  start=k == 0, stop=k == 1)
                full(last)

            write_out(OPENING, pe_A(0), late())
            pe.wait_ge(kv2_loaded, 16 * LOADS[1])
            write_out(FIRST, pe_A(1), pe_M(0))
            write_out(SECOND, pe_X(0), pe_A(2), pe_M(1))
            with pe.Fori(0, NB - 3) as i:
                write_out(STEADY, pe_X(i + 1), pe_A(i + 3), pe_F(i), pe_M(i + 2))
            write_out(LAST + SEGMENTS_M, pe_X(NB - 2), pe_F(NB - 3), pe_M(NB - 1))
            write_out(LAST, pe_X(NB - 1), pe_F(NB - 2))
            write_out(SEGMENTS_F, pe_F(NB - 1))


def kernel(**inputs):
    import numpy as np
    import ml_dtypes
    import concourse.bacc as bacc
    from concourse.bass_utils import run_bass_kernel_spmd as run

    g = {k: np.asarray(v) for k, v in inputs.items()}
    f32 = np.float32

    padded = np.concatenate([np.zeros(P - 1, f32), g["L0_attn_filt"][:T]])
    k, t = np.arange(P)[:, None], np.arange(P)[None, :]
    toep = np.stack([padded[k - t + P - 1], padded[k - t + 2 * P - 1]])

    def vec(a):
        return np.asarray(a).reshape(-1, P).T

    cols = np.concatenate([
        vec(g["L0_ffn_b1"]),
        g["L1_attn_conv_w"].reshape(NM, P, KC).transpose(1, 0, 2).reshape(P, NM * KC),
        vec(g["L1_attn_conv_b"]), vec(g["L1_attn_wd2_b"]), vec(g["L1_attn_W_D"]),
        vec(g["L1_xattn_bq"]), vec(g["L1_xattn_bk"]),
        vec(g["L1_ffn_q_b1"]), vec(g["L1_ffn_k_b1"]), vec(g["L1_ffn_v_b1"]),
        vec(g["L1_attn_norm_w"]),
        g["L1_attn_A_log"].reshape(NM, P, NS).transpose(1, 0, 2).reshape(P, NM * NS),
        np.broadcast_to(np.concatenate([g[f"L0_xattn_{s}_alpha"] for s in "qkvo"])[None], (P, 4)),
    ], axis=1)
    rows = np.broadcast_to(np.concatenate([
        g["L0_xattn_bo"], g["L0_ffn_router_b"], g["L1_xattn_bv"], g["L1_xattn_bo"],
        g["L1_ffn_q_node_b"], g["L1_ffn_k_node_b"], g["L1_ffn_v_node_b"],
        np.arange(EXPERTS).astype(f32)])[None], (P, NROWS))

    ctxT = g["ctx_768"].transpose(2, 0, 1)
    sel24 = np.tile(np.eye(EXPERTS, dtype=f32), (3, 1))
    sel96 = np.tile(np.eye(32, dtype=f32), (3, 1))
    sel48 = np.zeros((48, 3, MF, P), f32)
    for j in range(3):
        for m in range(MF):
            for a in range(2):
                sel48[LEAVES * j + 2 * m + a, j, m, LW * a:LW * (a + 1)] = 1
    fb2 = np.zeros((3, 48, D), f32)
    for j, s in enumerate("qkv"):
        fb2[j, LEAVES * j:LEAVES * (j + 1)] = g[f"L1_ffn_{s}_b2"]

    data = dict(
        x=g["x"], toep=toep, ctxT=ctxT.reshape(CTX, NB * KEYS), ctxiT=ctxT[:, :, TEXT:].reshape(CTX, NB * IPA),
        cols=cols, rows=rows, ident_in=np.eye(P, dtype=f32),
        sel24_in=sel24.astype(ml_dtypes.bfloat16), sel96_in=sel96.astype(ml_dtypes.bfloat16),
        sel48_in=sel48.astype(ml_dtypes.bfloat16),
        wq=g["L0_xattn_Wq"], wk=g["L0_xattn_Wk"], wv=g["L0_xattn_Wv"], wo=g["L0_xattn_Wo"],
        qdT=g["L0_xattn_q_down"].T, kdT=g["L0_xattn_k_down"].T, vdT=g["L0_xattn_v_down"].T, odT=g["L0_xattn_o_down"].T,
        qu=g["L0_xattn_q_up"], ku=g["L0_xattn_k_up"], vu=g["L0_xattn_v_up"], ou=g["L0_xattn_o_up"],
        wki=g["L0_xattn_Wk_ipa"], wvi=g["L0_xattn_Wv_ipa"],
        rw=g["L0_ffn_router_w"], w1=g["L0_ffn_W1"].transpose(1, 0, 2).reshape(D, EXPERTS * EF), w2=g["L0_ffn_W2"],
        b2=np.tile(g["L0_ffn_b2"], (3, 1)),
        win=g["L1_attn_in_w"].T, wsk=g["L1_attn_skip_w"].T,
        wdbc=np.concatenate([g["L1_attn_wd1"], g["L1_attn_wb"], g["L1_attn_wc"]]).T,
        wd2=g["L1_attn_wd2"].T, wout=g["L1_attn_out_w"].T,
        wq2=g["L1_xattn_Wq"], wk2=g["L1_xattn_Wk"], wv2=g["L1_xattn_Wv"], wo2=g["L1_xattn_Wo"],
        nw=np.concatenate([g[f"L1_ffn_{s}_node_w"] for s in "qkv"]).T,
        fw1=np.stack([g[f"L1_ffn_{s}_w1"].transpose(1, 0, 2).reshape(D, LEAVES * LW) for s in "qkv"]),
        fw2=np.stack([g[f"L1_ffn_{s}_w2"].reshape(LEAVES * LW, D) for s in "qkv"]),
        fb2=fb2,
    )
    nc = bacc.Bacc("TRN2", target_bir_lowering=False, num_devices=1)
    arrays, args = {}, {}
    for name, a in data.items():
        a = np.ascontiguousarray(a)
        arrays[f"in_{name}"] = a
        args[name] = nc.dram_tensor(f"in_{name}", a.shape, mybir.dt.from_np(a.dtype), kind="ExternalInput").ap()
    out = nc.dram_tensor("out_0_dram", (NB, T, D), mybir.dt.float32, kind="ExternalOutput").ap()
    decoder(nc, out=out, **args)
    r = run(nc, [arrays], core_ids=[0])
    return r.results[0]["out_0_dram"]
```
